# Optimizing a Trainium2 kernel written in Bass

```python
import numpy as np
import jax
import jax.numpy as jnp

def _softmax(x, axis=-1):
    return jax.nn.softmax(x, axis=axis)

def _gelu(x):
    return jax.nn.gelu(x, approximate=True)

def _silu(x):
    return jax.nn.silu(x)

def _sigmoid(x):
    return jax.nn.sigmoid(x)

def _layernorm(x, axis=-1, eps=1e-05):
    m = jnp.mean(x, axis=axis, keepdims=True)
    v = jnp.var(x, axis=axis, keepdims=True)
    return (x - m) / jnp.sqrt(v + eps)

def _scatter_add(tgt, idx, src, axis=0):
    return tgt.at[idx].add(src)

def _segment_sum(src, seg, n):
    return jax.ops.segment_sum(src, seg, n)
kernel_name = 'mk_gps_d1_gnn_r8_3ffd64'

def setup_inputs(seed: int=0):
    np.random.seed(seed)
    _w = jnp.asarray

    def _rec_inputs():
        import jax
        import jax.numpy as jnp
        _gk = jax.random.key(seed)
        x = -0.0002117 + 1 * jax.random.normal(jax.random.fold_in(_gk, 1), (6250, 256), jnp.float32)
        _s = jax.random.randint(jax.random.fold_in(_gk, 2), (50000,), 0, 6250, jnp.int32)
        _d = jax.random.randint(jax.random.fold_in(_gk, 3), (50000,), 0, 6250, jnp.int32)
        _loop = jnp.arange(6250, dtype=jnp.int32)
        src = jnp.concatenate([_s, _d, _loop])
        dst = jnp.concatenate([_d, _s, _loop])
        _o = jnp.argsort(dst, stable=True)
        src = src[_o]
        dst = dst[_o]
        edge_weight = jax.random.uniform(jax.random.fold_in(_gk, 12), (106250,), jnp.float32, 0.0, 1)
        return (x, src, dst, edge_weight)
    x, src, dst, edge_weight = _rec_inputs()

    def _L0_gnn_setup():
        import jax, jax.numpy as jnp
        import numpy as np
        N_NODES = 12500
        N_EDGES = 200000
        D_IN = 256
        D_OUT = 256
        key = jax.random.key(seed)
        k1, k2, k3, k4, k5 = jax.random.split(key, 5)
        x = jax.random.normal(k1, (N_NODES, D_IN), dtype=jnp.float32)
        edge_src = jax.random.randint(k2, (N_EDGES,), 0, N_NODES, dtype=jnp.int32)
        edge_dst = jax.random.randint(k3, (N_EDGES,), 0, N_NODES, dtype=jnp.int32)
        edge_val = jax.random.uniform(k4, (N_EDGES,), dtype=jnp.float32)
        stdv = 1.0 / np.sqrt(D_OUT)
        weight = jax.random.uniform(k5, (D_IN, D_OUT), dtype=jnp.float32, minval=-stdv, maxval=stdv)
        return {'x': x, 'edge_src': edge_src, 'edge_dst': edge_dst, 'edge_val': edge_val, 'weight': weight}
    _L0_gnn_all = _L0_gnn_setup()
    _L0_gnn_in = {k: v for k, v in _L0_gnn_all.items() if k in ('weight',)}
    del _L0_gnn_all

    def _L0_mix_setup():
        import jax, jax.numpy as jnp
        import numpy as np
        HEADS = 8
        DIM_HEAD = 64
        EPS = 1e-05

        def _inst_norm_lastdim(t):
            mu = jnp.mean(t, axis=-1, keepdims=True)
            var = jnp.mean(jnp.square(t - mu), axis=-1, keepdims=True)
            return (t - mu) * jax.lax.rsqrt(var + EPS)
        key = jax.random.key(seed)
        k1, k2, k3, k4 = jax.random.split(key, 4)
        b, n, dim = (4, 1024, 256)
        inner = HEADS * DIM_HEAD
        x = jax.random.normal(k1, (b, n, dim), dtype=jnp.float32)
        Wqkv = jax.random.normal(k2, (3 * inner, dim), dtype=jnp.float32) * (1.0 / np.sqrt(dim))
        Wout = jax.random.normal(k3, (dim, inner), dtype=jnp.float32) * (1.0 / np.sqrt(inner))
        bout = jax.random.normal(k4, (dim,), dtype=jnp.float32) * 0.01
        return {'x': x, 'Wqkv': Wqkv, 'Wout': Wout, 'bout': bout}
    _L0_mix_all = _L0_mix_setup()
    _L0_mix_in = {k: v for k, v in _L0_mix_all.items() if k in ('Wqkv', 'Wout', 'bout')}
    del _L0_mix_all

    def _L0_ffn_setup():
        import jax, jax.numpy as jnp
        import numpy as np
        B, S, H, F, E, K = (8, 512, 256, 512, 16, 2)
        EPS = 1e-05
        key = jax.random.key(seed)
        ks = jax.random.split(key, 9)
        sc = 0.02
        return {'x': jax.random.normal(ks[0], (B, S, H), dtype=jnp.float32), 'gate_w': jax.random.normal(ks[1], (H, E), dtype=jnp.float32) * sc, 'gate_b': jnp.zeros((E,), dtype=jnp.float32), 'w1': jax.random.normal(ks[2], (E, H, F), dtype=jnp.float32) * sc, 'b1': jnp.zeros((E, F), dtype=jnp.float32), 'w2': jax.random.normal(ks[3], (E, F, H), dtype=jnp.float32) * sc, 'b2': jnp.zeros((E, H), dtype=jnp.float32), 'gamma': jnp.ones((H,), dtype=jnp.float32), 'beta': jnp.zeros((H,), dtype=jnp.float32)}
    _L0_ffn_all = _L0_ffn_setup()
    _L0_ffn_in = {k: v for k, v in _L0_ffn_all.items() if k in ('gate_w', 'gate_b', 'w1', 'b1', 'w2', 'b2', 'gamma', 'beta')}
    del _L0_ffn_all
    return {'x': x, 'src': src, 'dst': dst, 'edge_weight': edge_weight, 'L0_gnn_weight': _L0_gnn_in['weight'], 'L0_mix_Wqkv': _L0_mix_in['Wqkv'], 'L0_mix_Wout': _L0_mix_in['Wout'], 'L0_mix_bout': _L0_mix_in['bout'], 'L0_ffn_gate_w': _L0_ffn_in['gate_w'], 'L0_ffn_gate_b': _L0_ffn_in['gate_b'], 'L0_ffn_w1': _L0_ffn_in['w1'], 'L0_ffn_b1': _L0_ffn_in['b1'], 'L0_ffn_w2': _L0_ffn_in['w2'], 'L0_ffn_b2': _L0_ffn_in['b2'], 'L0_ffn_gamma': _L0_ffn_in['gamma'], 'L0_ffn_beta': _L0_ffn_in['beta']}

def reference(x, src, dst, edge_weight, L0_gnn_weight, L0_mix_Wqkv, L0_mix_Wout, L0_mix_bout, L0_ffn_gate_w, L0_ffn_gate_b, L0_ffn_w1, L0_ffn_b1, L0_ffn_w2, L0_ffn_b2, L0_ffn_gamma, L0_ffn_beta):
    import jax
    import jax.numpy as jnp

    def _L0_gnn_ref(x, edge_src, edge_dst, edge_val, weight):
        import jax, jax.numpy as jnp
        import numpy as np
        N_NODES = 12500
        N_EDGES = 200000
        D_IN = 256
        D_OUT = 256
        msgs = x[edge_src] * edge_val[:, None]
        agg = jax.ops.segment_sum(msgs, edge_dst, num_segments=x.shape[0])
        return agg @ weight

    def _L0_mix_ref(x, Wqkv, Wout, bout):
        import jax, jax.numpy as jnp
        import numpy as np
        HEADS = 8
        DIM_HEAD = 64
        EPS = 1e-05

        def _inst_norm_lastdim(t):
            mu = jnp.mean(t, axis=-1, keepdims=True)
            var = jnp.mean(jnp.square(t - mu), axis=-1, keepdims=True)
            return (t - mu) * jax.lax.rsqrt(var + EPS)
        b, n, dim = x.shape
        qkv = jnp.einsum('bnc,fc->bnf', x, Wqkv)
        q, k, v = jnp.split(qkv, 3, axis=-1)

        def to_heads(t):
            return t.reshape(b, n, HEADS, DIM_HEAD).transpose(0, 2, 1, 3)
        q, k, v = (to_heads(q), to_heads(k), to_heads(v))
        k = _inst_norm_lastdim(k)
        v = _inst_norm_lastdim(v)
        dots = jnp.einsum('bhnd,bhne->bhde', k, v)
        out = jnp.einsum('bhnd,bhde->bhne', q, dots) / n
        out = out.transpose(0, 2, 1, 3).reshape(b, n, HEADS * DIM_HEAD)
        return jnp.einsum('bnf,cf->bnc', out, Wout) + bout

    def _L0_ffn_ref(x, gate_w, gate_b, w1, b1, w2, b2, gamma, beta):
        import jax, jax.numpy as jnp
        import numpy as np
        B, S, H, F, E, K = (8, 512, 256, 512, 16, 2)
        EPS = 1e-05
        gate_logits = x @ gate_w + gate_b
        topk_vals, topk_idx = jax.lax.top_k(gate_logits, K)
        topk_w = jax.nn.softmax(topk_vals, axis=-1)
        h = jax.nn.relu(jnp.einsum('bsh,ehf->bsef', x, w1) + b1)
        expert_out = jnp.einsum('bsef,efh->bseh', h, w2) + b2
        sel = jnp.take_along_axis(expert_out, topk_idx[:, :, :, None], axis=2)
        moe = jnp.sum(topk_w[..., None] * sel, axis=2)
        y = x + moe
        mu = jnp.mean(y, axis=-1, keepdims=True)
        var = jnp.var(y, axis=-1, keepdims=True)
        return (y - mu) / jnp.sqrt(var + EPS) * gamma + beta
    xn = _layernorm(x, axis=-1)
    x = x + _L0_gnn_ref(xn, src, dst, edge_weight, L0_gnn_weight) + _L0_mix_ref(xn[None], L0_mix_Wqkv, L0_mix_Wout, L0_mix_bout)[0]
    x = x + _L0_ffn_ref(_layernorm(x, axis=-1)[None], L0_ffn_gate_w, L0_ffn_gate_b, L0_ffn_w1, L0_ffn_b1, L0_ffn_w2, L0_ffn_b2, L0_ffn_gamma, L0_ffn_beta)[0]
    return x

_drawn_inputs = setup_inputs


def setup_inputs(seed=0):
    import zlib

    import numpy as np

    out = dict(_drawn_inputs(seed))
    spreads = {'L0_ffn_gate_b': (0.0, 0.317),
     'L0_ffn_b1': (0.0, 0.8),
     'L0_ffn_b2': (0.0, 0.302),
     'L0_ffn_gamma': (1.0, 0.2),
     'L0_ffn_beta': (0.0, 0.1)}
    factors = {'L0_mix_bout': 8.0}
    for name, (base, spread) in spreads.items():
        noise = np.random.default_rng([zlib.crc32(name.encode()), seed]).standard_normal(out[name].shape)
        drawn = base * np.exp(spread * noise) if base else spread * noise
        out[name] = jnp.asarray(drawn.astype(out[name].dtype))
    for name, factor in factors.items():
        out[name] = (out[name] * factor).astype(out[name].dtype)
    return out
```

```python
from contextlib import ExitStack

import concourse.bass as bass
from concourse import mybir

F32 = mybir.dt.float32
I32 = mybir.dt.int32
U32 = mybir.dt.uint32
ALU = mybir.AluOpType
ACT = mybir.ActivationFunctionType
AX = mybir.AxisListType

P = 128
N = 6250
D = 256
KD = D // P
CH = 7
NC = 7
NT = NC * CH
NP = NT * P
PADDED = NP - N
HEADS, DH = 8, 64
INNER = HEADS * DH
NJ = INNER // P
EPS = 1e-5

EDGES = 106250
GT = 4
BG = 2 * CH
BT = BG * GT
NB = -(-EDGES // (BT * P))
NG = NB * BG
ET = NB * BT
RING = 14
SEL = 8
W = 128
GW = 448
NW = NP // GW

E, F = 16, 512
FC = F // P
TS = 256
NS = (2 * N + E * (TS - 1)) // TS
NS += NS % 2
SLOTS = NS * TS
ZR = -(-(SLOTS + TS) // (NC * P))
XROWS = NC * ZR * P
assert NB == 2 * NC + 1 and BT % RING == 0 and BT % SEL == 0
W1ROW = KD * F + FC
W2ROW = FC * D

LEAD = BG


def gps_layer(nc, x, src, dst, first_dst, edge_w, gnn_w, wkv, wq, wout, bout, gate_w, gate_b,
              w1b, w2, b2, gamma, beta, out):
    table = nc.dram_tensor("normed_rows", (NP, D), F32, kind="Internal").ap()
    xs = nc.dram_tensor("rows_by_slot", (XROWS, D), F32, kind="Internal").ap()
    ys = nc.dram_tensor("results_by_slot", (SLOTS + TS, D), F32, kind="Internal").ap()

    with ExitStack() as ctx:
        def sb(name, shape, dt=F32):
            return ctx.enter_context(nc.sbuf_tensor(name, shape, dt))

        def sem(name):
            return ctx.enter_context(nc.semaphore(name))

        def sems(name, n):
            return [sem(f"{name}{i}") for i in range(n)]

        X2 = sb("X2", [P, NT, D])
        aggT = sb("aggT", [P, KD, NP])
        ring = sb("ring", [P, RING, D])
        S = sb("S", [P, SEL, W])
        wkv_sb = sb("wkv_sb", [P, KD, 2 * INNER])
        wq_sb = sb("wq_sb", [P, NJ, D])
        wout_sb = sb("wout_sb", [P, NJ, D])
        gnn_sb = sb("gnn_sb", [P, KD, D])
        M = sb("M", [P, KD, D])
        T1 = sb("T1", [P, NJ, D])
        bd = sb("bd", [P, NJ, P])
        dstrel = sb("dstrel", [P, ET])
        ew = sb("ew", [P, ET])
        idx = sb("idx", [P, 2, BT // 2], I32)
        base_i = sb("base_i", [P, NG], I32)
        base_f = sb("base_f", [P, NG])
        tile_in = sb("tile_in", [P, CH, D])
        tT = sb("tT", [P, 2, D])
        sq = sb("sq", [P, 2 * INNER])
        ks = sb("ks", [P, 2, INNER])
        vs = sb("vs", [P, 2, INNER])
        aT = sb("aT", [P, 2, D])
        yt = sb("yt", [P, 2, D])
        ident = sb("ident", [P, P])
        iota = sb("iota", [P, GW])
        ones = sb("ones", [P, P])
        upper = sb("upper", [P, P])
        gate_sb = sb("gate_sb", [P, KD, 96])
        bout_b = sb("bout_b", [P, D])
        gamma_b = sb("gamma_b", [P, D])
        beta_b = sb("beta_b", [P, D])
        gb_b = sb("gb_b", [P, E])
        logits = sb("logits", [P, CH, E])
        top8 = sb("top8", [P, CH, 8])
        top8_i = sb("top8_i", [P, CH, 8], U32)
        top = sb("top", [P, 2, NT])
        bn = sb("bn", [P, CH, 6])
        mv = sb("mv", [P, NT, 2])
        mvc = sb("mvc", [P, CH, 2])
        rstd = sb("rstd", [P, NT])
        nmr = sb("nmr", [P, NT])
        kv_var = sb("kv_var", [P, 2, 2 * HEADS])
        kv_r = sb("kv_r", [P, 2 * HEADS])
        kv_s = sb("kv_s", [P, 2, HEADS])
        eps_t = sb("eps_t", [P, 1])
        slot_f = sb("slot_f", [P, 2, NT + CH])
        zeros = sb("zeros", [P, D])
        prob = sb("prob", [P, 2, NT])
        sidx = sb("sidx", [P, 2, CH], I32)
        etab = sb("etab", [1, NS], I32)
        small = sb("small", [P, 160])
        flag = sb("flag", [1, 1], I32)
        idx_gen = sb("idx_gen", [P, GT], I32)

        late = aggT[:, :, :].rearrange("p k n -> p (k n)")
        at = [0]

        def take(n):
            at[0] += n
            return late[:, at[0] - n:at[0]]
        w1_sb = [take(W1ROW) for _ in range(2)]
        w2_sb = [take(W2ROW) for _ in range(2)]
        b2_sb = [take(D) for _ in range(2)]
        xg = [take(2 * D).rearrange("p (h d) -> p h d", h=2) for _ in range(2)]
        xgT = [take(2 * D).rearrange("p (k t) -> p k t", k=KD) for _ in range(2)]
        hT = [take(FC * TS).rearrange("p (f t) -> p f t", f=FC) for _ in range(2)]
        yo = [take(2 * D).rearrange("p (h d) -> p h d", h=2) for _ in range(2)]
        R = E * NT
        ringf = ring[:, :, :].rearrange("p a b -> p (a b)")
        wkvf = wkv_sb[:, :, :].rearrange("p a b -> p (a b)")
        H1, H2, Hs, pos = [ringf[:, R * i:R * (i + 1)].rearrange("p (e i) -> p e i", e=E) for i in range(4)]
        tot, scan = [wkvf[:, R * i:R * (i + 1)].rearrange("p (e i) -> p e i", e=E) for i in range(2)]
        iota_e = sq[:, 0:R].rearrange("p (e i) -> p e i", e=E)
        cmp_t = take(NS * E).rearrange("p (j e) -> p j e", e=E)
        Sgen = wkvf[:, 0:GT * GW].rearrange("p (t w) -> p t w", t=GT)
        dst_gen = kv_r[:, 0:GT]

        ps = ctx.enter_context(nc.psum_tensor("ps", [P, 8, 512], F32))
        aggps = [ps[:, i, 0:KD * W] for i in range(2)]
        tps = ps[:, 2, 0:D]
        yps = [ps[:, 2 + i, 0:D] for i in range(2)]
        dotps = ps[:, 3, :].rearrange("p (j e) -> p j e", j=NJ)
        wide = [ps[:, 4 + 2 * i:6 + 2 * i, :].rearrange("p a b -> p (a b)") for i in range(2)]

        consts_in = sem("consts_in")
        pool_consts = sem("pool_consts")
        dve_consts = sem("dve_consts")
        x_in = sems("x_in", CH)
        stats_done = sem("stats_done")
        std_done = sem("std_done")
        rstd_done = sem("rstd_done")
        normed = sem("normed")
        table_out = sem("table_out")
        idx_in = sems("idx_in", 2)
        gathered = sems("gathered", RING)
        selected = sem("selected")
        group_done = sem("group_done")
        group_added = sem("group_added")
        tile_loaded = sems("tile_loaded", CH)
        tile_turned = sem("tile_turned")
        turned_copied = sem("turned_copied")
        kv_done = sem("kv_done")
        kv_squared = sem("kv_squared")
        v_copied = sem("v_copied")
        kv_var_done = sem("kv_var_done")
        kv_std_done = sem("kv_std_done")
        kv_r_done = sem("kv_r_done")
        k_scaled = sem("k_scaled")
        dots_done = sem("dots_done")
        bd_done = sem("bd_done")
        t1_done = sem("t1_done")
        t1_copied = sem("t1_copied")
        m_done = sem("m_done")
        m_copied = sem("m_copied")
        x_again = sems("x_again", CH)
        x_biased = sem("x_biased")
        mix_done = sem("mix_done")
        mix_added = sem("mix_added")
        bad_found = sem("bad_found")
        bad_counted = sem("bad_counted")
        flag_ready = sem("flag_ready")
        gen_zeroed = sem("gen_zeroed")
        gen_idx_in = sem("gen_idx_in")
        gen_gathered = sems("gen_gathered", GT)
        gen_dst = sem("gen_dst")
        gen_selected = sem("gen_selected")
        gen_done = sem("gen_done")
        gen_added = sem("gen_added")
        agg_final = sem("agg_final")
        agg_staged = sem("agg_staged")
        gnn_done = sem("gnn_done")
        x2_done = sem("x2_done")
        y_bn = sem("y_bn")
        y_stats = sem("y_stats")
        y_std = sem("y_std")
        y_rstd = sem("y_rstd")
        y_normed = sem("y_normed")
        y_turned = sem("y_turned")
        y_copied = sem("y_copied")
        gate_done = sem("gate_done")
        logit_done = sem("logit_done")
        hot_done = sem("hot_done")
        ranked = sem("ranked")
        exp_in = sem("exp_in")
        exp_done = sem("exp_done")
        slots_done = sem("slots_done")
        zero_out = sem("zero_out")
        sidx_done = sem("sidx_done")
        row_ready = sem("row_ready")
        scattered = sems("scattered", CH)
        w1_in = sems("w1_in", 2)
        w2_in = sems("w2_in", 2)
        xg_in = sems("xg_in", 2)
        xg_turned = sem("xg_turned")
        xg_copied = sem("xg_copied")
        l1_done = sem("l1_done")
        relu_done = sem("relu_done")
        l2_done = sem("l2_done")
        y_done = sem("y_done")
        ys_out = sems("ys_out", 2)
        cidx_done = sem("cidx_done")
        picked = sems("picked", CH)
        y_again = sem("y_again")
        summed = sem("summed")
        f_stats = sem("f_stats")
        f_std = sem("f_std")
        f_rstd = sem("f_rstd")
        f_normed = sem("f_normed")
        f_done = sem("f_done")
        f_out = sems("f_out", CH)
        pool_past = sem("pool_past")
        dve_past = sem("dve_past")

        LEADERS = {"tensor": [group_done, gen_done, tile_turned, kv_done, dots_done, gnn_done, gate_done, y_turned,
                              mix_done, xg_turned, l1_done, l2_done],
                   "vector": [group_added, k_scaled, kv_var_done, mix_added, y_copied, logit_done, y_done, x2_done,
                              gen_added],
                   "scalar": [v_copied, kv_squared, turned_copied, xg_copied, relu_done]}
        ahead = {s for group in LEADERS.values() for s in group}

        def wait(eng, s, n):
            eng.wait_ge(s, n + LEAD if s in ahead else n)

        def start_counters(eng, names):
            for s in names:
                eng.sem_inc(s, LEAD)

        def prior(j):
            return 1 if j == 0 else 2

        def chunks(eng, first, last, body):
            with eng.Fori(first, last) as c:
                body(c)

        CONSTS = [(wkv_sb[:, :, :], wkv), (wq_sb[:, :, :], wq), (wout_sb[:, :, :], wout),
                  (gnn_sb[:, :, :], gnn_w), (ew[:, :], edge_w),
                  (gate_sb[:, :, :], gate_w), (dstrel[:, :].bitcast(I32), dst),
                  (base_i[:, :], first_dst.to_broadcast([P, NG])),
                  (bout_b[:, :], bout.to_broadcast([P, D])), (gamma_b[:, :], gamma.to_broadcast([P, D])),
                  (beta_b[:, :], beta.to_broadcast([P, D])), (gb_b[:, :], gate_b.to_broadcast([P, E]))]
        N_CONSTS = 16 * len(CONSTS)

        block = ctx.enter_context(nc.Block())

        @block.sync
        def _(sp):
            def load_x(c):
                for j in range(CH):
                    if not isinstance(c, int):
                        sp.wait_ge(x_in[j], 16 * c)
                    q = c * CH + j
                    sp.dma_start(X2[:, bass.ds(q, 1), :].rearrange("p a d -> p (a d)"),
                                 x[bass.ds(q * P, P), :]).then_inc(x_in[j], 16)
            load_x(0)
            for o, i in CONSTS:
                sp.dma_start(o, i).then_inc(consts_in, 16)
            chunks(sp, 1, NC, load_x)

            def store_table(c):
                sp.wait_ge(normed, CH * c + CH)
                sp.dma_start(table[bass.ds(c * (CH * P), CH * P), :].rearrange("(j p) d -> p j d", p=P),
                             X2[:, bass.ds(c * CH, CH), :]).then_inc(table_out, 16)
            chunks(sp, 0, NC, store_table)
            sp.wait_ge(table_out, 16 * NC)

            def load_tile(c, j, mix):
                q = c * CH + j
                wait(sp, tile_turned, q - CH + 1 + (NT if mix else 0))
                sp.dma_start(tile_in[:, j, :], table[bass.ds(q * P, P), :]).then_inc(tile_loaded[j], 16)
                if mix:
                    wait(sp, mix_added, q - CH + 1)
                    sp.dma_start(X2[:, bass.ds(q, 1), :].rearrange("p a d -> p (a d)"),
                                 x[bass.ds(q * P, P), :]).then_inc(x_again[j], 16)
            chunks(sp, 0, NC, lambda c: [load_tile(c, j, False) for j in range(CH)])
            chunks(sp, 0, NC, lambda c: [load_tile(c, j, True) for j in range(CH)])

            sp.wait_ge(flag_ready, 1)
            bad = sp.value_load(flag[0:1, 0:1], min_val=0, max_val=P)
            with sp.If(bad > 0):
                with sp.Fori(0, NG) as g:
                    wait(sp, gen_done, g * NW)
                    sp.dma_start(idx_gen[:, :], src[:, bass.ds(g * GT, GT)]).then_inc(gen_idx_in, 16)

            sp.wait_ge(slots_done, 1)

            def load_tiles(i):
                for s in range(2):
                    j = 2 * i + s
                    e = sp.value_load(etab[0:1, bass.ds(j, 1)], min_val=0, max_val=E - 1)
                    wait(sp, xg_turned, j - 1)
                    sp.dma_start(xg[s], xs[bass.ds(j * TS, TS), :].rearrange("(h p) d -> p h d", p=P)).then_inc(xg_in[s], 16)
                    wait(sp, relu_done, j - 1)
                    sp.dma_start(w1_sb[s], w1b[bass.ds(e, 1)].rearrange("a p w -> (a p) w")).then_inc(w1_in[s], 16)
            for q in range(CH):
                sp.wait_ge(scattered[q], 32 * NC)
            load_tiles(0)
            chunks(sp, 1, NS // 2, load_tiles)

            def store_out(c):
                for j in range(CH):
                    q = c * CH + j
                    sp.wait_ge(f_done, q + 1)
                    sp.dma_start(out[bass.ds(q * P, P), :], tile_in[:, j, :]).then_inc(f_out[j], 16)
            chunks(sp, 0, NC, store_out)
            for j in range(CH):
                sp.wait_ge(f_out[j], 16 * NC)

        @block.gpsimd
        def _(pool):
            pool.memset(ones[:], 1.0).then_inc(pool_consts, 1)
            pool.memset(eps_t[:], EPS).then_inc(pool_consts, 1)
            pool.memset(aggT[:, :, :], 0.0).then_inc(pool_consts, 1)
            pool.memset(bd[:, :, :], 0.0).then_inc(pool_consts, 1)
            pool.memset(zeros[:], 0.0).then_inc(pool_consts, 1)
            pool.iota(iota[:], [[1, GW]], base=0, channel_multiplier=0, allow_small_or_imprecise_dtypes=True).then_inc(pool_consts, 1)
            pool.wait_ge(pool_consts, 1)
            pool.affine_select(out=ident[:], in_=ones[:], compare_op=ALU.is_equal, fill=0.0, base=0,
                               pattern=[[-1, P]], channel_multiplier=1).then_inc(pool_consts, 1)
            pool.affine_select(out=upper[:], in_=ones[:], compare_op=ALU.is_gt, fill=0.0, base=0,
                               pattern=[[1, P]], channel_multiplier=-1).then_inc(pool_consts, 1)
            pool.iota(small[:, 128:129], [[0, 1]], base=0, channel_multiplier=1,
                      allow_small_or_imprecise_dtypes=True).then_inc(pool_consts, 1)

            pool.wait_ge(table_out, 16 * NC)

            def gather_block(b):
                for m in range(BT):
                    if m % (BT // 2) == 0:
                        pool.wait_ge(idx_in[m // (BT // 2)], 16 * (b + 1))
                    if (m - RING) // GT != (m - 1 - RING) // GT:
                        wait(pool, group_done, b * BG + (m - RING) // GT + 1)
                    if m % (BT // 2) == 0 or (m - RING) // GT != (m - 1 - RING) // GT:
                        pool.sem_inc(pool_past)
                    pool.indirect_dma_start(
                        out=ring[:, m % RING, :], out_offset=None, in_=table,
                        in_offset=bass.IndirectOffsetOnAxis(ap=idx[:, m // (BT // 2), m % (BT // 2):m % (BT // 2) + 1], axis=0),
                    ).then_inc(gathered[m % RING], 16)
            chunks(pool, 0, NB, gather_block)

            pool.wait_ge(flag_ready, 1)
            bad = pool.value_load(flag[0:1, 0:1], min_val=0, max_val=P)
            with pool.If(bad > 0):
                with pool.Fori(0, NG) as g:
                    pool.wait_ge(gen_idx_in, 16 * (g + 1))
                    wait(pool, group_done, NG)
                    pool.sem_inc(pool_past)
                    for t in range(GT):
                        pool.indirect_dma_start(
                            out=ring[:, t, :], out_offset=None, in_=table,
                            in_offset=bass.IndirectOffsetOnAxis(ap=idx_gen[:, t:t + 1], axis=0),
                        ).then_inc(gen_gathered[t], 16)

            pool.wait_ge(zero_out, 16 * (NC + 1))

            def scatter(c):
                pool.wait_ge(sidx_done, c + 1)
                for j in range(CH):
                    pool.wait_ge(row_ready, c * CH + j + 1)
                    pool.sem_inc(pool_past)
                    for k in range(2):
                        pool.indirect_dma_start(
                            out=xs, out_offset=bass.IndirectOffsetOnAxis(ap=sidx[:, k, j:j + 1], axis=0),
                            in_=tile_in[:, j, :], in_offset=None).then_inc(scattered[j], 16)
            chunks(pool, 0, NC, scatter)

            for s in range(2):
                pool.wait_ge(ys_out[s], 16 * (NS // 2))

            def pick(c):
                pool.wait_ge(cidx_done, c + 1)
                for j in range(CH):
                    wait(pool, x2_done, NT + c * CH + j - CH + 1)
                    pool.sem_inc(pool_past)
                    for k in range(2):
                        pool.indirect_dma_start(
                            out=ring[:, 2 * j + k, :], out_offset=None, in_=ys,
                            in_offset=bass.IndirectOffsetOnAxis(ap=sidx[:, k, j:j + 1], axis=0),
                        ).then_inc(picked[j], 16)
            chunks(pool, 0, NC, pick)

        @block.scalar
        def _(act):
            start_counters(act, LEADERS["scalar"])

            def load_idx(b, half):
                wait(act, group_done, (b - 1) * BG + (half + 1) * BG // 2)
                act.dma_start(idx[:, half, :], src[:, bass.ds(b * BT + half * (BT // 2), BT // 2)]).then_inc(idx_in[half], 16)
            load_idx(0, 0)
            load_idx(0, 1)

            act.wait_ge(pool_consts, 9)

            def norm_chunk(c):
                act.wait_ge(stats_done, c + 1)
                act.activation(rstd[:, bass.ds(c * CH, CH)], mv[:, bass.ds(c * CH, CH), 1], ACT.Sqrt,
                               bias=eps_t[:]).then_inc(std_done, 1)
                act.wait_ge(rstd_done, c + 1)
                for j in range(CH):
                    q = c * CH + j
                    act.activation(X2[:, bass.ds(q, 1), :], X2[:, bass.ds(q, 1), :], ACT.Identity,
                                   bias=nmr[:, bass.ds(q, 1)], scale=rstd[:, bass.ds(q, 1)]).then_inc(normed, 1)
            chunks(act, 0, NC, norm_chunk)

            def copy_turned(n, j):
                wait(act, tile_turned, n + 1)
                act.copy(tT[:, j % 2, :], tps).then_inc(turned_copied, 1)

            def kv_root(q, j):
                wait(act, kv_var_done, q + 1)
                act.activation(kv_var[:, j % 2, :], kv_var[:, j % 2, :], ACT.Sqrt, bias=eps_t[:],
                               scale=1.0 / DH).then_inc(kv_std_done, 1)

            def zero_slots(b):
                act.dma_start(xs[bass.ds(b * (ZR * P), ZR * P), :].rearrange("(p a) d -> p a d", p=P),
                              zeros[:].unsqueeze(1).to_broadcast([P, ZR, D])).then_inc(zero_out, 16)
            act.dma_start(ys[SLOTS:SLOTS + TS, :].rearrange("(p a) d -> p a d", p=P),
                          zeros[:].unsqueeze(1).to_broadcast([P, TS // P, D])).then_inc(zero_out, 16)

            def kv_tile(b, j, first):
                q = b * CH + j
                if j == 2:
                    zero_slots(b)
                if j == 4:
                    load_idx(b + 1, 0)
                if j == 0 and not first:
                    load_idx(b, 1)
                wait(act, kv_done, q - prior(j) + 1)
                copy_turned(q, j)
                if not (first and j == 0):
                    kv_root(q - 1, (j - 1) % CH)
                wait(act, kv_done, q + 1)
                wait(act, kv_var_done, q)
                act.activation(sq[:, :], wide[j % 2], ACT.Square).then_inc(kv_squared, 1)
                wait(act, dots_done, q - prior(j) + 1)
                act.copy(vs[:, j % 2, :], wide[j % 2][:, INNER:]).then_inc(v_copied, 1)

            for j in range(CH):
                kv_tile(0, j, True)
            chunks(act, 1, NC, lambda b: [kv_tile(b, j, False) for j in range(CH)])
            kv_root(NT - 1, CH - 1)

            act.wait_ge(t1_done, 1)
            act.copy(T1[:, :, :], wide[0].rearrange("p (j d) -> p j d", j=NJ)).then_inc(t1_copied, 1)
            act.wait_ge(m_done, 1)
            act.copy(M[:, :, :], wide[1][:, 0:KD * D].rearrange("p (k d) -> p k d", k=KD)).then_inc(m_copied, 1)

            def mix_tile(b, j):
                q = b * CH + j
                if j == 4:
                    load_idx(b + NC + 1, 0)
                if j == 0:
                    load_idx(b + NC, 1)
                wait(act, mix_done, q - prior(j) + 1)
                copy_turned(NT + q, j)
            chunks(act, 0, NC, lambda b: [mix_tile(b, j) for j in range(CH)])
            load_idx(NB - 1, 1)

            act.wait_ge(agg_final, 1)

            def gate_chunk(c):
                for j in range(CH):
                    q = c * CH + j
                    wait(act, gnn_done, q - prior(j) + 1)
                    act.copy(aT[:, j % 2, :].rearrange("p (k n) -> p k n", k=KD),
                             aggT[:, :, bass.ds(q * P, P)]).then_inc(agg_staged, 1)
                act.wait_ge(y_stats, c + 1)
                act.activation(rstd[:, bass.ds(c * CH, CH)], mv[:, bass.ds(c * CH, CH), 1], ACT.Sqrt,
                               bias=eps_t[:]).then_inc(y_std, 1)
                act.wait_ge(y_rstd, c + 1)
                for j in range(CH):
                    q = c * CH + j
                    wait(act, y_turned, q - prior(j) + 1)
                    act.activation(yt[:, j % 2, :], X2[:, bass.ds(q, 1), :], ACT.Identity,
                                   bias=nmr[:, bass.ds(q, 1)], scale=rstd[:, bass.ds(q, 1)]).then_inc(y_normed, 1)
            chunks(act, 0, NC, gate_chunk)

            act.wait_ge(exp_in, 1)
            act.activation(prob[:, 1, :], prob[:, 1, :], ACT.Exp).then_inc(exp_done, 1)

            def rows_chunk(c):
                for j in range(CH):
                    q = c * CH + j
                    if isinstance(c, int):
                        wait(act, tile_turned, 2 * NT)
                    else:
                        act.wait_ge(scattered[j], 32 * c)
                    act.activation(tile_in[:, j, :], X2[:, bass.ds(q, 1), :], ACT.Identity,
                                   bias=nmr[:, bass.ds(q, 1)], scale=rstd[:, bass.ds(q, 1)]).then_inc(row_ready, 1)
            rows_chunk(0)
            chunks(act, 1, NC, rows_chunk)

            def xg_copy(j, s):
                wait(act, xg_turned, j + 1)
                act.copy(xgT[s], ps[:, 2 + s, :].rearrange("p (k t) -> p k t", k=KD)).then_inc(xg_copied, 1)

            def moe_act(i, last=False):
                for s in range(2):
                    j = 2 * i + s
                    wait(act, l1_done, j + 1)
                    wait(act, l2_done, j - 1)
                    for f in range(FC):
                        r = act.activation(hT[s][:, f, :], wide[s][:, f * TS:(f + 1) * TS], ACT.Relu,
                                           bias=w1_sb[s][:, KD * F + f:KD * F + f + 1])
                    r.then_inc(relu_done, 1)
                    if not (last and s == 1):
                        xg_copy(j + 1, 1 - s)
                    if not (isinstance(i, int) and j == 0):
                        store_y(j - 1, 1 - s)
                    if not (last and s == 1):
                        load_w2(j + 1, 1 - s)

            def load_w2(j, s):
                e = act.value_load(etab[0:1, bass.ds(j, 1)], min_val=0, max_val=E - 1)
                wait(act, l2_done, j - 1)
                wait(act, y_done, j - 1)
                act.dma_start(w2_sb[s], w2[bass.ds(e, 1)].rearrange("a p w -> (a p) w")).then_inc(w2_in[s], 16)
                act.dma_start(b2_sb[s], b2[bass.ds(e, 1), :].to_broadcast([P, D])).then_inc(w2_in[s], 16)

            def store_y(j, s):
                wait(act, y_done, j + 1)
                act.dma_start(ys[bass.ds(j * TS, TS), :].rearrange("(h p) d -> p h d", p=P), yo[s]).then_inc(ys_out[s], 16)
            act.wait_ge(slots_done, 1)
            load_w2(0, 0)
            xg_copy(0, 0)
            moe_act(0)
            chunks(act, 1, NS // 2 - 1, moe_act)
            moe_act(NS // 2 - 1, last=True)
            store_y(NS - 1, 1)

            def out_chunk(c):
                for j in range(CH):
                    q = c * CH + j
                    if isinstance(c, int):
                        act.wait_ge(scattered[j], 32 * NC)
                    else:
                        act.wait_ge(f_out[j], 16 * c)
                    act.activation(tile_in[:, j, :], X2[:, bass.ds(q, 1), :], ACT.Identity,
                                   bias=nmr[:, bass.ds(q, 1)], scale=rstd[:, bass.ds(q, 1)]).then_inc(y_again, 1)
                act.wait_ge(f_stats, c + 1)
                act.activation(small[:, 8:8 + CH], small[:, 16:16 + CH], ACT.Sqrt, bias=eps_t[:]).then_inc(f_std, 1)
                act.wait_ge(f_rstd, c + 1)
                for j in range(CH):
                    act.activation(tile_in[:, j, :], tile_in[:, j, :], ACT.Identity,
                                   bias=small[:, 32 + j:33 + j], scale=small[:, 24 + j:25 + j]).then_inc(f_normed, 1)
            out_chunk(0)
            chunks(act, 1, NC, out_chunk)

        @block.vector
        def _(dve):
            start_counters(dve, LEADERS["vector"])

            def stats_chunk(c):
                for j in range(CH):
                    dve.wait_ge(x_in[j], 16 * (c + 1))
                    dve.sem_inc(dve_past)
                    dve.bn_stats(bn[:, j, :], X2[:, bass.ds(c * CH + j, 1), :].rearrange("p a d -> p (a d)"))
                dve.drain()
                for j in range(CH):
                    dve.bn_aggr(mvc[:, j, :], bn[:, j, :])
                dve.drain()
                dve.tensor_copy(mv[:, bass.ds(c * CH, CH), :], mvc[:, :, :]).then_inc(stats_done, 1)
                dve.wait_ge(std_done, c + 1)
                cols = bass.ds(c * CH, CH)
                dve.reciprocal(rstd[:, cols], rstd[:, cols])
                dve.drain()
                dve.scalar_tensor_tensor(out=nmr[:, cols], in0=mv[:, cols, 0], scalar=-1.0, in1=rstd[:, cols],
                                         op0=ALU.mult, op1=ALU.mult).then_inc(rstd_done, 1)
            chunks(dve, 0, NC, stats_chunk)

            dve.wait_ge(consts_in, N_CONSTS)
            dve.wait_ge(pool_consts, 9)
            dve.tensor_copy(base_f[:], base_i[:])
            dve.tensor_copy(dstrel[:, :], dstrel[:, :].bitcast(I32))
            dve.drain()
            dve.tensor_scalar(base_f[:], base_f[:], float(NP - W), None, ALU.min)
            dve.drain()
            dve.tensor_copy(base_i[:], base_f[:])
            d3 = dstrel[:, :].rearrange("p (g t) -> p g t", t=GT)
            dve.tensor_tensor(d3, d3, base_f[:, :].unsqueeze(2).to_broadcast([P, NG, GT]), ALU.subtract)
            dve.drain()
            dve.tensor_reduce(small[:, 0:1], dstrel[:, :], AX.X, ALU.max)
            dve.tensor_reduce(small[:, 1:2], dstrel[:, :], AX.X, ALU.min)
            dve.drain()
            dve.tensor_scalar(small[:, 2:3], small[:, 0:1], float(W), None, ALU.is_ge)
            dve.tensor_scalar(small[:, 3:4], small[:, 1:2], 0.0, None, ALU.is_lt)
            dve.drain()
            dve.tensor_tensor(small[:, 4:5], small[:, 2:3], small[:, 3:4], ALU.max).then_inc(bad_found, 1)
            dve.wait_ge(bad_counted, 1)
            dve.tensor_copy(flag[:, :], ps[0:1, 3, 0:1]).then_inc(flag_ready, 1)
            w3 = wkv_sb[:, :, :].rearrange("p k (h d) -> p (k h) d", d=DH)
            m3 = sq[:, 0:KD * 2 * HEADS]
            dve.tensor_reduce(m3, w3, AX.X, ALU.add)
            dve.drain()
            dve.tensor_scalar(m3, m3, 1.0 / DH, None, ALU.mult)
            dve.drain()
            dve.tensor_tensor(w3, w3, m3.unsqueeze(2).to_broadcast([P, KD * 2 * HEADS, DH]), ALU.subtract)
            dve.drain().then_inc(dve_consts, 1)

            def select(b, g):
                wait(dve, group_done, b * BG + g - 1)
                for t in range(GT):
                    m = g * GT + t
                    ins = dve.tensor_scalar(S[:, m % SEL, :], iota[:, 0:W], dstrel[:, bass.ds(b * BT + m, 1)],
                                            ew[:, bass.ds(b * BT + m, 1)], ALU.is_equal, ALU.mult)
                ins.then_inc(selected, 1)

            def add_group(b, g):
                G = b * BG + g
                start = dve.value_load(base_i[0:1, bass.ds(G, 1)], min_val=0, max_val=NP - W)
                wait(dve, group_done, G + 1)
                wait(dve, group_added, G)
                win = aggT[:, :, bass.ds(start, W)]
                dve.tensor_tensor(win, win, aggps[g % 2].rearrange("p (k n) -> p k n", k=KD),
                                  ALU.add).then_inc(group_added, 1)

            def kv_stats(q, j):
                wait(dve, kv_squared, q + 1)
                dve.tensor_reduce(kv_var[:, j % 2, :], sq[:, :].rearrange("p (h d) -> p h d", d=DH), AX.X,
                                  ALU.add).then_inc(kv_var_done, 1)

            def kv_recip(q, j):
                dve.wait_ge(kv_std_done, q + 1)
                dve.reciprocal(kv_r[:, :], kv_var[:, j % 2, :]).then_inc(kv_r_done, 1)
                dve.wait_ge(kv_r_done, 2 * q + 1)
                dve.tensor_tensor(kv_s[:, j % 2, :], kv_r[:, 0:HEADS], kv_r[:, HEADS:], ALU.mult).then_inc(kv_r_done, 1)
                dve.wait_ge(kv_r_done, 2 * q + 2)
                wait(dve, dots_done, q - prior(j) + 1)
                dve.tensor_tensor(ks[:, j % 2, :].rearrange("p (h d) -> p h d", d=DH),
                                  wide[j % 2][:, 0:INNER].rearrange("p (h d) -> p h d", d=DH),
                                  kv_s[:, j % 2, :].unsqueeze(2).to_broadcast([P, HEADS, DH]),
                                  ALU.mult).then_inc(k_scaled, 1)

            def kv_step(b, j, first):
                q = b * CH + j
                head = first and j == 0
                select(b, 2 * j)
                if not head:
                    add_group(b if j else b - 1, (2 * j - 1) % BG)
                    kv_stats(q - 1, (j - 1) % CH)
                select(b, 2 * j + 1)
                add_group(b, 2 * j)
                if not head:
                    kv_recip(q - 1, (j - 1) % CH)
            for j in range(CH):
                kv_step(0, j, True)
            chunks(dve, 1, NC, lambda b: [kv_step(b, j, False) for j in range(CH)])
            kv_stats(NT - 1, CH - 1)
            kv_recip(NT - 1, CH - 1)

            wait(dve, dots_done, NT)
            for a in range(2):
                half = slice(a * DH, (a + 1) * DH)
                dve.tensor_scalar(bd[half, :, half], dotps[half, :, half], 1.0 / N, None, ALU.mult).then_inc(bd_done, 1)

            def mix_step(b0, j):
                b = b0 + NC
                q = b0 * CH + j
                select(b, 2 * j)
                add_group(b if j else b - 1, (2 * j - 1) % BG)
                dve.wait_ge(x_again[j], 16 * (b0 + 1))
                row = X2[:, bass.ds(q, 1), :].rearrange("p a d -> p (a d)")
                dve.tensor_tensor(row, row, bout_b[:], ALU.add).then_inc(x_biased, 1)
                select(b, 2 * j + 1)
                add_group(b, 2 * j)
                dve.wait_ge(x_biased, q + 1)
                wait(dve, mix_done, q + 1)
                dve.tensor_tensor(row, row, wide[j % 2][:, 0:D], ALU.add).then_inc(mix_added, 1)
            chunks(dve, 0, NC, lambda b: [mix_step(b, j) for j in range(CH)])
            for g in range(BG):
                select(NB - 1, g)
                add_group(NB - 1 if g else NB - 2, (g - 1) % BG)
            add_group(NB - 1, BG - 1)
            dve.drain()

            dve.wait_ge(flag_ready, 1)
            bad = dve.value_load(flag[0:1, 0:1], min_val=0, max_val=P)
            with dve.If(bad > 0):
                dve.memset(aggT[:, :, :], 0.0)
                dve.drain()
                with dve.Fori(0, NG) as g:
                    dve.tensor_tensor(dst_gen, dstrel[:, bass.ds(g * GT, GT)],
                                      base_f[:, bass.ds(g, 1)].to_broadcast([P, GT]), ALU.add)
                    dve.drain()
                    with dve.Fori(0, NW) as v:
                        wait(dve, gen_done, g * NW + v)
                        for t in range(GT):
                            dve.tensor_scalar(Sgen[:, t, :], iota[:, :], dst_gen[:, t:t + 1],
                                              ew[:, bass.ds(g * GT + t, 1)], ALU.is_equal, ALU.mult)
                        dve.drain().then_inc(gen_selected, 1)
                        dve.tensor_scalar(dst_gen, dst_gen, float(-GW), None, ALU.add)
                        wait(dve, gen_done, g * NW + v + 1)
                        win = aggT[:, :, bass.ds(v * GW, GW)]
                        dve.tensor_tensor(win, win, ps[:, 4:4 + KD, 0:GW], ALU.add)
                        dve.drain().then_inc(gen_added, 1)
            dve.drain().then_inc(agg_final, 1)

            def gate_chunk(c):
                for j in range(CH):
                    q = c * CH + j
                    row = X2[:, bass.ds(q, 1), :].rearrange("p a d -> p (a d)")
                    wait(dve, gnn_done, q + 1)
                    dve.tensor_tensor(row, row, wide[j % 2][:, 0:D], ALU.add).then_inc(x2_done, 1)
                    if j:
                        wait(dve, x2_done, q)
                        dve.sem_inc(dve_past)
                        dve.bn_stats(bn[:, j - 1, :], X2[:, bass.ds(q - 1, 1), :].rearrange("p a d -> p (a d)"))
                wait(dve, x2_done, c * CH + CH)
                dve.sem_inc(dve_past)
                dve.bn_stats(bn[:, CH - 1, :], X2[:, bass.ds(c * CH + CH - 1, 1), :].rearrange("p a d -> p (a d)"))
                dve.drain()
                for j in range(CH):
                    dve.bn_aggr(mvc[:, j, :], bn[:, j, :])
                dve.drain()
                dve.tensor_copy(mv[:, bass.ds(c * CH, CH), :], mvc[:, :, :]).then_inc(y_stats, 1)
                dve.wait_ge(y_std, c + 1)
                cols = bass.ds(c * CH, CH)
                dve.reciprocal(rstd[:, cols], rstd[:, cols])
                dve.drain()
                dve.scalar_tensor_tensor(out=nmr[:, cols], in0=mv[:, cols, 0], scalar=-1.0, in1=rstd[:, cols],
                                         op0=ALU.mult, op1=ALU.mult).then_inc(y_rstd, 1)

                def logit(j):
                    q = c * CH + j
                    wait(dve, gate_done, q + 1)
                    dve.tensor_tensor(logits[:, j, :], aggps[j % 2][:, 0:E], gb_b[:], ALU.add).then_inc(logit_done, 1)
                for j in range(CH):
                    q = c * CH + j
                    wait(dve, y_turned, q + 1)
                    wait(dve, gate_done, q - prior(j) + 1)
                    dve.tensor_copy(tT[:, j % 2, :], yps[j % 2]).then_inc(y_copied, 1)
                    if j:
                        logit(j - 1)
                logit(CH - 1)
                dve.drain()
                for j in range(CH):
                    dve.max(out=top8[:, j, :], in_=logits[:, j, :])
                dve.drain()
                for j in range(CH):
                    dve.max_index(out=top8_i[:, j, :], in_max=top8[:, j, :], in_values=logits[:, j, :])
                dve.drain()
                dve.tensor_copy(top[:, :, cols], top8[:, :, 0:2].rearrange("p j k -> p k j"))
                dve.tensor_copy(slot_f[:, :, cols], top8_i[:, :, 0:2].rearrange("p j k -> p k j"))
            chunks(dve, 0, NC, gate_chunk)
            dve.drain()

            dve.tensor_tensor(prob[:, 1, :], top[:, 1, :], top[:, 0, :], ALU.subtract)
            dve.drain().then_inc(exp_in, 1)

            for k in range(2):
                dve.memset(slot_f[:, k, NT:], 0.0)
            for e in range(E):
                dve.memset(iota_e[:, e, :], float(e))
            pidx, pad, dummy = small[:, 128:129], small[:, 129:130], small[:, 130:131]
            dve.tensor_scalar(pad, pidx, float(P - PADDED), None, ALU.is_ge)
            dve.tensor_scalar(dummy, pidx, 2.0, float(SLOTS), ALU.mult, ALU.add)
            dve.drain()
            for k, H in enumerate((H1, H2)):
                dve.tensor_tensor(H, iota_e, slot_f[:, k, 0:NT].unsqueeze(1).to_broadcast([P, E, NT]), ALU.is_equal)
            dve.tensor_scalar(small[:, 131:132], pad, -1.0, 1.0, ALU.mult, ALU.add)
            dve.drain()
            for H in (H1, H2):
                dve.tensor_scalar(H[:, :, NT - 1], H[:, :, NT - 1], small[:, 131:132], None, ALU.mult)
            dve.drain()
            dve.tensor_tensor(Hs, H1, H2, ALU.add).then_inc(hot_done, 1)
            dve.wait_ge(ranked, 1)
            half = E // 2
            for a in range(2):
                dve.tensor_copy(tot[:, a * half:(a + 1) * half, :],
                                ps[:, 6 + a, 0:half * NT].rearrange("p (e i) -> p e i", i=NT))
            dve.drain()
            flat = lambda t: t.rearrange("p e i -> p (e i)")
            dve.tensor_tensor_scan(flat(scan), flat(tot), flat(tot), 0.0, ALU.add, ALU.max)
            dve.drain()
            ends = scan[:, :, NT - 1]
            cnt, pads, aend, adj = (small[:, 16 * i:16 * i + 16] for i in range(2, 6))
            dve.tensor_copy(cnt, ends)
            dve.drain()
            dve.tensor_tensor(cnt[:, 1:E], ends[:, 1:E], ends[:, 0:E - 1], ALU.subtract)
            dve.drain()
            cnt_i = small[:, 96:112].bitcast(I32)
            dve.tensor_scalar(cnt_i, cnt, float(TS - 1), None, ALU.add)
            dve.drain()
            shift = TS.bit_length() - 1
            dve.tensor_scalar(cnt_i, cnt_i, shift, None, ALU.arith_shift_right)
            dve.drain()
            dve.tensor_copy(pads, cnt_i)
            dve.drain()
            dve.tensor_tensor_scan(aend, pads, pads, 0.0, ALU.add, ALU.max)
            dve.drain()
            dve.tensor_tensor(adj, aend, pads, ALU.subtract)
            dve.tensor_tensor(cnt, ends, cnt, ALU.subtract)
            dve.drain()
            dve.scalar_tensor_tensor(out=adj, in0=adj, scalar=float(TS), in1=cnt, op0=ALU.mult, op1=ALU.subtract)
            dve.tensor_tensor(scan, scan, tot, ALU.subtract)
            dve.drain()
            dve.tensor_tensor(pos, scan, adj.unsqueeze(2).to_broadcast([P, E, NT]), ALU.add)
            dve.drain()
            for a in range(2):
                e = slice(a * half, (a + 1) * half)
                dve.tensor_tensor(pos[:, e, :], pos[:, e, :],
                                  ps[:, 4 + a, 0:half * NT].rearrange("p (e i) -> p e i", i=NT), ALU.add)
            dve.drain()
            for k, H in enumerate((H1, H2)):
                dve.tensor_tensor(H, H, pos, ALU.mult)
            dve.drain()
            for k, H in enumerate((H1, H2)):
                dve.tensor_reduce(slot_f[:, k, 0:NT], H.rearrange("p e i -> p i e"), AX.X, ALU.add)
            dve.drain()
            for k in range(2):
                dve.tensor_scalar(small[:, 132 + k:133 + k], dummy, float(k), None, ALU.add)
            dve.drain()
            for k in range(2):
                dve.tensor_tensor(small[:, 134 + k:135 + k], small[:, 132 + k:133 + k], pad, ALU.mult)
            dve.drain()
            for k in range(2):
                dve.tensor_tensor(slot_f[:, k, NT - 1:NT], slot_f[:, k, NT - 1:NT], small[:, 134 + k:135 + k], ALU.add)
            jj = top[:, :, :].rearrange("p a b -> p (a b)")[0:1, 0:NS]
            dve.tensor_tensor(cmp_t[0:1], iota[0:1, 0:NS].unsqueeze(2).to_broadcast([1, NS, E]),
                              aend[0:1].unsqueeze(1).to_broadcast([1, NS, E]), ALU.is_ge)
            dve.drain()
            dve.tensor_reduce(jj, cmp_t[0:1], AX.X, ALU.add)
            dve.drain()
            dve.tensor_scalar(etab[:, :], jj, float(E - 1), None, ALU.min)
            dve.wait_ge(exp_done, 1)
            dve.tensor_scalar(prob[:, 0, :], prob[:, 1, :], 1.0, None, ALU.add)
            dve.drain()
            dve.reciprocal(prob[:, 0, :], prob[:, 0, :])
            dve.drain()
            dve.tensor_tensor(prob[:, 1, :], prob[:, 1, :], prob[:, 0, :], ALU.mult)
            dve.drain().then_inc(slots_done, 1)

            def slots_chunk(c):
                if not isinstance(c, int):
                    for j in range(CH):
                        dve.wait_ge(scattered[j], 32 * c)
                dve.tensor_copy(sidx[:, :, :], slot_f[:, :, bass.ds(c * CH, CH)]).then_inc(sidx_done, 1)
            slots_chunk(0)
            chunks(dve, 1, NC, slots_chunk)

            def moe_y(j, s, skip=False):
                if skip:
                    return
                wait(dve, l2_done, j + 1)
                dve.wait_ge(w2_in[s], 32 * (j // 2 + 1) if isinstance(j, int) else 16 * (j + 2 - s))
                dve.tensor_tensor(yo[s], aggps_y[s], b2_sb[s].unsqueeze(1).to_broadcast([P, 2, D]), ALU.add).then_inc(y_done, 1)
            aggps_y = [ps[:, i, :].rearrange("p (h d) -> p h d", h=2) for i in range(2)]

            def moe_dve(i):
                for s in range(2):
                    if not isinstance(i, int):
                        dve.wait_ge(ys_out[s], 16 * i)
                    moe_y(2 * i + s, s)
            moe_dve(0)
            chunks(dve, 1, NS // 2, moe_dve)

            for j in range(CH):
                dve.wait_ge(scattered[j], 32 * NC)

            dve.tensor_copy(sidx[:, :, :], slot_f[:, :, 0:CH]).then_inc(cidx_done, 1)

            def out_chunk(c):
                for j in range(CH):
                    dve.wait_ge(picked[j], 32 * (c + 1))
                dve.tensor_copy(sidx[:, :, :], slot_f[:, :, bass.ds(c * CH + CH, CH)]).then_inc(cidx_done, 1)
                for k in range(2):
                    for j in range(CH):
                        q = c * CH + j
                        if k == 0:
                            dve.wait_ge(y_again, q + 1)
                        ins = dve.scalar_tensor_tensor(out=tile_in[:, j, :], in0=ring[:, 2 * j + k, :],
                                                       scalar=prob[:, k, bass.ds(q, 1)], in1=tile_in[:, j, :],
                                                       op0=ALU.mult, op1=ALU.add)
                        if k == 1:
                            ins.then_inc(x2_done, 1)
                    dve.drain()
                for j in range(CH):
                    dve.bn_stats(bn[:, j, :], tile_in[:, j, :])
                dve.drain()
                for j in range(CH):
                    dve.bn_aggr(mvc[:, j, :], bn[:, j, :])
                dve.drain()
                dve.tensor_copy(small[:, 16:16 + CH], mvc[:, :, 1])
                dve.drain().then_inc(f_stats, 1)
                dve.wait_ge(f_std, c + 1)
                dve.reciprocal(small[:, 24:24 + CH], small[:, 8:8 + CH])
                dve.drain()
                dve.scalar_tensor_tensor(out=small[:, 32:32 + CH], in0=mvc[:, :, 0], scalar=-1.0,
                                         in1=small[:, 24:24 + CH], op0=ALU.mult, op1=ALU.mult).then_inc(f_rstd, 1)
                for j in range(CH):
                    row = X2[:, bass.ds(c * CH + j, 1), :].rearrange("p a d -> p (a d)")
                    dve.tensor_tensor(row, row, beta_b[:], ALU.add)
                for j in range(CH):
                    dve.wait_ge(f_normed, c * CH + j + 1)
                    dve.tensor_tensor(tile_in[:, j, :], tile_in[:, j, :], gamma_b[:], ALU.mult)
                dve.drain()
                for j in range(CH):
                    row = X2[:, bass.ds(c * CH + j, 1), :].rearrange("p a d -> p (a d)")
                    dve.tensor_tensor(tile_in[:, j, :], tile_in[:, j, :], row, ALU.add).then_inc(f_done, 1)
            chunks(dve, 0, NC, out_chunk)

        @block.tensor
        def _(pe):
            start_counters(pe, LEADERS["tensor"])

            def edge_group(b, g):
                pe.wait_ge(selected, b * BG + g + 1)
                wait(pe, group_added, b * BG + g - 1)
                for t in range(GT):
                    m = g * GT + t
                    pe.wait_ge(gathered[m % RING], 16 * (b * (BT // RING) + m // RING + 1))
                    for f in range(KD):
                        mm = pe.matmul(aggps[g % 2][:, f * W:(f + 1) * W], ring[:, m % RING, f * P:(f + 1) * P],
                                       S[:, m % SEL, :], start=(t == 0 and f == 0), stop=(t == GT - 1),
                                       skip_group_check=True)
                mm.then_inc(group_done, 1)

            def turn(n, c, j, passes):
                pe.wait_ge(tile_loaded[j], 16 * (c + 1 + passes * NC))
                wait(pe, turned_copied, n)
                for k in range(KD):
                    mm = pe.transpose(tps[:, k * P:(k + 1) * P], tile_in[:, j, k * P:(k + 1) * P], ident[:])
                mm.then_inc(tile_turned, 1)

            def kv_mm(q, j):
                wait(pe, turned_copied, q + 1)
                wait(pe, k_scaled, q - prior(j) + 1)
                wait(pe, v_copied, q - prior(j) + 1)
                for h in range(2):
                    for k in range(KD):
                        mm = pe.matmul(wide[j % 2][:, h * 512:(h + 1) * 512], tT[:, j % 2, k * P:(k + 1) * P],
                                       wkv_sb[:, k, h * 512:(h + 1) * 512], start=(k == 0), stop=(k == KD - 1))
                mm.then_inc(kv_done, 1)

            def dots(q, j, first):
                wait(pe, k_scaled, q + 1)
                wait(pe, v_copied, q + 1)
                for a in range(NJ):
                    mm = pe.matmul(dotps[:, a, :], vs[:, j % 2, a * P:(a + 1) * P], ks[:, j % 2, a * P:(a + 1) * P],
                                   start=(first and a == 0), stop=False, skip_group_check=True)
                mm.then_inc(dots_done, 1)

            def kv_step(b, j, first):
                q = b * CH + j
                edge_group(b, 2 * j)
                turn(q, b, j, 0)
                edge_group(b, 2 * j + 1)
                kv_mm(q, j)
                if not (first and j == 0):
                    dots(q - 1, (j - 1) % CH, first and j == 1)

            pe.wait_ge(pool_consts, 9)
            pe.wait_ge(bad_found, 1)
            pe.matmul(ps[:, 3, 0:1], ones[:], small[:, 4:5], start=True, stop=True).then_inc(bad_counted, 1)
            pe.wait_ge(dve_consts, 1)
            for j in range(CH):
                kv_step(0, j, True)
            chunks(pe, 1, NC, lambda b: [kv_step(b, j, False) for j in range(CH)])
            dots(NT - 1, CH - 1, False)

            pe.wait_ge(bd_done, 2)
            for a in range(NJ):
                mm = pe.matmul(wide[0][:, a * D:(a + 1) * D], bd[:, a, :], wout_sb[:, a, :], start=True, stop=True)
            mm.then_inc(t1_done, 1)
            pe.wait_ge(t1_copied, 1)
            for k in range(KD):
                for a in range(NJ):
                    mm = pe.matmul(wide[1][:, k * D:(k + 1) * D], wq_sb[:, a, k * P:(k + 1) * P], T1[:, a, :],
                                   start=(a == 0), stop=(a == NJ - 1))
            mm.then_inc(m_done, 1)
            pe.wait_ge(m_copied, 1)

            def mix_step(b0, j):
                q = b0 * CH + j
                edge_group(b0 + NC, 2 * j)
                turn(NT + q, b0, j, 1)
                edge_group(b0 + NC, 2 * j + 1)
                wait(pe, turned_copied, NT + q + 1)
                wait(pe, mix_added, q - prior(j) + 1)
                for k in range(KD):
                    mm = pe.matmul(wide[j % 2][:, 0:D], tT[:, j % 2, k * P:(k + 1) * P], M[:, k, :],
                                   start=(k == 0), stop=(k == KD - 1))
                mm.then_inc(mix_done, 1)
            chunks(pe, 0, NC, lambda b: [mix_step(b, j) for j in range(CH)])
            for g in range(BG):
                edge_group(NB - 1, g)

            wait(pe, mix_added, NT)
            pe.wait_ge(flag_ready, 1)
            bad = pe.value_load(flag[0:1, 0:1], min_val=0, max_val=P)
            with pe.If(bad > 0):
                with pe.Fori(0, NG) as g:
                    with pe.Fori(0, NW) as v:
                        for t in range(GT):
                            pe.wait_ge(gen_gathered[t], 16 * (g + 1))
                        pe.wait_ge(gen_selected, g * NW + v + 1)
                        wait(pe, gen_added, g * NW + v)
                        for t in range(GT):
                            for f in range(KD):
                                mm = pe.matmul(ps[:, 4 + f, 0:GW], ring[:, t, f * P:(f + 1) * P], Sgen[:, t, :],
                                               start=(t == 0), stop=(t == GT - 1), skip_group_check=True)
                        mm.then_inc(gen_done, 1)

            def gate_chunk(c):
                for j in range(CH):
                    q = c * CH + j
                    pe.wait_ge(agg_staged, q + 1)
                    wait(pe, x2_done, q - prior(j) + 1)
                    for k in range(KD):
                        mm = pe.matmul(wide[j % 2][:, 0:D], aT[:, j % 2, k * P:(k + 1) * P], gnn_sb[:, k, :],
                                       start=(k == 0), stop=(k == KD - 1))
                    mm.then_inc(gnn_done, 1)

                def gate(j):
                    q = c * CH + j
                    wait(pe, y_copied, q + 1)
                    wait(pe, logit_done, q - prior(j) + 1)
                    for k in range(KD):
                        mm = pe.matmul(aggps[j % 2][:, 0:96], tT[:, j % 2, k * P:(k + 1) * P], gate_sb[:, k, :],
                                       start=(k == 0), stop=(k == KD - 1))
                    mm.then_inc(gate_done, 1)
                for j in range(CH):
                    q = c * CH + j
                    pe.wait_ge(y_normed, q + 1)
                    wait(pe, y_copied, q - prior(j) + 1)
                    for k in range(KD):
                        mm = pe.transpose(yps[j % 2][:, k * P:(k + 1) * P], yt[:, j % 2, k * P:(k + 1) * P], ident[:])
                    mm.then_inc(y_turned, 1)
                    if j:
                        gate(j - 1)
                gate(CH - 1)
            chunks(pe, 0, NC, gate_chunk)

            pe.wait_ge(hot_done, 1)
            for a in range(2):
                rows = Hs.rearrange("p e i -> p (e i)")[:, a * (R // 2):(a + 1) * (R // 2)]
                pe.matmul(ps[:, 4 + a, 0:R // 2], upper[:], rows, start=True, stop=True)
                mm = pe.matmul(ps[:, 6 + a, 0:R // 2], ones[:], rows, start=True, stop=True)
            mm.then_inc(ranked, 1)

            def xg_turn(j, s):
                pe.wait_ge(xg_in[s], 16 * (j // 2 + 1) if isinstance(j, int) else 8 * (j + 2 - s))
                wait(pe, xg_copied, j - 1)
                for h in range(2):
                    for k in range(KD):
                        mm = pe.transpose(ps[:, 2 + s, k * TS + h * P:k * TS + (h + 1) * P],
                                          xg[s][:, h, k * P:(k + 1) * P], ident[:])
                mm.then_inc(xg_turned, 1)

            def layer1(j, s):
                wait(pe, xg_copied, j + 1)
                wait(pe, relu_done, j - 1)
                pe.wait_ge(w1_in[s], 16 * (j // 2 + 1) if isinstance(j, int) else 8 * (j + 2 - s))
                for f in range(FC):
                    for k in range(KD):
                        mm = pe.matmul(wide[s][:, f * TS:(f + 1) * TS],
                                       w1_sb[s][:, k * F + f * P:k * F + (f + 1) * P], xgT[s][:, k, :],
                                       start=(k == 0), stop=(k == KD - 1))
                mm.then_inc(l1_done, 1)

            def layer2(j, s):
                wait(pe, relu_done, j + 1)
                wait(pe, y_done, j - 1)
                pe.wait_ge(w2_in[s], 32 * (j // 2 + 1) if isinstance(j, int) else 16 * (j + 2 - s))
                for h in range(2):
                    for f in range(FC):
                        mm = pe.matmul(ps[:, s, h * D:(h + 1) * D], hT[s][:, f, h * P:(h + 1) * P],
                                       w2_sb[s][:, f * D:(f + 1) * D], start=(f == 0), stop=(f == FC - 1))
                mm.then_inc(l2_done, 1)

            def moe(i, last=False):
                for s in range(2):
                    j = 2 * i + s
                    layer1(j, s)
                    if not (last and s == 1):
                        xg_turn(j + 1, 1 - s)
                    if not (isinstance(i, int) and i == 0 and s == 0):
                        layer2(j - 1, 1 - s)
            xg_turn(0, 0)
            moe(0)
            chunks(pe, 1, NS // 2 - 1, moe)
            moe(NS // 2 - 1, last=True)
            layer2(NS - 1, 1)


def kernel(x, src, dst, edge_weight, L0_gnn_weight, L0_mix_Wqkv, L0_mix_Wout, L0_mix_bout,
           L0_ffn_gate_w, L0_ffn_gate_b, L0_ffn_w1, L0_ffn_b1, L0_ffn_w2, L0_ffn_b2, L0_ffn_gamma,
           L0_ffn_beta):
    import numpy as np
    import concourse.bacc as bacc
    from concourse.bass_utils import run_bass_kernel_spmd

    def pad(a, n, value):
        a = np.asarray(a)
        return np.concatenate([a, np.full((n - len(a),) + a.shape[1:], value, a.dtype)])

    def by_partition(w):
        w = np.asarray(w)
        return np.ascontiguousarray(w.reshape(-1, P, w.shape[1]).transpose(1, 0, 2))

    n_edges = ET * P
    src_p, dst_p = pad(src, n_edges, 0), pad(dst, n_edges, N - 1)
    wqkv = np.asarray(L0_mix_Wqkv)
    gate_w = np.zeros((D, 96), np.float32)
    gate_w[:, :E] = np.asarray(L0_ffn_gate_w)
    w1 = np.asarray(L0_ffn_w1).reshape(E, KD, P, F).transpose(0, 2, 1, 3).reshape(E, P, KD * F)
    b1 = np.asarray(L0_ffn_b1).reshape(E, FC, P).transpose(0, 2, 1)
    arrays = {
        "x": pad(x, NP, 0),
        "src": src_p.reshape(ET, P).T, "dst": dst_p.reshape(ET, P).T,
        "first_dst": dst_p[::GT * P].reshape(1, NG),
        "edge_w": pad(edge_weight, n_edges, 0).reshape(ET, P).T,
        "gnn_w": by_partition(L0_gnn_weight),
        "wkv": by_partition(wqkv[INNER:].T), "wq": by_partition(wqkv[:INNER]),
        "wout": by_partition(np.asarray(L0_mix_Wout).T),
        "bout": np.asarray(L0_mix_bout).reshape(1, D),
        "gate_w": by_partition(gate_w), "gate_b": np.asarray(L0_ffn_gate_b).reshape(1, E),
        "w1b": np.concatenate([w1, b1], axis=2),
        "w2": np.asarray(L0_ffn_w2).reshape(E, FC, P, D).transpose(0, 2, 1, 3).reshape(E, P, W2ROW),
        "b2": np.asarray(L0_ffn_b2),
        "gamma": np.asarray(L0_ffn_gamma).reshape(1, D), "beta": np.asarray(L0_ffn_beta).reshape(1, D),
    }
    nc = bacc.Bacc("TRN2", target_bir_lowering=False, num_devices=1)
    feed, args = {}, {}
    for name, a in arrays.items():
        a = np.ascontiguousarray(a)
        feed[f"in_{name}"] = a
        args[name] = nc.dram_tensor(f"in_{name}", a.shape, mybir.dt.from_np(a.dtype), kind="ExternalInput").ap()
    args["out"] = nc.dram_tensor("result", (NP, D), F32, kind="ExternalOutput").ap()
    gps_layer(nc, **args)
    r = run_bass_kernel_spmd(nc, [feed], core_ids=[0])
    return r.results[0]["result"][:N]
```

```python
from contextlib import ExitStack

import concourse.bass as bass
from concourse import mybir

F32 = mybir.dt.float32
I32 = mybir.dt.int32
U32 = mybir.dt.uint32
ALU = mybir.AluOpType
ACT = mybir.ActivationFunctionType
AX = mybir.AxisListType

P = 128
N = 6250
D = 256
KD = D // P
CH = 7
NC = 7
NT = NC * CH
NP = NT * P
PADDED = NP - N
HEADS, DH = 8, 64
INNER = HEADS * DH
NJ = INNER // P
EPS = 1e-5

EDGES = 106250
GT = 4
BG = 2 * CH
BT = BG * GT
NB = -(-EDGES // (BT * P))
NG = NB * BG
ET = NB * BT
HG = CH
HB = BT // 2
RING = 14
W = 128
GW = 448
NW = NP // GW

E, F = 16, 512
FC = F // P
TS = 256
CA = 3
NA = CA * CH * P
B0 = NC
ROUNDS = NC - CA - 1
STARTS = [(B0, CA)] + [(B0 + 3 + 2 * i, CA + 1 + i) for i in range(ROUNDS)]


def expert_tiles(rows, multiple):
    return -(-((rows + E * (TS - 1)) // TS) // multiple) * multiple


SA = expert_tiles(2 * NA, 6)
PER = 6
LATE = SA - PER * ROUNDS
SB = expert_tiles(2 * (N - NA), 2)
NS = SA + SB
XROWS = [SA * TS, SB * TS + TS]
ZR = [-(-n // (NC * P)) for n in XROWS]
assert HB % RING == 0 and NB == B0 + 2 + 2 * ROUNDS
W1ROW = KD * F + FC
W2ROW = FC * D
W2BROW = W2ROW + D

LEAD = BG


def gps_layer(nc, x, src, dst, first_dst, edge_w, gnn_w, wkv, wq, wout, bout, gate_w, gate_b,
              w1b, w2b, gamma, beta, out):
    table = nc.dram_tensor("normed_rows", (NP, D), F32, kind="Internal").ap()
    xs = [nc.dram_tensor(f"rows_by_slot{i}", (NC * ZR[i] * P, D), F32, kind="Internal").ap() for i in range(2)]
    ys = [nc.dram_tensor(f"results_by_slot{i}", (XROWS[i], D), F32, kind="Internal").ap() for i in range(2)]

    with ExitStack() as ctx:
        def sb(name, shape, dt=F32):
            return ctx.enter_context(nc.sbuf_tensor(name, shape, dt))

        def sem(name):
            return ctx.enter_context(nc.semaphore(name))

        def sems(name, n):
            return [sem(f"{name}{i}") for i in range(n)]

        X2 = sb("X2", [P, NT, D])
        aggT = sb("aggT", [P, KD, NP])
        ring = sb("ring", [P, RING, D])
        S = sb("S", [P, RING, W])
        gnn_sb = sb("gnn_sb", [P, KD, D])
        M = sb("M", [P, KD, D])

        R = E * max(CA, NC - CA) * CH
        room = sb("room", [P, max(KD * 2 * INNER + 3 * NJ * D + NJ * P + 3 * 2 * INNER,
                                  2 * (W1ROW + W2BROW + FC * TS + 2 * D + KD * TS) + R)])

        def carve(space):
            at = [0]

            def take(*shape):
                n = 1
                for k in shape:
                    n *= k
                at[0] += n
                assert at[0] <= space.shape[1]
                piece = space[:, at[0] - n:at[0]]
                return piece if len(shape) == 1 else piece.rearrange("p (a b) -> p a b", a=shape[0])
            return take
        take = carve(room[:, :])
        wkv_sb = take(KD, 2 * INNER)
        wq_sb = take(NJ, D)
        wout_sb = take(NJ, D)
        T1 = take(NJ, D)
        bd = take(NJ, P)
        sq = take(2 * INNER)
        ks = take(2, INNER)
        vs = take(2, INNER)
        dstrel = sb("dstrel", [P, ET])
        ew = sb("ew", [P, ET])
        src_sb = sb("src_sb", [P, ET], I32)
        idx = sb("idx", [P, 2, HB], I32)
        base_i = sb("base_i", [P, NG], I32)
        base_f = sb("base_f", [P, NG])
        tile_in = sb("tile_in", [P, CH, D])
        tT = sb("tT", [P, 2, D])
        aT = sb("aT", [P, 2, D])
        yT = sb("yT", [P, 2, D])
        yt = sb("yt", [P, 2, D])
        ident = sb("ident", [P, P])
        iota = sb("iota", [P, GW])
        ones = sb("ones", [P, P])
        upper = sb("upper", [P, P])
        gate_sb = sb("gate_sb", [P, KD, 96])
        bout_b = sb("bout_b", [P, D])
        gamma_b = sb("gamma_b", [P, D])
        beta_b = sb("beta_b", [P, D])
        gb_b = sb("gb_b", [P, E])
        logits = sb("logits", [P, CH, E])
        top8 = sb("top8", [P, CH, 8])
        top8_i = sb("top8_i", [P, CH, 8], U32)
        top = sb("top", [P, 2, NT])
        bn = sb("bn", [P, CH, 6])
        mv = sb("mv", [P, NT, 2])
        mvc = sb("mvc", [P, CH, 2])
        rstd = sb("rstd", [P, NT])
        nmr = sb("nmr", [P, NT])
        kv_var = sb("kv_var", [P, 2, 2 * HEADS])
        kv_r = sb("kv_r", [P, 2 * HEADS])
        kv_s = sb("kv_s", [P, 2, HEADS])
        eps_t = sb("eps_t", [P, 1])
        slot_f = sb("slot_f", [P, 2, NT + CH])
        zeros = sb("zeros", [P, D])
        prob = sb("prob", [P, 2, NT])
        slot_i = sb("slot_i", [P, 2, NT], I32)
        sidx = sb("sidx", [P, 2, CH], I32)
        ay = sb("ay", [P, D])
        cy = sb("cy", [P, D])
        etab = sb("etab", [1, NS], I32)
        taken = sb("taken", [1, NS], I32)
        small = sb("small", [P, 160])
        flag = sb("flag", [1, 1], I32)
        idx_gen = sb("idx_gen", [P, GT], I32)

        take = carve(room[:, :])
        w1_sb = [take(W1ROW) for _ in range(2)]
        w2_sb = [take(W2BROW) for _ in range(2)]
        hT = [take(FC, TS) for _ in range(2)]
        xg = [take(2, D) for _ in range(2)]
        xgT = [take(KD, TS) for _ in range(2)]
        tot = take(R)
        take = carve(aggT[:, 0, 0:NA])
        yo = [take(2, D) for _ in range(2)]
        H1, H2 = [take(R) for _ in range(2)]
        take = carve(aggT[:, 1, 0:NA])
        Hs, pos, scan, iota_e = [take(R) for _ in range(4)]
        cmp_t = take(max(SA, SB), E)
        Sgen = X2[:, :, :].rearrange("p q d -> p (q d)")[:, 0:GT * GW].rearrange("p (t w) -> p t w", t=GT)
        dst_gen = kv_r[:, 0:GT]

        ps = ctx.enter_context(nc.psum_tensor("ps", [P, 8, 512], F32))
        aggps = [ps[:, i, 0:KD * W] for i in range(2)]
        tps = ps[:, 2, 0:D]
        yps = ps[:, 3, 0:D]
        xgps = ps[:, 2, :]
        outps = ps[:, 3, :]
        dotps = ps[:, 3, :].rearrange("p (j e) -> p j e", j=NJ)
        wide = [ps[:, 4 + 2 * i:6 + 2 * i, :].rearrange("p a b -> p (a b)") for i in range(2)]

        consts_in = sem("consts_in")
        pool_consts = sem("pool_consts")
        dve_consts = sem("dve_consts")
        x_in = sems("x_in", CH)
        stats_done = sem("stats_done")
        std_done = sem("std_done")
        rstd_done = sem("rstd_done")
        normed = sem("normed")
        table_out = sem("table_out")
        idx_staged = sem("idx_staged")
        gathered = sems("gathered", RING)
        selected = sem("selected")
        group_done = sem("group_done")
        group_added = sem("group_added")
        tile_loaded = sems("tile_loaded", CH)
        tile_turned = sem("tile_turned")
        turned_copied = sem("turned_copied")
        kv_done = sem("kv_done")
        kv_squared = sem("kv_squared")
        v_copied = sem("v_copied")
        kv_var_done = sem("kv_var_done")
        kv_std_done = sem("kv_std_done")
        kv_r_done = sem("kv_r_done")
        k_scaled = sem("k_scaled")
        dots_done = sem("dots_done")
        bd_done = sem("bd_done")
        t1_done = sem("t1_done")
        t1_copied = sem("t1_copied")
        m_done = sem("m_done")
        m_copied = sem("m_copied")
        x_again = sems("x_again", CH)
        x_biased = sem("x_biased")
        bad_found = sem("bad_found")
        bad_counted = sem("bad_counted")
        flag_ready = sem("flag_ready")
        gen_zeroed = sem("gen_zeroed")
        gen_idx_in = sem("gen_idx_in")
        gen_gathered = sems("gen_gathered", GT)
        gen_dst = sem("gen_dst")
        gen_selected = sem("gen_selected")
        gen_done = sem("gen_done")
        gen_added = sem("gen_added")
        agg_final = sem("agg_final")
        agg_staged = sem("agg_staged")
        layers_done = sem("layers_done")
        x2_done = sem("x2_done")
        y_bn = sem("y_bn")
        y_stats = sem("y_stats")
        y_std = sem("y_std")
        y_rstd = sem("y_rstd")
        y_normed = sem("y_normed")
        y_turned = sem("y_turned")
        y_copied = sem("y_copied")
        gate_done = sem("gate_done")
        logit_done = sem("logit_done")
        hot_done = sem("hot_done")
        ranked = sem("ranked")
        exp_in = sem("exp_in")
        exp_done = sem("exp_done")
        slots_done = sem("slots_done")
        zero_out = sem("zero_out")
        sidx_done = sem("sidx_done")
        row_ready = sem("row_ready")
        scattered = sems("scattered", CH)
        w1_in = sems("w1_in", 2)
        w2_in = sems("w2_in", 2)
        xg_in = sems("xg_in", 2)
        xg_turned = sem("xg_turned")
        xg_copied = sem("xg_copied")
        l1_done = sem("l1_done")
        relu_done = sem("relu_done")
        l2_done = sem("l2_done")
        y_done = sem("y_done")
        ys_out = sems("ys_out", 2)
        sidx_staged = sem("sidx_staged")
        a_picked = sem("a_picked")
        a_again = sem("a_again")
        a_stats = sem("a_stats")
        a_std = sem("a_std")
        a_rstd = sem("a_rstd")
        a_normed = sem("a_normed")
        a_summed = sem("a_summed")
        a_done = sem("a_done")
        a_out = sem("a_out")
        picked = sems("picked", CH)
        y_again = sem("y_again")
        summed = sem("summed")
        half_summed = sem("half_summed")
        f_stats = sem("f_stats")
        f_std = sem("f_std")
        f_rstd = sem("f_rstd")
        f_normed = sem("f_normed")
        f_done = sem("f_done")
        f_out = sems("f_out", CH)
        pool_past = sem("pool_past")
        dve_past = sem("dve_past")

        LEADERS = {"tensor": [group_done, gen_done, tile_turned, kv_done, dots_done, layers_done, gate_done,
                              y_turned, xg_turned, l1_done, l2_done],
                   "vector": [group_added, k_scaled, kv_var_done, x2_done, y_copied, logit_done, y_done,
                              gen_added, half_summed, summed],
                   "scalar": [v_copied, kv_squared, turned_copied, xg_copied, relu_done]}
        ahead = {s for group in LEADERS.values() for s in group}

        def wait(eng, s, n):
            eng.wait_ge(s, n + LEAD if s in ahead else n)

        def start_counters(eng, names):
            for s in names:
                eng.sem_inc(s, LEAD)

        def where_taken(eng, j, work, done, n, by=1):
            some = eng.value_load(taken[0:1, bass.ds(j, 1)], min_val=0, max_val=1)
            with eng.If(some > 0):
                work()
            with eng.Else():
                for s in done:
                    if n(s) is not None:
                        wait(eng, s, n(s))
                    eng.sem_inc(s, by)

        def before(j, s, each):
            return lambda _: None if isinstance(j, int) and j < 2 else each * (j - s)

        def prior(j):
            return 1 if j == 0 else 2

        def chunks(eng, first, last, body):
            with eng.Fori(first, last) as c:
                body(c)

        CONSTS = [(wkv_sb, wkv), (wq_sb, wq), (wout_sb, wout),
                  (gnn_sb[:, :, :], gnn_w), (ew[:, :], edge_w),
                  (gate_sb[:, :, :], gate_w), (src_sb[:, :], src), (dstrel[:, :].bitcast(I32), dst),
                  (base_i[:, :], first_dst.to_broadcast([P, NG])),
                  (bout_b[:, :], bout.to_broadcast([P, D])), (gamma_b[:, :], gamma.to_broadcast([P, D])),
                  (beta_b[:, :], beta.to_broadcast([P, D])), (gb_b[:, :], gate_b.to_broadcast([P, E]))]
        N_CONSTS = 16 * len(CONSTS)

        SHARE = [(BG * k // PER, BG * (k + 1) // PER) for k in range(PER)]
        J0 = SA - LATE

        block = ctx.enter_context(nc.Block())

        @block.sync
        def _(sp):
            def load_x(c):
                for j in range(CH):
                    if not isinstance(c, int):
                        sp.wait_ge(x_in[j], 16 * c)
                    q = c * CH + j
                    sp.dma_start(X2[:, bass.ds(q, 1), :].rearrange("p a d -> p (a d)"),
                                 x[bass.ds(q * P, P), :]).then_inc(x_in[j], 16)
            load_x(0)
            for o, i in CONSTS:
                sp.dma_start(o, i).then_inc(consts_in, 16)
            chunks(sp, 1, NC, load_x)

            def store_table(c):
                sp.wait_ge(normed, CH * c + CH)
                sp.dma_start(table[bass.ds(c * (CH * P), CH * P), :].rearrange("(j p) d -> p j d", p=P),
                             X2[:, bass.ds(c * CH, CH), :]).then_inc(table_out, 16)
            chunks(sp, 0, NC, store_table)
            sp.wait_ge(table_out, 16 * NC)

            sp.wait_ge(flag_ready, 1)
            bad = sp.value_load(flag[0:1, 0:1], min_val=0, max_val=P)
            with sp.If(bad > 0):
                with sp.Fori(0, NG) as g:
                    wait(sp, gen_done, g * NW)
                    sp.dma_start(idx_gen[:, :], src[:, bass.ds(g * GT, GT)]).then_inc(gen_idx_in, 16)

            def load_tile(c, j, again):
                q = c * CH + j
                wait(sp, tile_turned, q - CH + 1 + (NT if again else 0))
                sp.dma_start(tile_in[:, j, :], table[bass.ds(q * P, P), :]).then_inc(tile_loaded[j], 16)
                if again:
                    wait(sp, x2_done, q - CH + 1)
                    sp.dma_start(X2[:, bass.ds(q, 1), :].rearrange("p a d -> p (a d)"),
                                 x[bass.ds(q * P, P), :]).then_inc(x_again[j], 16)
            chunks(sp, 0, NC, lambda c: [load_tile(c, j, False) for j in range(CH)])
            chunks(sp, 0, CA, lambda c: [load_tile(c, j, True) for j in range(CH)])

            def load_rows(part, j, s):
                wait(sp, xg_turned, j - 1)
                sp.dma_start(xg[s], xs[part][bass.ds((j - SA * part) * TS, TS), :].rearrange("(h p) d -> p h d", p=P)).then_inc(xg_in[s], 16)

            def load_w1(j, s):
                def load():
                    e = sp.value_load(etab[0:1, bass.ds(j, 1)], min_val=0, max_val=E - 1)
                    wait(sp, relu_done, j - 1)
                    sp.dma_start(w1_sb[s], w1b[bass.ds(e, 1)].rearrange("a p w -> (a p) w")).then_inc(w1_in[s], 16)
                where_taken(sp, j, load, (w1_in[s],), before(j, s, 8), 16)

            def load_w2(j, s):
                def load():
                    e = sp.value_load(etab[0:1, bass.ds(j, 1)], min_val=0, max_val=E - 1)
                    wait(sp, y_done, j - 1)
                    sp.dma_start(w2_sb[s], w2b[bass.ds(e, 1)].rearrange("a p w -> (a p) w")).then_inc(w2_in[s], 16)
                where_taken(sp, j, load, (w2_in[s],), before(j, s, 8), 16)

            def load_tiles(part, i, first=False, flush=False, last=False, store=False):
                for s in range(2):
                    j = 2 * i + s
                    if not (last and s):
                        load_rows(part, j + 1, 1 - s)
                    load_w1(j, s)
                    if not (first and s == 0):
                        load_w2(j - 1, 1 - s)
                if flush or last:
                    load_w2(2 * i + 1, 1)
                if store:
                    store_a(i - SA // 2 - 1)

            def store_a(q):
                sp.wait_ge(a_done, q + 1)
                sp.dma_start(out[bass.ds(q * P, P), :], cy[:]).then_inc(a_out, 16)
            sp.wait_ge(slots_done, 1)
            for j in range(CH):
                sp.wait_ge(scattered[j], 32 * CA)

            def load_round(i):
                for k in range(PER // 2):
                    load_tiles(0, i * (PER // 2) + k, first=(k == 0), flush=(k == PER // 2 - 1))
                for j in range(CH):
                    load_tile(CA + i, j, True)
            load_rows(0, 0, 0)
            chunks(sp, 0, ROUNDS, load_round)
            for j in range(CH):
                load_tile(NC - 1, j, True)
            load_tiles(0, J0 // 2, first=True)
            chunks(sp, J0 // 2 + 1, SA // 2 - 1, lambda i: load_tiles(0, i))
            load_tiles(0, SA // 2 - 1, last=True)
            sp.wait_ge(slots_done, 2)
            for j in range(CH):
                sp.wait_ge(scattered[j], 32 * NC)
            load_rows(1, SA, 0)
            load_tiles(1, SA // 2, first=True)
            chunks(sp, SA // 2 + 1, SA // 2 + CA * CH, lambda i: load_tiles(1, i, store=True))
            for i in range(SA // 2 + CA * CH, NS // 2):
                load_tiles(1, i, last=(i == NS // 2 - 1), store=(i == SA // 2 + CA * CH))
            sp.wait_ge(a_out, 16 * CA * CH)

            def store_out(c):
                for j in range(CH):
                    q = c * CH + j
                    sp.wait_ge(f_done, q + 1 - CA * CH)
                    sp.dma_start(out[bass.ds(q * P, P), :], tile_in[:, j, :]).then_inc(f_out[j], 16)
            chunks(sp, CA, NC, store_out)
            for j in range(CH):
                sp.wait_ge(f_out[j], 16 * (NC - CA))

        @block.gpsimd
        def _(pool):
            pool.memset(ones[:], 1.0).then_inc(pool_consts, 1)
            pool.memset(eps_t[:], EPS).then_inc(pool_consts, 1)
            pool.memset(aggT[:, :, :], 0.0).then_inc(pool_consts, 1)
            pool.memset(bd, 0.0).then_inc(pool_consts, 1)
            pool.memset(zeros[:], 0.0).then_inc(pool_consts, 1)
            pool.iota(iota[:], [[1, GW]], base=0, channel_multiplier=0, allow_small_or_imprecise_dtypes=True).then_inc(pool_consts, 1)
            pool.wait_ge(pool_consts, 1)
            pool.affine_select(out=ident[:], in_=ones[:], compare_op=ALU.is_equal, fill=0.0, base=0,
                               pattern=[[-1, P]], channel_multiplier=1).then_inc(pool_consts, 1)
            pool.affine_select(out=upper[:], in_=ones[:], compare_op=ALU.is_gt, fill=0.0, base=0,
                               pattern=[[1, P]], channel_multiplier=-1).then_inc(pool_consts, 1)
            pool.iota(small[:, 128:129], [[0, 1]], base=0, channel_multiplier=1,
                      allow_small_or_imprecise_dtypes=True).then_inc(pool_consts, 1)

            pool.wait_ge(table_out, 16 * NC)

            pool.wait_ge(flag_ready, 1)
            bad = pool.value_load(flag[0:1, 0:1], min_val=0, max_val=P)
            with pool.If(bad > 0):
                with pool.Fori(0, NG) as g:
                    pool.wait_ge(gen_idx_in, 16 * (g + 1))
                    pool.sem_inc(pool_past)
                    for t in range(GT):
                        pool.indirect_dma_start(
                            out=ring[:, t, :], out_offset=None, in_=table,
                            in_offset=bass.IndirectOffsetOnAxis(ap=idx_gen[:, t:t + 1], axis=0),
                        ).then_inc(gen_gathered[t], 16)
                wait(pool, gen_done, NG * NW)

            def stage_idx(b, half):
                pool.tensor_copy(idx[:, half, :], src_sb[:, bass.ds(b * BT + half * HB, HB)]).then_inc(idx_staged, 1)
            pool.wait_ge(consts_in, N_CONSTS)
            stage_idx(0, 0)

            def gather_block(b, last=False):
                for m in range(BT):
                    half = m // HB
                    carries = False
                    if m % HB == 0:
                        pool.wait_ge(idx_staged, 2 * b + half + 1)
                        carries = True
                    if (m - RING) // GT != (m - 1 - RING) // GT:
                        wait(pool, group_done, b * BG + (m - RING) // GT + 1)
                        carries = True
                    if carries:
                        pool.sem_inc(pool_past)
                    if m % HB == RING and not (last and half):
                        stage_idx(b + half, 1 - half)
                    pool.indirect_dma_start(
                        out=ring[:, m % RING, :], out_offset=None, in_=table,
                        in_offset=bass.IndirectOffsetOnAxis(ap=idx[:, half, m % HB:m % HB + 1], axis=0),
                    ).then_inc(gathered[m % RING], 16)

            def scatter(part, c):
                if isinstance(c, int):
                    pool.wait_ge(slots_done, 1 if c == 0 else 2)
                if not (isinstance(c, int) and c == 0):
                    for j in range(CH):
                        pool.wait_ge(scattered[j], 32 * c)
                pool.sem_inc(pool_past)
                pool.tensor_copy(sidx[:, :, :], slot_i[:, :, bass.ds(c * CH, CH)]).then_inc(sidx_staged, 1)
                for j in range(CH):
                    if j == 0:
                        pool.wait_ge(sidx_staged, c + 1)
                    pool.wait_ge(row_ready, c * CH + j + 1)
                    pool.sem_inc(pool_past)
                    for k in range(2):
                        pool.indirect_dma_start(
                            out=xs[part], out_offset=bass.IndirectOffsetOnAxis(ap=sidx[:, k, j:j + 1], axis=0),
                            in_=ring[:, j, :], in_offset=None).then_inc(scattered[j], 16)
            chunks(pool, 0, B0 + 2, gather_block)
            pool.wait_ge(zero_out, 16 * (2 * NC + 1))
            scatter(0, 0)
            chunks(pool, 1, CA, lambda c: scatter(0, c))
            for j in range(CH):
                pool.wait_ge(scattered[j], 32 * CA)
            chunks(pool, B0 + 2, NB - 1, gather_block)
            gather_block(NB - 1, last=True)
            scatter(1, CA)
            chunks(pool, CA + 1, NC, lambda c: scatter(1, c))

            for s in range(2):
                pool.wait_ge(ys_out[s], 16 * (SA // 2))
            for j in range(CH):
                pool.wait_ge(scattered[j], 32 * NC)

            def pick_a(q):
                if not isinstance(q, int):
                    pool.wait_ge(a_picked, 32 * q)
                    pool.sem_inc(pool_past)
                pool.tensor_copy(sidx[:, :, 0:1], slot_i[:, :, bass.ds(q, 1)]).then_inc(sidx_staged, 1)
                pool.wait_ge(sidx_staged, NC + q + 1)
                wait(pool, a_summed, q)
                pool.sem_inc(pool_past)
                for k in range(2):
                    pool.indirect_dma_start(
                        out=ring[:, k, :], out_offset=None, in_=ys[0],
                        in_offset=bass.IndirectOffsetOnAxis(ap=sidx[:, k, 0:1], axis=0),
                    ).then_inc(a_picked, 16)
            pick_a(0)
            chunks(pool, 1, CA * CH, pick_a)
            pool.wait_ge(a_picked, 32 * CA * CH)
            pool.wait_ge(a_summed, CA * CH)

            for s in range(2):
                pool.wait_ge(ys_out[s], 16 * (NS // 2))

            def pick(c):
                if not isinstance(c, int):
                    for j in range(CH):
                        pool.wait_ge(picked[j], 32 * (c - CA))
                    pool.sem_inc(pool_past)
                pool.tensor_copy(sidx[:, :, :], slot_i[:, :, bass.ds(c * CH, CH)]).then_inc(sidx_staged, 1)
                for j in range(CH):
                    if j == 0:
                        pool.wait_ge(sidx_staged, NC + CA * CH + c - CA + 1)
                    wait(pool, summed, (c - CA) * CH + j - CH + 1)
                    pool.sem_inc(pool_past)
                    for k in range(2):
                        pool.indirect_dma_start(
                            out=ring[:, 2 * j + k, :], out_offset=None, in_=ys[1],
                            in_offset=bass.IndirectOffsetOnAxis(ap=sidx[:, k, j:j + 1], axis=0),
                        ).then_inc(picked[j], 16)
            pick(CA)
            chunks(pool, CA + 1, NC, pick)

        @block.scalar
        def _(act):
            start_counters(act, LEADERS["scalar"])

            act.wait_ge(pool_consts, 9)

            def norm_chunk(c):
                act.wait_ge(stats_done, c + 1)
                act.activation(rstd[:, bass.ds(c * CH, CH)], mv[:, bass.ds(c * CH, CH), 1], ACT.Sqrt,
                               bias=eps_t[:]).then_inc(std_done, 1)
                act.wait_ge(rstd_done, c + 1)
                for j in range(CH):
                    q = c * CH + j
                    act.activation(X2[:, bass.ds(q, 1), :], X2[:, bass.ds(q, 1), :], ACT.Identity,
                                   bias=nmr[:, bass.ds(q, 1)], scale=rstd[:, bass.ds(q, 1)]).then_inc(normed, 1)
            chunks(act, 0, NC, norm_chunk)

            def copy_turned(n, j):
                wait(act, tile_turned, n + 1)
                act.copy(tT[:, j % 2, :], tps).then_inc(turned_copied, 1)

            def kv_root(q, j):
                wait(act, kv_var_done, q + 1)
                act.activation(kv_var[:, j % 2, :], kv_var[:, j % 2, :], ACT.Sqrt, bias=eps_t[:],
                               scale=1.0 / DH).then_inc(kv_std_done, 1)

            def zero_slots(b):
                for rows, zr in zip(xs, ZR):
                    act.dma_start(rows[bass.ds(b * (zr * P), zr * P), :].rearrange("(p a) d -> p a d", p=P),
                                  zeros[:].unsqueeze(1).to_broadcast([P, zr, D])).then_inc(zero_out, 16)
            act.dma_start(ys[1][SB * TS:, :].rearrange("(p a) d -> p a d", p=P),
                          zeros[:].unsqueeze(1).to_broadcast([P, TS // P, D])).then_inc(zero_out, 16)

            def kv_tile(b, j, first):
                q = b * CH + j
                if j == 2:
                    zero_slots(b)
                wait(act, kv_done, q - prior(j) + 1)
                copy_turned(q, j)
                if not (first and j == 0):
                    kv_root(q - 1, (j - 1) % CH)
                wait(act, kv_done, q + 1)
                wait(act, kv_var_done, q)
                act.activation(sq, wide[j % 2], ACT.Square).then_inc(kv_squared, 1)
                wait(act, dots_done, q - prior(j) + 1)
                act.copy(vs[:, j % 2, :], wide[j % 2][:, INNER:]).then_inc(v_copied, 1)

            for j in range(CH):
                kv_tile(0, j, True)
            chunks(act, 1, NC, lambda b: [kv_tile(b, j, False) for j in range(CH)])
            kv_root(NT - 1, CH - 1)

            act.wait_ge(t1_done, 1)
            act.copy(T1, wide[0].rearrange("p (j d) -> p j d", j=NJ)).then_inc(t1_copied, 1)
            act.wait_ge(m_done, 1)
            act.copy(M[:, :, :], wide[1][:, 0:KD * D].rearrange("p (k d) -> p k d", k=KD)).then_inc(m_copied, 1)

            def layers(c1, c2):
                def normed_row(j):
                    q = c2 * CH + j
                    wait(act, y_turned, q - prior(j) + 1)
                    act.activation(yt[:, j % 2, :], X2[:, bass.ds(q, 1), :], ACT.Identity,
                                   bias=nmr[:, bass.ds(q, 1)], scale=rstd[:, bass.ds(q, 1)]).then_inc(y_normed, 1)

                if c2 is not None:
                    act.wait_ge(y_rstd, c2 + 1)
                    normed_row(0)
                for j in range(CH):
                    if c1 is not None:
                        q = c1 * CH + j
                        wait(act, layers_done, q - prior(j) + 1)
                        act.copy(aT[:, j % 2, :].rearrange("p (k n) -> p k n", k=KD),
                                 aggT[:, :, bass.ds(q * P, P)]).then_inc(agg_staged, 1)
                        copy_turned(NT + q, j)
                    if c2 is not None and j + 1 < CH:
                        normed_row(j + 1)
                if c1 is not None:
                    cols = bass.ds(c1 * CH, CH)
                    act.wait_ge(y_stats, c1 + 1)
                    act.activation(rstd[:, cols], mv[:, cols, 1], ACT.Sqrt, bias=eps_t[:]).then_inc(y_std, 1)

            def row(out_ap, q):
                return act.activation(out_ap, X2[:, bass.ds(q, 1), :], ACT.Identity,
                                      bias=nmr[:, bass.ds(q, 1)], scale=rstd[:, bass.ds(q, 1)])

            def exp_part(part, c0, c1):
                act.wait_ge(exp_in, part + 1)
                p1 = prob[:, 1, c0 * CH:c1 * CH]
                act.activation(p1, p1, ACT.Exp).then_inc(exp_done, 1)

            def row_for_scatter(c, j):
                if not isinstance(c, int) or c > 0:
                    act.wait_ge(scattered[j], 32 * c)
                row(ring[:, j, :], c * CH + j).then_inc(row_ready, 1)

            def rows_chunk(c):
                for j in range(CH):
                    if isinstance(c, int):
                        wait(act, group_done, BG * (B0 + 2 if c == 0 else NB))
                    row_for_scatter(c, j)

            def xg_copy(j, s):
                wait(act, xg_turned, j + 1)
                act.copy(xgT[s], xgps.rearrange("p (k t) -> p k t", k=KD)).then_inc(xg_copied, 1)

            def store_y(j, s, part=1):
                wait(act, y_done, j + 1)
                act.dma_start(ys[part][bass.ds((j - SA * part) * TS, TS), :].rearrange("(h p) d -> p h d", p=P), yo[s]).then_inc(ys_out[s], 16)

            def moe_tile(j, s, first=False, last=False, part=1):
                def relu():
                    wait(act, l1_done, j + 1)
                    wait(act, l2_done, j - 1)
                    for f in range(FC):
                        r = act.activation(hT[s][:, f, :], wide[s][:, f * TS:(f + 1) * TS], ACT.Relu,
                                           bias=w1_sb[s][:, KD * F + f:KD * F + f + 1])
                    r.then_inc(relu_done, 1)
                if not last:
                    xg_copy(j + 1, 1 - s)
                where_taken(act, j, relu, (relu_done,), lambda _: j)
                if not first:
                    store_y(j - 1, 1 - s, part)

            layers(0, None)
            chunks(act, 1, CA, lambda c: layers(c, c - 1))
            layers(None, CA - 1)
            exp_part(0, 0, CA)
            rows_chunk(0)
            chunks(act, 1, CA, rows_chunk)

            def one_round(i, c2):
                xg_copy(PER * i, 0)
                for k in range(PER):
                    moe_tile(PER * i + k, k % 2, first=(k == 0), last=(k == PER - 1), part=0)
                store_y(PER * i + PER - 1, 1, part=0)
                layers(CA + i, c2)
            act.wait_ge(slots_done, 1)
            one_round(0, None)
            chunks(act, 1, ROUNDS, lambda i: one_round(i, CA + i - 1))
            layers(NC - 1, NC - 2)
            layers(None, NC - 1)
            xg_copy(J0, 0)
            exp_part(1, CA, NC)
            rows_chunk(CA)
            for j in range(J0, SA):
                moe_tile(j, j % 2, first=(j == J0), last=(j == SA - 1), part=0)
                n = 7 * (j - J0 - 5) // 2
                for i in range(max(n, 0), max(n + 4 - (j - J0) % 2, 0)):
                    if i < CH * (NC - CA - 1):
                        row_for_scatter(CA + 1 + i // CH, i % CH)
            store_y(SA - 1, 1, part=0)
            act.wait_ge(slots_done, 2)
            xg_copy(SA, 0)

            def again_a(q):
                row(ay[:], q).then_inc(a_again, 1)

            def finish_a(q):
                act.wait_ge(a_stats, q + 1)
                act.activation(small[:, 48:49], mvc[:, 0, 1:2], ACT.Sqrt, bias=eps_t[:]).then_inc(a_std, 1)
                if not isinstance(q, int):
                    act.wait_ge(a_out, 16 * q)
                act.wait_ge(a_rstd, q + 1)
                act.activation(cy[:], ay[:], ACT.Identity, bias=small[:, 50:51], scale=small[:, 49:50]).then_inc(a_normed, 1)

            def moe_a(i, first=False):
                q = i - SA // 2
                moe_tile(2 * i, 0, first=first)
                again_a(q)
                moe_tile(2 * i + 1, 1)
                finish_a(q)
            moe_a(SA // 2, first=True)
            chunks(act, SA // 2 + 1, SA // 2 + CA * CH, moe_a)
            for j in range(SA + 2 * CA * CH, NS):
                moe_tile(j, j % 2, last=(j == NS - 1))
            store_y(NS - 1, 1)

            def out_chunk(c):
                for j in range(CH):
                    if isinstance(c, int):
                        act.wait_ge(scattered[j], 32 * NC)
                    else:
                        act.wait_ge(f_out[j], 16 * (c - CA))
                    row(tile_in[:, j, :], c * CH + j).then_inc(y_again, 1)
                act.wait_ge(f_stats, c - CA + 1)
                act.activation(small[:, 8:8 + CH], small[:, 16:16 + CH], ACT.Sqrt, bias=eps_t[:]).then_inc(f_std, 1)
                act.wait_ge(f_rstd, c - CA + 1)
                for j in range(CH):
                    act.activation(tile_in[:, j, :], tile_in[:, j, :], ACT.Identity,
                                   bias=small[:, 32 + j:33 + j], scale=small[:, 24 + j:25 + j]).then_inc(f_normed, 1)
            out_chunk(CA)
            chunks(act, CA + 1, NC, out_chunk)

        @block.vector
        def _(dve):
            start_counters(dve, LEADERS["vector"])

            def stats_chunk(c):
                for j in range(CH):
                    dve.wait_ge(x_in[j], 16 * (c + 1))
                    dve.sem_inc(dve_past)
                    dve.bn_stats(bn[:, j, :], X2[:, bass.ds(c * CH + j, 1), :].rearrange("p a d -> p (a d)"))
                dve.drain()
                for j in range(CH):
                    dve.bn_aggr(mvc[:, j, :], bn[:, j, :])
                dve.drain()
                dve.tensor_copy(mv[:, bass.ds(c * CH, CH), :], mvc[:, :, :]).then_inc(stats_done, 1)
                dve.wait_ge(std_done, c + 1)
                cols = bass.ds(c * CH, CH)
                dve.reciprocal(rstd[:, cols], rstd[:, cols])
                dve.drain()
                dve.scalar_tensor_tensor(out=nmr[:, cols], in0=mv[:, cols, 0], scalar=-1.0, in1=rstd[:, cols],
                                         op0=ALU.mult, op1=ALU.mult).then_inc(rstd_done, 1)
            chunks(dve, 0, NC, stats_chunk)

            dve.wait_ge(consts_in, N_CONSTS)
            dve.wait_ge(pool_consts, 9)
            dve.tensor_copy(base_f[:], base_i[:])
            dve.tensor_copy(dstrel[:, :], dstrel[:, :].bitcast(I32))
            dve.drain()
            dve.tensor_scalar(base_f[:], base_f[:], float(NP - W), None, ALU.min)
            for n, (b, c) in enumerate(STARTS):
                dve.tensor_reduce(small[:, 140 + n:141 + n], dstrel[:, b * BT:], AX.X, ALU.min)
            dve.drain()
            for n, (b, c) in enumerate(STARTS):
                dve.tensor_scalar(base_f[:, b * BG:], base_f[:, b * BG:], float(c * CH * P), None, ALU.max)
                dve.tensor_scalar(small[:, 150 + n:151 + n], small[:, 140 + n:141 + n], float(c * CH * P), None, ALU.is_lt)
                dve.drain()
            dve.tensor_reduce(small[:, 6:7], small[:, 150:150 + len(STARTS)], AX.X, ALU.max)
            dve.drain()
            dve.tensor_copy(base_i[:], base_f[:])
            d3 = dstrel[:, :].rearrange("p (g t) -> p g t", t=GT)
            dve.tensor_tensor(d3, d3, base_f[:, :].unsqueeze(2).to_broadcast([P, NG, GT]), ALU.subtract)
            dve.drain()
            dve.tensor_reduce(small[:, 0:1], dstrel[:, :], AX.X, ALU.max)
            dve.tensor_reduce(small[:, 1:2], dstrel[:, :], AX.X, ALU.min)
            dve.drain()
            dve.tensor_scalar(small[:, 2:3], small[:, 0:1], float(W), None, ALU.is_ge)
            dve.tensor_scalar(small[:, 3:4], small[:, 1:2], 0.0, None, ALU.is_lt)
            dve.drain()
            dve.tensor_tensor(small[:, 4:5], small[:, 2:3], small[:, 3:4], ALU.max)
            dve.drain()
            dve.tensor_tensor(small[:, 4:5], small[:, 4:5], small[:, 6:7], ALU.max).then_inc(bad_found, 1)
            dve.wait_ge(bad_counted, 1)
            dve.tensor_copy(flag[:, :], ps[0:1, 3, 0:1]).then_inc(flag_ready, 1)
            dve.tensor_scalar(small[:, 7:8], ps[:, 3, 0:1], 0.0, None, ALU.is_equal)
            w3 = wkv_sb.rearrange("p k (h d) -> p (k h) d", d=DH)
            m3 = sq[:, 0:KD * 2 * HEADS]
            dve.tensor_reduce(m3, w3, AX.X, ALU.add)
            dve.drain()
            dve.tensor_scalar(m3, m3, 1.0 / DH, None, ALU.mult)
            dve.drain()
            dve.tensor_tensor(w3, w3, m3.unsqueeze(2).to_broadcast([P, KD * 2 * HEADS, DH]), ALU.subtract)
            dve.drain().then_inc(dve_consts, 1)

            dve.wait_ge(flag_ready, 1)
            bad = dve.value_load(flag[0:1, 0:1], min_val=0, max_val=P)
            with dve.If(bad > 0):
                dve.wait_ge(table_out, 16 * NC)
                dve.memset(aggT[:, :, :], 0.0)
                dve.drain()
                with dve.Fori(0, NG) as g:
                    dve.tensor_tensor(dst_gen, dstrel[:, bass.ds(g * GT, GT)],
                                      base_f[:, bass.ds(g, 1)].to_broadcast([P, GT]), ALU.add)
                    dve.drain()
                    with dve.Fori(0, NW) as v:
                        wait(dve, gen_done, g * NW + v)
                        for t in range(GT):
                            dve.tensor_scalar(Sgen[:, t, :], iota[:, :], dst_gen[:, t:t + 1],
                                              ew[:, bass.ds(g * GT + t, 1)], ALU.is_equal, ALU.mult)
                        dve.drain().then_inc(gen_selected, 1)
                        dve.tensor_scalar(dst_gen, dst_gen, float(-GW), None, ALU.add)
                        wait(dve, gen_done, g * NW + v + 1)
                        win = aggT[:, :, bass.ds(v * GW, GW)]
                        dve.tensor_tensor(win, win, ps[:, 4:4 + KD, 0:GW], ALU.add)
                        dve.drain().then_inc(gen_added, 1)
            dve.tensor_scalar(ew[:, :], ew[:, :], small[:, 7:8], None, ALU.mult)
            dve.drain()

            def select(h, g):
                wait(dve, group_done, h * HG + g - 2)
                for t in range(GT):
                    m = g * GT + t
                    ins = dve.tensor_scalar(S[:, m % RING, :], iota[:, 0:W], dstrel[:, bass.ds(h * HB + m, 1)],
                                            ew[:, bass.ds(h * HB + m, 1)], ALU.is_equal, ALU.mult)
                ins.then_inc(selected, 1)

            def add_group(h, g, n):
                G = h * HG + g
                start = dve.value_load(base_i[0:1, bass.ds(G, 1)], min_val=0, max_val=NP - W)
                wait(dve, group_done, G + 1)
                wait(dve, group_added, G)
                win = aggT[:, :, bass.ds(start, W)]
                dve.tensor_tensor(win, win, aggps[g % n % 2].rearrange("p (k n) -> p k n", k=KD),
                                  ALU.add).then_inc(group_added, 1)

            def kv_stats(q, j):
                wait(dve, kv_squared, q + 1)
                dve.tensor_reduce(kv_var[:, j % 2, :], sq.rearrange("p (h d) -> p h d", d=DH), AX.X,
                                  ALU.add).then_inc(kv_var_done, 1)

            def kv_recip(q, j):
                dve.wait_ge(kv_std_done, q + 1)
                dve.reciprocal(kv_r[:, :], kv_var[:, j % 2, :]).then_inc(kv_r_done, 1)
                dve.wait_ge(kv_r_done, 2 * q + 1)
                dve.tensor_tensor(kv_s[:, j % 2, :], kv_r[:, 0:HEADS], kv_r[:, HEADS:], ALU.mult).then_inc(kv_r_done, 1)
                dve.wait_ge(kv_r_done, 2 * q + 2)
                wait(dve, dots_done, q - prior(j) + 1)
                dve.tensor_tensor(ks[:, j % 2, :].rearrange("p (h d) -> p h d", d=DH),
                                  wide[j % 2][:, 0:INNER].rearrange("p (h d) -> p h d", d=DH),
                                  kv_s[:, j % 2, :].unsqueeze(2).to_broadcast([P, HEADS, DH]),
                                  ALU.mult).then_inc(k_scaled, 1)

            def kv_step(b, j, first):
                q = b * CH + j
                head = first and j == 0
                if not head:
                    add_group(2 * b, 2 * j - 1, BG)
                select(2 * b, 2 * j + 1)
                if not head:
                    kv_stats(q - 1, (j - 1) % CH)
                add_group(2 * b, 2 * j, BG)
                select(2 * b, 2 * j + 2)
                if not head:
                    kv_recip(q - 1, (j - 1) % CH)
            select(0, 0)
            for j in range(CH):
                kv_step(0, j, True)
            chunks(dve, 1, NC, lambda b: [kv_step(b, j, False) for j in range(CH)])
            kv_stats(NT - 1, CH - 1)
            kv_recip(NT - 1, CH - 1)

            wait(dve, dots_done, NT)
            for a in range(2):
                half = slice(a * DH, (a + 1) * DH)
                dve.tensor_scalar(bd[half, :, half], dotps[half, :, half], 1.0 / N, None, ALU.mult).then_inc(bd_done, 1)

            add_group(2 * B0, -1, BG)

            def layers(c1, c2, h=None, n=HG, selected_first=False):
                def group(g):
                    if g + 1 < n:
                        select(h, g + 1)
                    add_group(h, g, n)

                def logit(j):
                    wait(dve, gate_done, c2 * CH + j + 1)
                    dve.tensor_tensor(logits[:, j, :], wide[j % 2][:, 512:512 + E], gb_b[:], ALU.add).then_inc(logit_done, 1)

                if h is not None and not selected_first:
                    select(h, 0)
                for j in range(CH + 2):
                    if c1 is not None and j < CH:
                        dve.wait_ge(x_again[j], 16 * (c1 + 1))
                        row = X2[:, bass.ds(c1 * CH + j, 1), :].rearrange("p a d -> p (a d)")
                        dve.tensor_tensor(row, row, bout_b[:], ALU.add).then_inc(x_biased, 1)
                    if h is not None and j < CH:
                        for g in range(j * n // CH, (j + 1) * n // CH):
                            group(g)
                    if c2 is not None and j < CH:
                        wait(dve, y_turned, c2 * CH + j + 1)
                        wait(dve, gate_done, c2 * CH + j - prior(j) + 1)
                        dve.tensor_copy(yT[:, j % 2, :], yps).then_inc(y_copied, 1)
                    if c1 is not None:
                        q = c1 * CH + j
                        if 1 <= j <= CH:
                            row = X2[:, bass.ds(q - 1, 1), :].rearrange("p a d -> p (a d)")
                            dve.wait_ge(x_biased, q)
                            wait(dve, layers_done, q)
                            dve.tensor_tensor(row, row, wide[(j - 1) % 2][:, 0:D], ALU.add).then_inc(x2_done, 1)
                        if j >= 2:
                            wait(dve, x2_done, q - 1)
                            dve.sem_inc(dve_past)
                            dve.bn_stats(bn[:, j - 2, :], X2[:, bass.ds(q - 2, 1), :].rearrange("p a d -> p (a d)"))
                    if c2 is not None and 1 <= j <= CH:
                        logit(j - 1)
                dve.drain()
                if c1 is not None:
                    for j in range(CH):
                        dve.bn_aggr(mvc[:, j, :], bn[:, j, :])
                    dve.drain()
                    dve.tensor_copy(mv[:, bass.ds(c1 * CH, CH), :], mvc[:, :, :]).then_inc(y_stats, 1)
                if c2 is not None:
                    for j in range(CH):
                        dve.max(out=top8[:, j, :], in_=logits[:, j, :])
                    dve.drain()
                    for j in range(CH):
                        dve.max_index(out=top8_i[:, j, :], in_max=top8[:, j, :], in_values=logits[:, j, :])
                    dve.drain()
                    cols = bass.ds(c2 * CH, CH)
                    dve.tensor_copy(top[:, :, cols], top8[:, :, 0:2].rearrange("p j k -> p k j"))
                    dve.tensor_copy(slot_f[:, :, cols], top8_i[:, :, 0:2].rearrange("p j k -> p k j"))
                    dve.drain()
                if c1 is not None:
                    cols = bass.ds(c1 * CH, CH)
                    dve.wait_ge(y_std, c1 + 1)
                    dve.reciprocal(rstd[:, cols], rstd[:, cols])
                    dve.drain()
                    dve.scalar_tensor_tensor(out=nmr[:, cols], in0=mv[:, cols, 0], scalar=-1.0, in1=rstd[:, cols],
                                             op0=ALU.mult, op1=ALU.mult).then_inc(y_rstd, 1)

            def route(part, c0, c1, tile0, n_tiles, bank, beside):
                nt = (c1 - c0) * CH
                cols = slice(c0 * CH, c1 * CH)
                h1, h2, hs, ps_, tt, sc, ie = [t[:, 0:E * nt].rearrange("p (e i) -> p e i", e=E)
                                               for t in (H1, H2, Hs, pos, tot, scan, iota_e)]
                ends_here = c1 == NC
                dve.tensor_tensor(prob[:, 1, cols], top[:, 1, cols], top[:, 0, cols], ALU.subtract)
                dve.drain().then_inc(exp_in, 1)
                for e in range(E):
                    dve.memset(ie[:, e, :], float(e))
                pidx, pad, dummy = small[:, 128:129], small[:, 129:130], small[:, 130:131]
                dve.tensor_scalar(pad, pidx, float(P - PADDED), None, ALU.is_ge)
                dve.tensor_scalar(dummy, pidx, 2.0, float(SB * TS), ALU.mult, ALU.add)
                dve.drain()
                for k, H in enumerate((h1, h2)):
                    dve.tensor_tensor(H, ie, slot_f[:, k, cols].unsqueeze(1).to_broadcast([P, E, nt]), ALU.is_equal)
                dve.tensor_scalar(small[:, 131:132], pad, -1.0, 1.0, ALU.mult, ALU.add)
                dve.drain()
                if ends_here:
                    for H in (h1, h2):
                        dve.tensor_scalar(H[:, :, nt - 1], H[:, :, nt - 1], small[:, 131:132], None, ALU.mult)
                    dve.drain()
                dve.tensor_tensor(hs, h1, h2, ALU.add).then_inc(hot_done, 1)
                dve.wait_ge(ranked, part + 1)
                dve.tensor_copy(tot[:, 0:E * nt], ps[:, bank + 1, 0:E * nt])
                dve.drain()
                dve.tensor_tensor_scan(scan[:, 0:E * nt], tot[:, 0:E * nt], tot[:, 0:E * nt], 0.0, ALU.add, ALU.max)
                dve.drain()
                beside(0)
                ends = sc[:, :, nt - 1]
                cnt, pads, aend, adj = (small[:, 16 * i:16 * i + 16] for i in range(2, 6))
                dve.tensor_copy(cnt, ends)
                dve.drain()
                dve.tensor_tensor(cnt[:, 1:E], ends[:, 1:E], ends[:, 0:E - 1], ALU.subtract)
                dve.drain()
                beside(1)
                cnt_i = small[:, 96:112].bitcast(I32)
                dve.tensor_scalar(cnt_i, cnt, float(TS - 1), None, ALU.add)
                dve.drain()
                dve.tensor_scalar(cnt_i, cnt_i, TS.bit_length() - 1, None, ALU.arith_shift_right)
                dve.drain()
                dve.tensor_copy(pads, cnt_i)
                dve.drain()
                dve.tensor_tensor_scan(aend, pads, pads, 0.0, ALU.add, ALU.max)
                dve.drain()
                beside(2)
                dve.tensor_tensor(adj, aend, pads, ALU.subtract)
                dve.tensor_tensor(cnt, ends, cnt, ALU.subtract)
                dve.drain()
                dve.tensor_scalar(adj, adj, float(TS), None, ALU.mult)
                dve.tensor_tensor(sc, sc, tt, ALU.subtract)
                dve.drain()
                beside(3)
                dve.tensor_tensor(adj, adj, cnt, ALU.subtract)
                dve.drain()
                dve.tensor_tensor(ps_, sc, adj.unsqueeze(2).to_broadcast([P, E, nt]), ALU.add)
                dve.drain()
                dve.tensor_tensor(pos[:, 0:E * nt], pos[:, 0:E * nt], ps[:, bank, 0:E * nt], ALU.add)
                dve.drain()
                beside(4)
                for H in (h1, h2):
                    dve.tensor_tensor(H, H, ps_, ALU.mult)
                dve.drain()
                beside(5)
                for k, H in enumerate((h1, h2)):
                    dve.tensor_reduce(slot_f[:, k, cols], H.rearrange("p e i -> p i e"), AX.X, ALU.add)
                dve.drain()
                if ends_here:
                    for k in range(2):
                        dve.tensor_scalar(small[:, 132 + k:133 + k], dummy, float(k), None, ALU.add)
                    dve.drain()
                    for k in range(2):
                        dve.tensor_tensor(small[:, 134 + k:135 + k], small[:, 132 + k:133 + k], pad, ALU.mult)
                    dve.drain()
                    for k in range(2):
                        dve.tensor_tensor(slot_f[:, k, NT - 1:NT], slot_f[:, k, NT - 1:NT], small[:, 134 + k:135 + k], ALU.add)
                    dve.drain()
                dve.tensor_copy(slot_i[:, :, cols], slot_f[:, :, cols])
                jj = small[0:1, 136:137]
                cmp = cmp_t[0:1, 0:n_tiles, :]
                dve.tensor_tensor(cmp, iota[0:1, 0:n_tiles].unsqueeze(2).to_broadcast([1, n_tiles, E]),
                                  aend[0:1].unsqueeze(1).to_broadcast([1, n_tiles, E]), ALU.is_ge)
                dve.drain()
                row = tot[0:1, 0:n_tiles]
                dve.tensor_reduce(row, cmp, AX.X, ALU.add)
                dve.drain()
                dve.tensor_scalar(etab[:, tile0:tile0 + n_tiles], row, float(E - 1), None, ALU.min)
                dve.tensor_scalar(taken[:, tile0:tile0 + n_tiles], row, float(E), None, ALU.is_lt)
                beside(6)
                dve.wait_ge(exp_done, part + 1)
                dve.tensor_scalar(prob[:, 0, cols], prob[:, 1, cols], 1.0, None, ALU.add)
                dve.drain()
                dve.reciprocal(prob[:, 0, cols], prob[:, 0, cols])
                dve.drain()
                dve.tensor_tensor(prob[:, 1, cols], prob[:, 1, cols], prob[:, 0, cols], ALU.mult)
                dve.drain().then_inc(slots_done, 1)

            def moe_y(j, s):
                wait(dve, l2_done, j + 1)
                dve.wait_ge(w2_in[s], 8 * (j + 2 - s))
                if not (isinstance(j, int) and j < 2):
                    dve.wait_ge(ys_out[s], 8 * (j - s))
                dve.tensor_tensor(yo[s], outps.rearrange("p (h d) -> p h d", h=2),
                                  w2_sb[s][:, W2ROW:].unsqueeze(1).to_broadcast([P, 2, D]), ALU.add).then_inc(y_done, 1)

            layers(0, None, 2 * B0, selected_first=True)
            chunks(dve, 1, CA, lambda c: layers(c, c - 1, 2 * B0 + c))
            layers(None, CA - 1)
            def edges_beside(g):
                select(2 * B0 + CA, g)
                if g:
                    add_group(2 * B0 + CA, g - 1, HG)
            route(0, 0, CA, 0, SA, 4, edges_beside)
            add_group(2 * B0 + CA, HG - 1, HG)

            def one_round(i, c2):
                h = 2 * B0 + CA + 1 + 4 * i
                for k in range(PER):
                    for g in range(*SHARE[k]):
                        select(h, g)
                        if g:
                            add_group(h, g - 1, BG)
                    if k:
                        moe_y(PER * i + k - 1, (k - 1) % 2)
                add_group(h, BG - 1, BG)
                moe_y(PER * i + PER - 1, 1)
                layers(CA + i, c2, h + 2, BG)
            one_round(0, None)
            chunks(dve, 1, ROUNDS, lambda i: one_round(i, CA + i - 1))
            layers(NC - 1, NC - 2)
            layers(None, NC - 1)
            LATE_Y = {1: J0, 4: J0 + 1, 6: J0 + 2}

            def experts_beside(n):
                if n in LATE_Y:
                    moe_y(LATE_Y[n], LATE_Y[n] % 2)
            route(1, CA, NC, SA, SB, 0, experts_beside)
            for j in range(J0 + len(LATE_Y), SA):
                moe_y(j, j % 2)

            def finish_a(q, part):
                row = X2[:, bass.ds(q, 1), :].rearrange("p a d -> p (a d)")
                if part == 0:
                    dve.wait_ge(a_picked, 32 * (q + 1))
                    dve.wait_ge(a_again, q + 1)
                    for k in range(2):
                        dve.scalar_tensor_tensor(out=ay[:], in0=ring[:, k, :], scalar=prob[:, k, bass.ds(q, 1)],
                                                 in1=ay[:], op0=ALU.mult, op1=ALU.add)
                        dve.drain()
                    dve.sem_inc(a_summed)
                    dve.bn_stats(bn[:, 0, :], ay[:])
                    dve.tensor_tensor(row, row, beta_b[:], ALU.add)
                    dve.drain()
                    dve.bn_aggr(mvc[:, 0, :], bn[:, 0, :])
                    dve.drain().then_inc(a_stats, 1)
                else:
                    dve.wait_ge(a_std, q + 1)
                    dve.reciprocal(small[:, 49:50], small[:, 48:49])
                    dve.drain()
                    dve.scalar_tensor_tensor(out=small[:, 50:51], in0=mvc[:, 0, 0:1], scalar=-1.0,
                                             in1=small[:, 49:50], op0=ALU.mult, op1=ALU.mult).then_inc(a_rstd, 1)
                    dve.wait_ge(a_normed, q + 1)
                    dve.tensor_tensor(cy[:], cy[:], gamma_b[:], ALU.mult)
                    dve.drain()
                    dve.tensor_tensor(cy[:], cy[:], row, ALU.add).then_inc(a_done, 1)

            def moe_a(i, first=False):
                q = i - SA // 2
                if not first:
                    moe_y(2 * i - 1, 1)
                finish_a(q, 0)
                moe_y(2 * i, 0)
                finish_a(q, 1)
            moe_a(SA // 2, first=True)
            chunks(dve, SA // 2 + 1, SA // 2 + CA * CH, moe_a)
            for j in range(SA + 2 * CA * CH - 1, NS):
                moe_y(j, j % 2)

            def out_chunk(c):
                def weigh(j, k):
                    q = c * CH + j
                    if k == 0:
                        dve.wait_ge(picked[j], 32 * (c - CA + 1))
                        dve.wait_ge(y_again, q + 1 - CA * CH)
                    else:
                        wait(dve, half_summed, q + 1 - CA * CH)
                    dve.scalar_tensor_tensor(out=tile_in[:, j, :], in0=ring[:, 2 * j + k, :],
                                             scalar=prob[:, k, bass.ds(q, 1)], in1=tile_in[:, j, :],
                                             op0=ALU.mult, op1=ALU.add).then_inc((half_summed, summed)[k], 1)
                for j in range(CH + 1):
                    if j < CH:
                        weigh(j, 0)
                    if j:
                        weigh(j - 1, 1)
                dve.drain()
                for j in range(CH):
                    dve.bn_stats(bn[:, j, :], tile_in[:, j, :])
                dve.drain()
                for j in range(CH):
                    dve.bn_aggr(mvc[:, j, :], bn[:, j, :])
                dve.drain()
                dve.tensor_copy(small[:, 16:16 + CH], mvc[:, :, 1])
                dve.drain().then_inc(f_stats, 1)
                dve.wait_ge(f_std, c - CA + 1)
                dve.reciprocal(small[:, 24:24 + CH], small[:, 8:8 + CH])
                dve.drain()
                dve.scalar_tensor_tensor(out=small[:, 32:32 + CH], in0=mvc[:, :, 0], scalar=-1.0,
                                         in1=small[:, 24:24 + CH], op0=ALU.mult, op1=ALU.mult).then_inc(f_rstd, 1)
                for j in range(CH):
                    row = X2[:, bass.ds(c * CH + j, 1), :].rearrange("p a d -> p (a d)")
                    dve.tensor_tensor(row, row, beta_b[:], ALU.add)
                for j in range(CH):
                    dve.wait_ge(f_normed, (c - CA) * CH + j + 1)
                    dve.tensor_tensor(tile_in[:, j, :], tile_in[:, j, :], gamma_b[:], ALU.mult)
                dve.drain()
                for j in range(CH):
                    row = X2[:, bass.ds(c * CH + j, 1), :].rearrange("p a d -> p (a d)")
                    dve.tensor_tensor(tile_in[:, j, :], tile_in[:, j, :], row, ALU.add).then_inc(f_done, 1)
            chunks(dve, CA, NC, out_chunk)

        @block.tensor
        def _(pe):
            start_counters(pe, LEADERS["tensor"])

            def edge_group(h, g):
                G = h * HG + g
                pe.wait_ge(selected, G + 1)
                wait(pe, group_added, G if g == 0 else G - 1)
                for t in range(GT):
                    m = g * GT + t
                    pe.wait_ge(gathered[m % RING], 16 * (h * (HB // RING) + m // RING + 1))
                    for f in range(KD):
                        mm = pe.matmul(aggps[g % 2][:, f * W:(f + 1) * W], ring[:, m % RING, f * P:(f + 1) * P],
                                       S[:, m % RING, :], start=(t == 0 and f == 0), stop=(t == GT - 1),
                                       skip_group_check=True)
                mm.then_inc(group_done, 1)

            def turn(n, c, j, passes):
                pe.wait_ge(tile_loaded[j], 16 * (c + 1 + passes * NC))
                wait(pe, turned_copied, n)
                for k in range(KD):
                    mm = pe.transpose(tps[:, k * P:(k + 1) * P], tile_in[:, j, k * P:(k + 1) * P], ident[:])
                mm.then_inc(tile_turned, 1)

            def kv_mm(q, j):
                wait(pe, turned_copied, q + 1)
                wait(pe, k_scaled, q - prior(j) + 1)
                wait(pe, v_copied, q - prior(j) + 1)
                for h in range(2):
                    for k in range(KD):
                        mm = pe.matmul(wide[j % 2][:, h * 512:(h + 1) * 512], tT[:, j % 2, k * P:(k + 1) * P],
                                       wkv_sb[:, k, h * 512:(h + 1) * 512], start=(k == 0), stop=(k == KD - 1))
                mm.then_inc(kv_done, 1)

            def dots(q, j, first):
                wait(pe, k_scaled, q + 1)
                wait(pe, v_copied, q + 1)
                for a in range(NJ):
                    mm = pe.matmul(dotps[:, a, :], vs[:, j % 2, a * P:(a + 1) * P], ks[:, j % 2, a * P:(a + 1) * P],
                                   start=(first and a == 0), stop=False, skip_group_check=True)
                mm.then_inc(dots_done, 1)

            def kv_step(b, j, first):
                q = b * CH + j
                edge_group(2 * b, 2 * j)
                turn(q, b, j, 0)
                edge_group(2 * b, 2 * j + 1)
                kv_mm(q, j)
                if not (first and j == 0):
                    dots(q - 1, (j - 1) % CH, first and j == 1)

            pe.wait_ge(pool_consts, 9)
            pe.wait_ge(bad_found, 1)
            pe.matmul(ps[:, 3, 0:1], ones[:], small[:, 4:5], start=True, stop=True).then_inc(bad_counted, 1)
            pe.wait_ge(dve_consts, 1)
            pe.wait_ge(flag_ready, 1)
            bad = pe.value_load(flag[0:1, 0:1], min_val=0, max_val=P)
            with pe.If(bad > 0):
                with pe.Fori(0, NG) as g:
                    with pe.Fori(0, NW) as v:
                        for t in range(GT):
                            pe.wait_ge(gen_gathered[t], 16 * (g + 1))
                        pe.wait_ge(gen_selected, g * NW + v + 1)
                        wait(pe, gen_added, g * NW + v)
                        for t in range(GT):
                            for f in range(KD):
                                mm = pe.matmul(ps[:, 4 + f, 0:GW], ring[:, t, f * P:(f + 1) * P], Sgen[:, t, :],
                                               start=(t == 0), stop=(t == GT - 1), skip_group_check=True)
                        mm.then_inc(gen_done, 1)
                wait(pe, gen_added, NG * NW)
            for j in range(CH):
                kv_step(0, j, True)
            chunks(pe, 1, NC, lambda b: [kv_step(b, j, False) for j in range(CH)])
            dots(NT - 1, CH - 1, False)

            pe.wait_ge(bd_done, 2)
            for a in range(NJ):
                mm = pe.matmul(wide[0][:, a * D:(a + 1) * D], bd[:, a, :], wout_sb[:, a, :], start=True, stop=True)
            mm.then_inc(t1_done, 1)
            pe.wait_ge(t1_copied, 1)
            for k in range(KD):
                for a in range(NJ):
                    mm = pe.matmul(wide[1][:, k * D:(k + 1) * D], wq_sb[:, a, k * P:(k + 1) * P], T1[:, a, :],
                                   start=(a == 0), stop=(a == NJ - 1))
            mm.then_inc(m_done, 1)
            pe.wait_ge(m_copied, 1)

            def layers(c1, c2, h=None, n=HG):
                def mix_gnn(j):
                    q = c1 * CH + j
                    wait(pe, turned_copied, NT + q + 1)
                    pe.wait_ge(agg_staged, q + 1)
                    wait(pe, x2_done, q - prior(j) + 1)
                    for m, (lhs, rhs) in enumerate(((tT, M), (aT, gnn_sb))):
                        for k in range(KD):
                            mm = pe.matmul(wide[j % 2][:, 0:D], lhs[:, j % 2, k * P:(k + 1) * P], rhs[:, k, :],
                                           start=(m == 0 and k == 0), stop=(m == 1 and k == KD - 1))
                    mm.then_inc(layers_done, 1)

                def gate(j):
                    q = c2 * CH + j
                    wait(pe, y_copied, q + 1)
                    wait(pe, logit_done, q - prior(j) + 1)
                    for k in range(KD):
                        mm = pe.matmul(wide[j % 2][:, 512:512 + 96], yT[:, j % 2, k * P:(k + 1) * P], gate_sb[:, k, :],
                                       start=(k == 0), stop=(k == KD - 1))
                    mm.then_inc(gate_done, 1)

                for j in range(CH + 1):
                    if j < CH:
                        if h is not None:
                            for g in range(j * n // CH, (j + 1) * n // CH):
                                edge_group(h, g)
                        if c1 is not None:
                            turn(NT + c1 * CH + j, c1, j, 1)
                        if c2 is not None:
                            q = c2 * CH + j
                            pe.wait_ge(y_normed, q + 1)
                            wait(pe, y_copied, q)
                            for k in range(KD):
                                mm = pe.transpose(yps[:, k * P:(k + 1) * P], yt[:, j % 2, k * P:(k + 1) * P], ident[:])
                            mm.then_inc(y_turned, 1)
                    if j:
                        if c1 is not None:
                            mix_gnn(j - 1)
                        if c2 is not None:
                            gate(j - 1)

            def rank(part, nt, bank):
                pe.wait_ge(hot_done, part + 1)
                pe.matmul(ps[:, bank, 0:E * nt], upper[:], Hs[:, 0:E * nt], start=True, stop=True)
                pe.matmul(ps[:, bank + 1, 0:E * nt], ones[:], Hs[:, 0:E * nt], start=True, stop=True).then_inc(ranked, 1)

            def xg_turn(j, s):
                pe.wait_ge(xg_in[s], 8 * (j + 2 - s))
                wait(pe, xg_copied, j)
                for h in range(2):
                    for k in range(KD):
                        mm = pe.transpose(xgps[:, k * TS + h * P:k * TS + (h + 1) * P],
                                          xg[s][:, h, k * P:(k + 1) * P], ident[:])
                mm.then_inc(xg_turned, 1)

            def layer1(j, s):
                def products():
                    wait(pe, xg_copied, j + 1)
                    wait(pe, relu_done, j - 1)
                    pe.wait_ge(w1_in[s], 8 * (j + 2 - s))
                    for f in range(FC):
                        for k in range(KD):
                            mm = pe.matmul(wide[s][:, f * TS:(f + 1) * TS],
                                           w1_sb[s][:, k * F + f * P:k * F + (f + 1) * P], xgT[s][:, k, :],
                                           start=(k == 0), stop=(k == KD - 1))
                    mm.then_inc(l1_done, 1)
                where_taken(pe, j, products, (l1_done,), lambda _: j)

            def layer2(j, s):
                def products():
                    wait(pe, relu_done, j + 1)
                    wait(pe, y_done, j)
                    pe.wait_ge(w2_in[s], 8 * (j + 2 - s))
                    for h in range(2):
                        for f in range(FC):
                            mm = pe.matmul(outps[:, h * D:(h + 1) * D], hT[s][:, f, h * P:(h + 1) * P],
                                           w2_sb[s][:, f * D:(f + 1) * D], start=(f == 0), stop=(f == FC - 1))
                    mm.then_inc(l2_done, 1)
                where_taken(pe, j, products, (l2_done,), lambda _: j)

            def moe_tile(j, s, first=False, last=False, edges=()):
                layer1(j, s)
                for h, g in edges:
                    edge_group(h, g)
                if not last:
                    xg_turn(j + 1, 1 - s)
                if not first:
                    layer2(j - 1, 1 - s)

            layers(0, None, 2 * B0)
            chunks(pe, 1, CA, lambda c: layers(c, c - 1, 2 * B0 + c))
            layers(None, CA - 1)
            rank(0, CA * CH, 4)
            for g in range(HG):
                edge_group(2 * B0 + CA, g)
            pe.wait_ge(slots_done, 1)

            def one_round(i, c2):
                h = 2 * B0 + CA + 1 + 4 * i
                if c2 is not None:
                    free_banks(CA + i, CA + i - 1)
                xg_turn(PER * i, 0)
                for k in range(PER):
                    moe_tile(PER * i + k, k % 2, first=(k == 0), last=(k == PER - 1),
                             edges=[(h, g) for g in range(*SHARE[k])])
                layer2(PER * i + PER - 1, 1)
                wait(pe, y_done, PER * (i + 1))
                layers(CA + i, c2, h + 2, BG)

            def free_banks(c1, c2):
                wait(pe, x2_done, c1 * CH)
                wait(pe, y_copied, c2 * CH)
                wait(pe, logit_done, c2 * CH)
            one_round(0, None)
            chunks(pe, 1, ROUNDS, lambda i: one_round(i, CA + i - 1))
            layers(NC - 1, NC - 2)
            layers(None, NC - 1)

            free_banks(NC, NC)
            xg_turn(J0, 0)
            moe_tile(J0, 0, first=True)
            rank(1, (NC - CA) * CH, 0)
            for j in range(J0 + 1, SA):
                moe_tile(j, j % 2, last=(j == SA - 1))
            layer2(SA - 1, 1)
            pe.wait_ge(slots_done, 2)
            xg_turn(SA, 0)
            moe_tile(SA, 0, first=True)
            moe_tile(SA + 1, 1)
            chunks(pe, SA // 2 + 1, NS // 2 - 1, lambda i: [moe_tile(2 * i + s, s) for s in range(2)])
            moe_tile(NS - 2, 0)
            moe_tile(NS - 1, 1, last=True)
            layer2(NS - 1, 1)


def kernel(x, src, dst, edge_weight, L0_gnn_weight, L0_mix_Wqkv, L0_mix_Wout, L0_mix_bout,
           L0_ffn_gate_w, L0_ffn_gate_b, L0_ffn_w1, L0_ffn_b1, L0_ffn_w2, L0_ffn_b2, L0_ffn_gamma,
           L0_ffn_beta):
    import numpy as np
    import concourse.bacc as bacc
    from concourse.bass_utils import run_bass_kernel_spmd

    def pad(a, n, value):
        a = np.asarray(a)
        return np.concatenate([a, np.full((n - len(a),) + a.shape[1:], value, a.dtype)])

    def by_partition(w):
        w = np.asarray(w)
        return np.ascontiguousarray(w.reshape(-1, P, w.shape[1]).transpose(1, 0, 2))

    n_edges = ET * P
    src_p, dst_p = pad(src, n_edges, 0), pad(dst, n_edges, N - 1)
    wqkv = np.asarray(L0_mix_Wqkv)
    gate_w = np.zeros((D, 96), np.float32)
    gate_w[:, :E] = np.asarray(L0_ffn_gate_w)
    w1 = np.asarray(L0_ffn_w1).reshape(E, KD, P, F).transpose(0, 2, 1, 3).reshape(E, P, KD * F)
    b1 = np.asarray(L0_ffn_b1).reshape(E, FC, P).transpose(0, 2, 1)
    w2 = np.asarray(L0_ffn_w2).reshape(E, FC, P, D).transpose(0, 2, 1, 3).reshape(E, P, W2ROW)
    arrays = {
        "x": pad(x, NP, 0),
        "src": src_p.reshape(ET, P).T, "dst": dst_p.reshape(ET, P).T,
        "first_dst": dst_p[::GT * P].reshape(1, NG),
        "edge_w": pad(edge_weight, n_edges, 0).reshape(ET, P).T,
        "gnn_w": by_partition(L0_gnn_weight),
        "wkv": by_partition(wqkv[INNER:].T), "wq": by_partition(wqkv[:INNER]),
        "wout": by_partition(np.asarray(L0_mix_Wout).T),
        "bout": np.asarray(L0_mix_bout).reshape(1, D),
        "gate_w": by_partition(gate_w), "gate_b": np.asarray(L0_ffn_gate_b).reshape(1, E),
        "w1b": np.concatenate([w1, b1], axis=2),
        "w2b": np.concatenate([w2, np.broadcast_to(np.asarray(L0_ffn_b2)[:, None, :], (E, P, D))], axis=2),
        "gamma": np.asarray(L0_ffn_gamma).reshape(1, D), "beta": np.asarray(L0_ffn_beta).reshape(1, D),
    }
    nc = bacc.Bacc("TRN2", target_bir_lowering=False, num_devices=1)
    feed, args = {}, {}
    for name, a in arrays.items():
        a = np.ascontiguousarray(a)
        feed[f"in_{name}"] = a
        args[name] = nc.dram_tensor(f"in_{name}", a.shape, mybir.dt.from_np(a.dtype), kind="ExternalInput").ap()
    args["out"] = nc.dram_tensor("result", (NP, D), F32, kind="ExternalOutput").ap()
    gps_layer(nc, **args)
    r = run_bass_kernel_spmd(nc, [feed], core_ids=[0])
    return r.results[0]["result"][:N]
```

```python
from contextlib import ExitStack

import concourse.bass as bass
from concourse import mybir

F32 = mybir.dt.float32
I32 = mybir.dt.int32
U32 = mybir.dt.uint32
ALU = mybir.AluOpType
ACT = mybir.ActivationFunctionType
AX = mybir.AxisListType

P = 128
N = 6250
D = 256
KD = D // P
CH = 7
NC = 7
NT = NC * CH
NP = NT * P
PADDED = NP - N
HEADS, DH = 8, 64
INNER = HEADS * DH
NJ = INNER // P
EPS = 1e-5

EDGES = 106250
GT = 4
BG = 2 * CH
BT = BG * GT
NB = -(-EDGES // (BT * P))
NG = NB * BG
ET = NB * BT
HG = CH
HB = BT // 2
RING = 14
W = 128
GW = 448
NW = NP // GW

E, F = 16, 512
FC = F // P
TS = 256
ACT_ROWS = 5
CA = 3
NA = CA * CH * P
AC = 2
B0 = NC
ROUNDS = NC - CA - 1
STARTS = [(B0, CA)] + [(B0 + 3 + 2 * i, CA + 1 + i) for i in range(ROUNDS)]


def expert_tiles(rows, multiple):
    return -(-((rows + E * (TS - 1)) // TS) // multiple) * multiple


SA = expert_tiles(2 * NA, 6)
PER = 6
EXPERT_G = 19
EARLY_G = 3
LATE = SA - PER * ROUNDS
SB = expert_tiles(2 * (N - NA), 2)
NS = SA + SB
XROWS = [SA * TS, SB * TS + TS]
ZR = [-(-n // (NC * P)) for n in XROWS]
assert (NC - CA) * CH == 2 * AC * CH
assert HB % RING == 0 and NB == B0 + 2 + 2 * ROUNDS
W1ROW = KD * F + FC
W2ROW = FC * D
W2BROW = W2ROW + D

LEAD = BG


def gps_layer(nc, x, src, dst, first_dst, edge_w, gnn_w, wkv, wq, wout, bout, gate_w, gate_b,
              w1b, w2b, gamma, beta, out):
    table = nc.dram_tensor("normed_rows", (NP, D), F32, kind="Internal").ap()
    xs = [nc.dram_tensor(f"rows_by_slot{i}", (NC * ZR[i] * P, D), F32, kind="Internal").ap() for i in range(2)]
    ys = [nc.dram_tensor(f"results_by_slot{i}", (XROWS[i], D), F32, kind="Internal").ap() for i in range(2)]

    with ExitStack() as ctx:
        def sb(name, shape, dt=F32):
            return ctx.enter_context(nc.sbuf_tensor(name, shape, dt))

        def sem(name):
            return ctx.enter_context(nc.semaphore(name))

        def sems(name, n):
            return [sem(f"{name}{i}") for i in range(n)]

        X2 = sb("X2", [P, NT, D])
        aggT = sb("aggT", [P, KD, NP])
        ring = sb("ring", [P, RING, D])
        S = sb("S", [P, RING, W])
        gnn_sb = sb("gnn_sb", [P, KD, D])
        M = sb("M", [P, KD, D])

        R = E * max(CA, NC - CA) * CH
        room = sb("room", [P, max(KD * 2 * INNER + 3 * NJ * D + NJ * P + 3 * 2 * INNER,
                                  2 * (W1ROW + W2BROW + FC * TS + 2 * D + KD * TS) + R)])

        def carve(space):
            at = [0]

            def take(*shape):
                n = 1
                for k in shape:
                    n *= k
                at[0] += n
                assert at[0] <= space.shape[1]
                piece = space[:, at[0] - n:at[0]]
                return piece if len(shape) == 1 else piece.rearrange("p (a b) -> p a b", a=shape[0])
            return take
        take = carve(room[:, :])
        wkv_sb = take(KD, 2 * INNER)
        wq_sb = take(NJ, D)
        wout_sb = take(NJ, D)
        T1 = take(NJ, D)
        bd = take(NJ, P)
        sq = take(2 * INNER)
        ks = take(2, INNER)
        vs = take(2, INNER)
        dstrel = sb("dstrel", [P, ET])
        ew = sb("ew", [P, ET])
        src_sb = sb("src_sb", [P, ET], I32)
        idx = sb("idx", [P, 2, HB], I32)
        base_i = sb("base_i", [P, NG], I32)
        base_f = sb("base_f", [P, NG])
        tile_in = sb("tile_in", [P, CH, D])
        tT = sb("tT", [P, 2, D])
        aT = sb("aT", [P, 2, D])
        yT = sb("yT", [P, 2, D])
        yt = sb("yt", [P, 2, D])
        ident = sb("ident", [P, P])
        iota = sb("iota", [P, GW])
        ones = sb("ones", [P, P])
        upper = sb("upper", [P, P])
        gate_sb = sb("gate_sb", [P, KD, 96])
        bout_b = sb("bout_b", [P, D])
        gamma_b = sb("gamma_b", [P, D])
        beta_b = sb("beta_b", [P, D])
        gb_b = sb("gb_b", [P, E])
        logits = sb("logits", [P, CH, E])
        top8 = sb("top8", [P, CH, 8])
        top8_i = sb("top8_i", [P, CH, 8], U32)
        top = sb("top", [P, 2, NT])
        bn = sb("bn", [P, CH, 6])
        mv = sb("mv", [P, NT, 2])
        mvc = sb("mvc", [P, CH, 2])
        rstd = sb("rstd", [P, NT])
        nmr = sb("nmr", [P, NT])
        kv_var = sb("kv_var", [P, 2, 2 * HEADS])
        kv_r = sb("kv_r", [P, 2 * HEADS])
        kv_s = sb("kv_s", [P, 2, HEADS])
        eps_t = sb("eps_t", [P, 1])
        slot_f = sb("slot_f", [P, 2, NT + CH])
        zeros = sb("zeros", [P, D])
        prob = sb("prob", [P, 2, NT])
        slot_i = sb("slot_i", [P, 2, NT], I32)
        sidx = sb("sidx", [P, 2, CH], I32)
        sidx_odd = sb("sidx_odd", [P, 2, CH], I32)
        ay = sb("ay", [P, D])
        cy = sb("cy", [P, D])
        etab = sb("etab", [1, NS], I32)
        taken = sb("taken", [1, NS], I32)
        small = sb("small", [P, 160])
        flag = sb("flag", [1, 1], I32)
        idx_gen = sb("idx_gen", [P, GT], I32)

        take = carve(room[:, :])
        w1_sb = [take(W1ROW) for _ in range(2)]
        w2_sb = [take(W2BROW) for _ in range(2)]
        hT = [take(FC, TS) for _ in range(2)]
        xg = [take(2, D) for _ in range(2)]
        xgT = [take(KD, TS) for _ in range(2)]
        tot = take(R)
        take = carve(aggT[:, 0, 0:NA])
        yo = [take(2, D) for _ in range(2)]
        H1, H2 = [take(R) for _ in range(2)]
        take = carve(aggT[:, 1, 0:NA])
        Hs, pos, scan, iota_e = [take(R) for _ in range(4)]
        cmp_t = take(max(SA, SB), E)
        Sgen = X2[:, :, :].rearrange("p q d -> p (q d)")[:, 0:GT * GW].rearrange("p (t w) -> p t w", t=GT)
        dst_gen = kv_r[:, 0:GT]

        ps = ctx.enter_context(nc.psum_tensor("ps", [P, 8, 512], F32))
        aggps = [ps[:, i, 0:KD * W] for i in range(2)]
        tps = ps[:, 2, 0:D]
        yps = ps[:, 3, 0:D]
        xgps = ps[:, 2, :]
        outps = ps[:, 3, :]
        dotps = ps[:, 3, :].rearrange("p (j e) -> p j e", j=NJ)
        wide = [ps[:, 4 + 2 * i:6 + 2 * i, :].rearrange("p a b -> p (a b)") for i in range(2)]

        consts_in = sem("consts_in")
        pool_consts = sem("pool_consts")
        dve_consts = sem("dve_consts")
        tables_in = sem("tables_in")
        later_in = sem("later_in")
        x_in = sems("x_in", 2)
        xs_in = sems("xs_in", 2)
        stats_done = sem("stats_done")
        std_done = sem("std_done")
        rstd_done = sem("rstd_done")
        normed = sem("normed")
        dve_normed = sem("dve_normed")
        table_out = sem("table_out")
        idx_staged = sem("idx_staged")
        gathered = sems("gathered", RING)
        selected = sem("selected")
        group_done = sem("group_done")
        group_added = sem("group_added")
        tile_loaded = sems("tile_loaded", CH)
        tile_turned = sem("tile_turned")
        turned_copied = sem("turned_copied")
        kv_done = sem("kv_done")
        kv_squared = sem("kv_squared")
        v_copied = sem("v_copied")
        kv_var_done = sem("kv_var_done")
        kv_std_done = sem("kv_std_done")
        kv_r_done = sem("kv_r_done")
        k_scaled = sem("k_scaled")
        dots_done = sem("dots_done")
        bd_done = sem("bd_done")
        t1_done = sem("t1_done")
        t1_copied = sem("t1_copied")
        m_done = sem("m_done")
        m_copied = sem("m_copied")
        x_again = sems("x_again", CH)
        x_biased = sem("x_biased")
        bad_found = sem("bad_found")
        bad_counted = sem("bad_counted")
        flag_ready = sem("flag_ready")
        gen_zeroed = sem("gen_zeroed")
        gen_idx_in = sem("gen_idx_in")
        gen_gathered = sems("gen_gathered", GT)
        gen_dst = sem("gen_dst")
        gen_selected = sem("gen_selected")
        gen_done = sem("gen_done")
        gen_added = sem("gen_added")
        agg_final = sem("agg_final")
        agg_staged = sem("agg_staged")
        layers_done = sem("layers_done")
        x2_done = sem("x2_done")
        y_bn = sem("y_bn")
        y_stats = sem("y_stats")
        y_std = sem("y_std")
        y_rstd = sem("y_rstd")
        y_normed = sem("y_normed")
        y_turned = sem("y_turned")
        y_copied = sem("y_copied")
        gate_done = sem("gate_done")
        logit_done = sem("logit_done")
        hot_done = sem("hot_done")
        ranked = sem("ranked")
        exp_in = sem("exp_in")
        exp_done = sem("exp_done")
        slots_done = sem("slots_done")
        zero_out = sem("zero_out")
        sidx_done = sem("sidx_done")
        row_ready = sem("row_ready")
        scattered = sems("scattered", CH)
        w1_in = sems("w1_in", 2)
        w2_in = sems("w2_in", 2)
        xg_in = sems("xg_in", 2)
        xg_turned = sem("xg_turned")
        xg_copied = sem("xg_copied")
        l1_done = sem("l1_done")
        relu_done = sem("relu_done")
        l2_done = sem("l2_done")
        y_done = sem("y_done")
        ys_out = sems("ys_out", 2)
        sidx_staged = sem("sidx_staged")
        a_picked = sem("a_picked")
        a_again = sem("a_again")
        a_stats = sem("a_stats")
        a_std = sem("a_std")
        a_rstd = sem("a_rstd")
        a_normed = sem("a_normed")
        a_summed = sem("a_summed")
        a_done = sem("a_done")
        a_out = sem("a_out")
        picked = sems("picked", CH)
        y_again = sem("y_again")
        summed = sem("summed")
        beta_added = sem("beta_added")
        rows_again = sem("rows_again")
        half_summed = sem("half_summed")
        f_stats = sem("f_stats")
        f_std = sem("f_std")
        f_rstd = sem("f_rstd")
        f_normed = sem("f_normed")
        f_done = sem("f_done")
        f_out = sems("f_out", CH)
        pool_past = sem("pool_past")
        dve_past = sem("dve_past")

        LEADERS = {"tensor": [group_done, gen_done, tile_turned, kv_done, dots_done, layers_done, gate_done,
                              y_turned, xg_turned, l1_done, l2_done],
                   "vector": [group_added, k_scaled, kv_var_done, x2_done, y_copied, logit_done, y_done,
                              gen_added, half_summed, summed],
                   "scalar": [v_copied, kv_squared, turned_copied, xg_copied, relu_done]}
        ahead = {s for group in LEADERS.values() for s in group}

        def wait(eng, s, n):
            eng.wait_ge(s, n + LEAD if s in ahead else n)

        def start_counters(eng, names):
            for s in names:
                eng.sem_inc(s, LEAD)

        def where_taken(eng, j, work, done, n, by=1):
            some = eng.value_load(taken[0:1, bass.ds(j, 1)], min_val=0, max_val=1)
            with eng.If(some > 0):
                work()
            with eng.Else():
                for s in done:
                    if n(s) is not None:
                        wait(eng, s, n(s))
                    eng.sem_inc(s, by)

        def before(j, s, each):
            return lambda _: None if isinstance(j, int) and j < 2 else each * (j - s)

        def prior(j):
            return 1 if j == 0 else 2

        def chunks(eng, first, last, body):
            with eng.Fori(first, last) as c:
                body(c)

        TABLES = [(dstrel[:, :].bitcast(I32), dst), (base_i[:, :], first_dst.to_broadcast([P, NG]))]
        CONSTS = [(ew[:, :], edge_w), (src_sb[:, :], src), (wkv_sb, wkv)]
        LATER = [(wq_sb, wq), (wout_sb, wout), (gnn_sb[:, :, :], gnn_w), (gate_sb[:, :, :], gate_w),
                 (bout_b[:, :], bout.to_broadcast([P, D])), (gamma_b[:, :], gamma.to_broadcast([P, D])),
                 (beta_b[:, :], beta.to_broadcast([P, D])), (gb_b[:, :], gate_b.to_broadcast([P, E]))]

        def share(k, g0):
            return range(g0 + (EXPERT_G - g0) * k // PER, g0 + (EXPERT_G - g0) * (k + 1) // PER)
        J0 = SA - LATE

        block = ctx.enter_context(nc.Block())

        @block.sync
        def _(sp):
            for n, (j0, j1) in enumerate(((0, 2), (2, CH))):
                sp.dma_start(X2[:, j0:j1, :], x[j0 * P:j1 * P, :].rearrange("(j p) d -> p j d", p=P)).then_inc(x_in[n], 16)
            for o, i in TABLES:
                sp.dma_start(o, i).then_inc(tables_in, 16)

            def load_x(i):
                for s in range(2):
                    c = 2 * i + 1 + s
                    if not isinstance(i, int):
                        sp.wait_ge(xs_in[s], 16 * i)
                    sp.dma_start(X2[:, bass.ds(c * CH, CH), :],
                                 x[bass.ds(c * (CH * P), CH * P), :].rearrange("(j p) d -> p j d", p=P)).then_inc(xs_in[s], 16)
            load_x(0)
            chunks(sp, 1, NC // 2, load_x)
            for o, i in CONSTS:
                sp.dma_start(o, i).then_inc(consts_in, 16)

            def store_table(c):
                sp.wait_ge(normed, ACT_ROWS * (c + 1))
                sp.wait_ge(dve_normed, c + 1)
                sp.dma_start(table[bass.ds(c * (CH * P), CH * P), :].rearrange("(j p) d -> p j d", p=P),
                             X2[:, bass.ds(c * CH, CH), :]).then_inc(table_out, 16)
            chunks(sp, 0, NC, store_table)
            for o, i in LATER:
                sp.dma_start(o, i).then_inc(later_in, 16)
            sp.wait_ge(table_out, 16 * NC)

            sp.wait_ge(flag_ready, 1)
            bad = sp.value_load(flag[0:1, 0:1], min_val=0, max_val=P)
            with sp.If(bad > 0):
                with sp.Fori(0, NG) as g:
                    wait(sp, gen_done, g * NW)
                    sp.dma_start(idx_gen[:, :], src[:, bass.ds(g * GT, GT)]).then_inc(gen_idx_in, 16)

            def load_tile(c, j, again):
                q = c * CH + j
                wait(sp, tile_turned, q - CH + 1 + (NT if again else 0))
                sp.dma_start(tile_in[:, j, :], table[bass.ds(q * P, P), :]).then_inc(tile_loaded[j], 16)
                if again:
                    wait(sp, x2_done, q - CH + 1)
                    sp.dma_start(X2[:, bass.ds(q, 1), :].rearrange("p a d -> p (a d)"),
                                 x[bass.ds(q * P, P), :]).then_inc(x_again[j], 16)
            chunks(sp, 0, NC, lambda c: [load_tile(c, j, False) for j in range(CH)])
            chunks(sp, 0, CA, lambda c: [load_tile(c, j, True) for j in range(CH)])

            def load_rows(part, j, s):
                wait(sp, xg_turned, j - 1)
                sp.dma_start(xg[s], xs[part][bass.ds((j - SA * part) * TS, TS), :].rearrange("(h p) d -> p h d", p=P)).then_inc(xg_in[s], 16)

            def load_w1(j, s):
                def load():
                    e = sp.value_load(etab[0:1, bass.ds(j, 1)], min_val=0, max_val=E - 1)
                    wait(sp, relu_done, j - 1)
                    sp.dma_start(w1_sb[s], w1b[bass.ds(e, 1)].rearrange("a p w -> (a p) w")).then_inc(w1_in[s], 16)
                where_taken(sp, j, load, (w1_in[s],), before(j, s, 8), 16)

            def load_w2(j, s):
                def load():
                    e = sp.value_load(etab[0:1, bass.ds(j, 1)], min_val=0, max_val=E - 1)
                    wait(sp, y_done, j - 1)
                    sp.dma_start(w2_sb[s], w2b[bass.ds(e, 1)].rearrange("a p w -> (a p) w")).then_inc(w2_in[s], 16)
                where_taken(sp, j, load, (w2_in[s],), before(j, s, 8), 16)

            def load_tiles(part, i, first=False, flush=False, last=False, store=False):
                for s in range(2):
                    j = 2 * i + s
                    if not (last and s):
                        load_rows(part, j + 1, 1 - s)
                    load_w1(j, s)
                    if not (first and s == 0):
                        load_w2(j - 1, 1 - s)
                if flush or last:
                    load_w2(2 * i + 1, 1)
                if store:
                    store_a(i - SA // 2 - 1)

            def store_a(q):
                sp.wait_ge(a_done, q + 1)
                sp.dma_start(out[bass.ds(q * P, P), :], cy[:]).then_inc(a_out, 16)
            sp.wait_ge(slots_done, 1)
            for j in range(CH):
                sp.wait_ge(scattered[j], 32 * CA)

            def load_round(i):
                for k in range(PER // 2):
                    load_tiles(0, i * (PER // 2) + k, first=(k == 0), flush=(k == PER // 2 - 1))
                for j in range(CH):
                    load_tile(CA + i, j, True)
            load_rows(0, 0, 0)
            chunks(sp, 0, ROUNDS, load_round)
            for j in range(CH):
                load_tile(NC - 1, j, True)
            load_tiles(0, J0 // 2, first=True)
            chunks(sp, J0 // 2 + 1, SA // 2 - 1, lambda i: load_tiles(0, i))
            load_tiles(0, SA // 2 - 1, last=True)
            sp.wait_ge(slots_done, 2)
            for j in range(CH):
                sp.wait_ge(scattered[j], 32 * NC)
            load_rows(1, SA, 0)
            load_tiles(1, SA // 2, first=True)
            chunks(sp, SA // 2 + 1, SA // 2 + 1 + AC * CH, lambda i: load_tiles(1, i, store=True))
            chunks(sp, SA // 2 + 1 + AC * CH, NS // 2 - 1, lambda i: load_tiles(1, i))
            load_tiles(1, NS // 2 - 1, last=True)
            sp.wait_ge(a_out, 16 * AC * CH)

            def store_out(c):
                for j in range(CH):
                    q = c * CH + j
                    sp.wait_ge(f_done, q + 1 - AC * CH)
                    sp.dma_start(out[bass.ds(q * P, P), :], tile_in[:, j, :]).then_inc(f_out[j], 16)
            chunks(sp, AC, NC, store_out)
            for j in range(CH):
                sp.wait_ge(f_out[j], 16 * (NC - AC))

        @block.gpsimd
        def _(pool):
            pool.memset(ones[:], 1.0).then_inc(pool_consts, 1)
            pool.memset(eps_t[:], EPS).then_inc(pool_consts, 1)
            pool.memset(aggT[:, :, :], 0.0).then_inc(pool_consts, 1)
            pool.memset(bd, 0.0).then_inc(pool_consts, 1)
            pool.memset(zeros[:], 0.0).then_inc(pool_consts, 1)
            pool.iota(iota[:], [[1, GW]], base=0, channel_multiplier=0, allow_small_or_imprecise_dtypes=True).then_inc(pool_consts, 1)
            pool.wait_ge(pool_consts, 1)
            pool.affine_select(out=ident[:], in_=ones[:], compare_op=ALU.is_equal, fill=0.0, base=0,
                               pattern=[[-1, P]], channel_multiplier=1).then_inc(pool_consts, 1)
            pool.affine_select(out=upper[:], in_=ones[:], compare_op=ALU.is_gt, fill=0.0, base=0,
                               pattern=[[1, P]], channel_multiplier=-1).then_inc(pool_consts, 1)
            pool.iota(small[:, 128:129], [[0, 1]], base=0, channel_multiplier=1,
                      allow_small_or_imprecise_dtypes=True).then_inc(pool_consts, 1)

            pool.wait_ge(table_out, 16 * NC)

            pool.wait_ge(flag_ready, 1)
            bad = pool.value_load(flag[0:1, 0:1], min_val=0, max_val=P)
            with pool.If(bad > 0):
                with pool.Fori(0, NG) as g:
                    pool.wait_ge(gen_idx_in, 16 * (g + 1))
                    pool.sem_inc(pool_past)
                    for t in range(GT):
                        pool.indirect_dma_start(
                            out=ring[:, t, :], out_offset=None, in_=table,
                            in_offset=bass.IndirectOffsetOnAxis(ap=idx_gen[:, t:t + 1], axis=0),
                        ).then_inc(gen_gathered[t], 16)
                wait(pool, gen_done, NG * NW)

            def stage_idx(b, half):
                pool.tensor_copy(idx[:, half, :], src_sb[:, bass.ds(b * BT + half * HB, HB)]).then_inc(idx_staged, 1)
            pool.wait_ge(consts_in, 16 * len(CONSTS))
            stage_idx(0, 0)

            def gather_block(b, m0=0, m1=BT, last=False):
                for m in range(m0, m1):
                    half = m // HB
                    carries = False
                    if m % HB == 0:
                        pool.wait_ge(idx_staged, 2 * b + half + 1)
                        carries = True
                    if (m - RING) // GT != (m - 1 - RING) // GT:
                        wait(pool, group_done, b * BG + (m - RING) // GT + 1)
                        carries = True
                    if carries:
                        pool.sem_inc(pool_past)
                    if m % HB == RING and not (last and half):
                        stage_idx(b + half, 1 - half)
                    pool.indirect_dma_start(
                        out=ring[:, m % RING, :], out_offset=None, in_=table,
                        in_offset=bass.IndirectOffsetOnAxis(ap=idx[:, half, m % HB:m % HB + 1], axis=0),
                    ).then_inc(gathered[m % RING], 16)

            def scatter(part, c):
                if isinstance(c, int):
                    pool.wait_ge(slots_done, 1 if c == 0 else 2)
                if not (isinstance(c, int) and c == 0):
                    for j in range(CH):
                        pool.wait_ge(scattered[j], 32 * c)
                pool.sem_inc(pool_past)
                pool.tensor_copy(sidx[:, :, :], slot_i[:, :, bass.ds(c * CH, CH)]).then_inc(sidx_staged, 1)
                for j in range(CH):
                    if j == 0:
                        pool.wait_ge(sidx_staged, c + 1)
                    pool.wait_ge(row_ready, c * CH + j + 1)
                    pool.sem_inc(pool_past)
                    for k in range(2):
                        pool.indirect_dma_start(
                            out=xs[part], out_offset=bass.IndirectOffsetOnAxis(ap=sidx[:, k, j:j + 1], axis=0),
                            in_=tile_in[:, j, :], in_offset=None).then_inc(scattered[j], 16)
            chunks(pool, 0, B0 + 2, gather_block)
            pool.wait_ge(zero_out, 16 * (2 * NC + 1))
            gather_block(B0 + 2, m1=RING)
            scatter(0, 0)
            chunks(pool, 1, CA, lambda c: scatter(0, c))
            gather_block(B0 + 2, m0=RING)
            chunks(pool, B0 + 3, NB - 1, gather_block)
            gather_block(NB - 1, last=True)
            scatter(1, CA)
            chunks(pool, CA + 1, NC, lambda c: scatter(1, c))

            for s in range(2):
                pool.wait_ge(ys_out[s], 16 * (SA // 2))
            for j in range(CH):
                pool.wait_ge(scattered[j], 32 * NC)

            def pick_a(q):
                if not isinstance(q, int):
                    pool.wait_ge(a_picked, 32 * q)
                    pool.sem_inc(pool_past)
                pool.tensor_copy(sidx[:, :, 0:1], slot_i[:, :, bass.ds(q, 1)]).then_inc(sidx_staged, 1)
                pool.wait_ge(sidx_staged, NC + q + 1)
                wait(pool, a_summed, q)
                pool.sem_inc(pool_past)
                for k in range(2):
                    pool.indirect_dma_start(
                        out=ring[:, k, :], out_offset=None, in_=ys[0],
                        in_offset=bass.IndirectOffsetOnAxis(ap=sidx[:, k, 0:1], axis=0),
                    ).then_inc(a_picked, 16)
            pick_a(0)
            chunks(pool, 1, AC * CH, pick_a)
            pool.wait_ge(a_picked, 32 * AC * CH)
            pool.wait_ge(a_summed, AC * CH)

            def pick(part, c):
                rows = (sidx, sidx_odd)[c % 2]
                if c - AC >= 2:
                    for j in range(CH):
                        pool.wait_ge(picked[j], 32 * (c - AC - 1))
                pool.tensor_copy(rows[:, :, :], slot_i[:, :, c * CH:(c + 1) * CH]).then_inc(sidx_staged, 1)
                for j in range(CH):
                    if j == 0:
                        pool.wait_ge(sidx_staged, NC + AC * CH + c - AC + 1)
                    wait(pool, summed, (c - AC) * CH + j - CH + 1)
                    for k in range(2):
                        pool.indirect_dma_start(
                            out=ring[:, 2 * j + k, :], out_offset=None, in_=ys[part],
                            in_offset=bass.IndirectOffsetOnAxis(ap=rows[:, k, j:j + 1], axis=0),
                        ).then_inc(picked[j], 16)
            for c in range(AC, CA):
                pick(0, c)
            for s in range(2):
                pool.wait_ge(ys_out[s], 16 * (NS // 2))
            for c in range(CA, NC):
                pick(1, c)

        @block.scalar
        def _(act):
            start_counters(act, LEADERS["scalar"])

            act.wait_ge(pool_consts, 2)

            def norm_chunk(c):
                act.wait_ge(stats_done, c + 1)
                act.activation(rstd[:, bass.ds(c * CH, CH)], mv[:, bass.ds(c * CH, CH), 1], ACT.Sqrt,
                               bias=eps_t[:]).then_inc(std_done, 1)
                act.wait_ge(rstd_done, c + 1)
                for j in range(ACT_ROWS):
                    q = c * CH + j
                    act.activation(X2[:, bass.ds(q, 1), :], X2[:, bass.ds(q, 1), :], ACT.Identity,
                                   bias=nmr[:, bass.ds(q, 1)], scale=rstd[:, bass.ds(q, 1)]).then_inc(normed, 1)
            chunks(act, 0, NC, norm_chunk)

            def copy_turned(n, j):
                wait(act, tile_turned, n + 1)
                act.copy(tT[:, j % 2, :], tps).then_inc(turned_copied, 1)

            def kv_root(q, j):
                wait(act, kv_var_done, q + 1)
                act.activation(kv_var[:, j % 2, :], kv_var[:, j % 2, :], ACT.Sqrt, bias=eps_t[:],
                               scale=1.0 / DH).then_inc(kv_std_done, 1)

            def zero_slots(b):
                for rows, zr in zip(xs, ZR):
                    act.dma_start(rows[bass.ds(b * (zr * P), zr * P), :].rearrange("(p a) d -> p a d", p=P),
                                  zeros[:].unsqueeze(1).to_broadcast([P, zr, D])).then_inc(zero_out, 16)
            act.wait_ge(pool_consts, 9)
            act.dma_start(ys[1][SB * TS:, :].rearrange("(p a) d -> p a d", p=P),
                          zeros[:].unsqueeze(1).to_broadcast([P, TS // P, D])).then_inc(zero_out, 16)

            def kv_tile(b, j, first):
                q = b * CH + j
                if j == 2:
                    zero_slots(b)
                wait(act, kv_done, q - prior(j) + 1)
                copy_turned(q, j)
                if not (first and j == 0):
                    kv_root(q - 1, (j - 1) % CH)
                wait(act, kv_done, q + 1)
                wait(act, kv_var_done, q)
                act.activation(sq, wide[j % 2], ACT.Square).then_inc(kv_squared, 1)
                wait(act, dots_done, q - prior(j) + 1)
                act.copy(vs[:, j % 2, :], wide[j % 2][:, INNER:]).then_inc(v_copied, 1)

            for j in range(CH):
                kv_tile(0, j, True)
            chunks(act, 1, NC, lambda b: [kv_tile(b, j, False) for j in range(CH)])
            kv_root(NT - 1, CH - 1)

            act.wait_ge(t1_done, 1)
            act.copy(T1, wide[0].rearrange("p (j d) -> p j d", j=NJ)).then_inc(t1_copied, 1)
            act.wait_ge(m_done, 1)
            act.copy(M[:, :, :], wide[1][:, 0:KD * D].rearrange("p (k d) -> p k d", k=KD)).then_inc(m_copied, 1)

            def layers(c1, c2):
                def normed_row(j):
                    q = c2 * CH + j
                    wait(act, y_turned, q - prior(j) + 1)
                    act.activation(yt[:, j % 2, :], X2[:, bass.ds(q, 1), :], ACT.Identity,
                                   bias=nmr[:, bass.ds(q, 1)], scale=rstd[:, bass.ds(q, 1)]).then_inc(y_normed, 1)

                if c2 is not None:
                    act.wait_ge(y_rstd, c2 + 1)
                    normed_row(0)
                for j in range(CH):
                    if c1 is not None:
                        q = c1 * CH + j
                        wait(act, layers_done, q - prior(j) + 1)
                        act.copy(aT[:, j % 2, :].rearrange("p (k n) -> p k n", k=KD),
                                 aggT[:, :, bass.ds(q * P, P)]).then_inc(agg_staged, 1)
                        copy_turned(NT + q, j)
                    if c2 is not None and j + 1 < CH:
                        normed_row(j + 1)
                if c1 is not None:
                    cols = bass.ds(c1 * CH, CH)
                    act.wait_ge(y_stats, c1 + 1)
                    act.activation(rstd[:, cols], mv[:, cols, 1], ACT.Sqrt, bias=eps_t[:]).then_inc(y_std, 1)

            def row(out_ap, q):
                return act.activation(out_ap, X2[:, bass.ds(q, 1), :], ACT.Identity,
                                      bias=nmr[:, bass.ds(q, 1)], scale=rstd[:, bass.ds(q, 1)])

            def exp_part(part, c0, c1):
                act.wait_ge(exp_in, part + 1)
                p1 = prob[:, 1, c0 * CH:c1 * CH]
                act.activation(p1, p1, ACT.Exp).then_inc(exp_done, 1)

            def row_for_scatter(c, j):
                if not isinstance(c, int) or c > 0:
                    act.wait_ge(scattered[j], 32 * c)
                row(tile_in[:, j, :], c * CH + j).then_inc(row_ready, 1)

            def rows_chunk(c):
                for j in range(CH):
                    if isinstance(c, int):
                        wait(act, tile_turned, NT + (CA if c == 0 else NC) * CH)
                    row_for_scatter(c, j)

            def xg_copy(j, s):
                wait(act, xg_turned, j + 1)
                act.copy(xgT[s], xgps.rearrange("p (k t) -> p k t", k=KD)).then_inc(xg_copied, 1)

            def store_y(j, s, part=1):
                wait(act, y_done, j + 1)
                act.dma_start(ys[part][bass.ds((j - SA * part) * TS, TS), :].rearrange("(h p) d -> p h d", p=P), yo[s]).then_inc(ys_out[s], 16)

            def moe_tile(j, s, first=False, last=False, part=1):
                def relu():
                    wait(act, l1_done, j + 1)
                    wait(act, l2_done, j - 1)
                    for f in range(FC):
                        r = act.activation(hT[s][:, f, :], wide[s][:, f * TS:(f + 1) * TS], ACT.Relu,
                                           bias=w1_sb[s][:, KD * F + f:KD * F + f + 1])
                    r.then_inc(relu_done, 1)
                if not last:
                    xg_copy(j + 1, 1 - s)
                where_taken(act, j, relu, (relu_done,), lambda _: j)
                if not first:
                    store_y(j - 1, 1 - s, part)

            layers(0, None)
            chunks(act, 1, CA, lambda c: layers(c, c - 1))
            layers(None, CA - 1)
            exp_part(0, 0, CA)
            rows_chunk(0)
            chunks(act, 1, CA, rows_chunk)

            def one_round(i, c2):
                xg_copy(PER * i, 0)
                for k in range(PER):
                    moe_tile(PER * i + k, k % 2, first=(k == 0), last=(k == PER - 1), part=0)
                store_y(PER * i + PER - 1, 1, part=0)
                layers(CA + i, c2)
            act.wait_ge(slots_done, 1)
            one_round(0, None)
            chunks(act, 1, ROUNDS, lambda i: one_round(i, CA + i - 1))
            layers(NC - 1, NC - 2)
            layers(None, NC - 1)
            xg_copy(J0, 0)
            exp_part(1, CA, NC)
            rows_chunk(CA)
            for j in range(J0, SA):
                moe_tile(j, j % 2, first=(j == J0), last=(j == SA - 1), part=0)
                n = 7 * (j - J0 - 5) // 2
                for i in range(max(n, 0), max(n + 4 - (j - J0) % 2, 0)):
                    if i < CH * (NC - CA - 1):
                        row_for_scatter(CA + 1 + i // CH, i % CH)
            store_y(SA - 1, 1, part=0)
            act.wait_ge(slots_done, 2)
            xg_copy(SA, 0)

            def again_a(q):
                row(ay[:], q).then_inc(a_again, 1)

            def finish_a(q):
                act.wait_ge(a_stats, q + 1)
                act.activation(small[:, 48:49], mvc[:, 0, 1:2], ACT.Sqrt, bias=eps_t[:]).then_inc(a_std, 1)
                if not isinstance(q, int):
                    act.wait_ge(a_out, 16 * q)
                act.wait_ge(a_rstd, q + 1)
                act.activation(cy[:], ay[:], ACT.Identity, bias=small[:, 50:51], scale=small[:, 49:50]).then_inc(a_normed, 1)

            def moe_a(i, first=False):
                q = i - SA // 2
                moe_tile(2 * i, 0, first=first)
                again_a(q)
                moe_tile(2 * i + 1, 1)
                finish_a(q)
                if not first:
                    rows_in_place(q - 1)

            def rows_in_place(q):
                for s in range(2):
                    act.wait_ge(beta_added, 2 * q + s + 1)
                    row(X2[:, bass.ds(CA * CH + 2 * q + s, 1), :], CA * CH + 2 * q + s).then_inc(rows_again, 1)
            moe_a(SA // 2, first=True)
            chunks(act, SA // 2 + 1, SA // 2 + AC * CH, moe_a)
            rows_in_place(AC * CH - 1)
            chunks(act, SA // 2 + AC * CH, NS // 2 - 1, lambda i: [moe_tile(2 * i + s, s) for s in range(2)])
            for s in range(2):
                moe_tile(NS - 2 + s, s, last=(s == 1))
            store_y(NS - 1, 1)

            def out_chunk(c):
                if isinstance(c, int):
                    for j in range(CH):
                        act.wait_ge(scattered[j], 32 * NC)
                        row(tile_in[:, j, :], c * CH + j).then_inc(y_again, 1)
                act.wait_ge(f_stats, c - AC + 1)
                act.activation(small[:, 8:8 + CH], small[:, 16:16 + CH], ACT.Sqrt, bias=eps_t[:]).then_inc(f_std, 1)
                act.wait_ge(f_rstd, c - AC + 1)
                for j in range(CH):
                    act.activation(tile_in[:, j, :], tile_in[:, j, :], ACT.Identity,
                                   bias=small[:, 32 + j:33 + j], scale=small[:, 24 + j:25 + j]).then_inc(f_normed, 1)
            out_chunk(AC)
            chunks(act, CA, NC, out_chunk)

        @block.vector
        def _(dve):
            start_counters(dve, LEADERS["vector"])

            def stats_chunk(c, s):
                if s is not None:
                    dve.wait_ge(xs_in[s], 8 * (c + 1 - s))
                    dve.sem_inc(dve_past)
                for j in range(CH):
                    if s is None and j in (0, 2):
                        dve.wait_ge(x_in[j // 2], 16)
                    dve.bn_stats(bn[:, j, :], X2[:, bass.ds(c * CH + j, 1), :].rearrange("p a d -> p (a d)"))
                dve.drain()
                for j in range(CH):
                    dve.bn_aggr(mvc[:, j, :], bn[:, j, :])
                dve.drain()
                dve.tensor_copy(mv[:, bass.ds(c * CH, CH), :], mvc[:, :, :]).then_inc(stats_done, 1)

            def scale_chunk(c):
                dve.wait_ge(std_done, c + 1)
                cols = bass.ds(c * CH, CH)
                dve.reciprocal(rstd[:, cols], rstd[:, cols])
                dve.drain()
                dve.scalar_tensor_tensor(out=nmr[:, cols], in0=mv[:, cols, 0], scalar=-1.0, in1=rstd[:, cols],
                                         op0=ALU.mult, op1=ALU.mult)
                dve.drain().then_inc(rstd_done, 1)
                for j in range(ACT_ROWS, CH):
                    q = c * CH + j
                    ins = dve.tensor_scalar(X2[:, bass.ds(q, 1), :].rearrange("p a d -> p (a d)"),
                                            X2[:, bass.ds(q, 1), :].rearrange("p a d -> p (a d)"),
                                            rstd[:, bass.ds(q, 1)], nmr[:, bass.ds(q, 1)], ALU.mult, ALU.add)
                ins.then_inc(dve_normed, 1)

            def next_chunk(c, s):
                stats_chunk(c, s)
                scale_chunk(c - 1)
            stats_chunk(0, None)
            chunks(dve, 0, NC // 2, lambda i: [next_chunk(2 * i + 1 + s, s) for s in range(2)])
            scale_chunk(NC - 1)

            dve.wait_ge(tables_in, 16 * len(TABLES))
            dve.tensor_copy(base_f[:], base_i[:])
            dve.tensor_copy(dstrel[:, :], dstrel[:, :].bitcast(I32))
            dve.drain()
            dve.tensor_scalar(base_f[:], base_f[:], float(NP - W), None, ALU.min)
            for n, (b, c) in enumerate(STARTS):
                dve.tensor_reduce(small[:, 140 + n:141 + n], dstrel[:, b * BT:], AX.X, ALU.min)
            dve.drain()
            for n, (b, c) in enumerate(STARTS):
                dve.tensor_scalar(base_f[:, b * BG:], base_f[:, b * BG:], float(c * CH * P), None, ALU.max)
                dve.tensor_scalar(small[:, 150 + n:151 + n], small[:, 140 + n:141 + n], float(c * CH * P), None, ALU.is_lt)
                dve.drain()
            dve.tensor_reduce(small[:, 6:7], small[:, 150:150 + len(STARTS)], AX.X, ALU.max)
            dve.drain()
            dve.tensor_copy(base_i[:], base_f[:])
            d3 = dstrel[:, :].rearrange("p (g t) -> p g t", t=GT)
            dve.tensor_tensor(d3, d3, base_f[:, :].unsqueeze(2).to_broadcast([P, NG, GT]), ALU.subtract)
            dve.drain()
            dve.tensor_reduce(small[:, 0:1], dstrel[:, :], AX.X, ALU.max)
            dve.tensor_reduce(small[:, 1:2], dstrel[:, :], AX.X, ALU.min)
            dve.drain()
            dve.tensor_scalar(small[:, 2:3], small[:, 0:1], float(W), None, ALU.is_ge)
            dve.tensor_scalar(small[:, 3:4], small[:, 1:2], 0.0, None, ALU.is_lt)
            dve.drain()
            dve.tensor_tensor(small[:, 4:5], small[:, 2:3], small[:, 3:4], ALU.max)
            dve.drain()
            dve.tensor_tensor(small[:, 4:5], small[:, 4:5], small[:, 6:7], ALU.max).then_inc(bad_found, 1)
            dve.wait_ge(bad_counted, 1)
            dve.tensor_copy(flag[:, :], ps[0:1, 3, 0:1]).then_inc(flag_ready, 1)
            dve.tensor_scalar(small[:, 7:8], ps[:, 3, 0:1], 0.0, None, ALU.is_equal)

            dve.wait_ge(pool_consts, 9)
            dve.wait_ge(consts_in, 16 * len(CONSTS))
            w3 = wkv_sb.rearrange("p k (h d) -> p (k h) d", d=DH)
            m3 = sq[:, 0:KD * 2 * HEADS]
            dve.tensor_reduce(m3, w3, AX.X, ALU.add)
            dve.drain()
            dve.tensor_scalar(m3, m3, 1.0 / DH, None, ALU.mult)
            dve.drain()
            dve.tensor_tensor(w3, w3, m3.unsqueeze(2).to_broadcast([P, KD * 2 * HEADS, DH]), ALU.subtract)
            dve.drain().then_inc(dve_consts, 1)

            dve.wait_ge(flag_ready, 1)
            bad = dve.value_load(flag[0:1, 0:1], min_val=0, max_val=P)
            with dve.If(bad > 0):
                dve.wait_ge(table_out, 16 * NC)
                dve.memset(aggT[:, :, :], 0.0)
                dve.drain()
                with dve.Fori(0, NG) as g:
                    dve.tensor_tensor(dst_gen, dstrel[:, bass.ds(g * GT, GT)],
                                      base_f[:, bass.ds(g, 1)].to_broadcast([P, GT]), ALU.add)
                    dve.drain()
                    with dve.Fori(0, NW) as v:
                        wait(dve, gen_done, g * NW + v)
                        for t in range(GT):
                            dve.tensor_scalar(Sgen[:, t, :], iota[:, :], dst_gen[:, t:t + 1],
                                              ew[:, bass.ds(g * GT + t, 1)], ALU.is_equal, ALU.mult)
                        dve.drain().then_inc(gen_selected, 1)
                        dve.tensor_scalar(dst_gen, dst_gen, float(-GW), None, ALU.add)
                        wait(dve, gen_done, g * NW + v + 1)
                        win = aggT[:, :, bass.ds(v * GW, GW)]
                        dve.tensor_tensor(win, win, ps[:, 4:4 + KD, 0:GW], ALU.add)
                        dve.drain().then_inc(gen_added, 1)
            dve.tensor_scalar(ew[:, :], ew[:, :], small[:, 7:8], None, ALU.mult)
            dve.drain()

            def select(h, g):
                wait(dve, group_done, h * HG + g - 2)
                for t in range(GT):
                    m = g * GT + t
                    ins = dve.tensor_scalar(S[:, m % RING, :], iota[:, 0:W], dstrel[:, bass.ds(h * HB + m, 1)],
                                            ew[:, bass.ds(h * HB + m, 1)], ALU.is_equal, ALU.mult)
                ins.then_inc(selected, 1)

            def add_group(h, g):
                G = h * HG + g
                start = dve.value_load(base_i[0:1, bass.ds(G, 1)], min_val=0, max_val=NP - W)
                wait(dve, group_done, G + 1)
                wait(dve, group_added, G)
                win = aggT[:, :, bass.ds(start, W)]
                dve.tensor_tensor(win, win, aggps[g % 2].rearrange("p (k n) -> p k n", k=KD),
                                  ALU.add).then_inc(group_added, 1)

            def kv_stats(q, j):
                wait(dve, kv_squared, q + 1)
                dve.tensor_reduce(kv_var[:, j % 2, :], sq.rearrange("p (h d) -> p h d", d=DH), AX.X,
                                  ALU.add).then_inc(kv_var_done, 1)

            def kv_recip(q, j):
                dve.wait_ge(kv_std_done, q + 1)
                dve.reciprocal(kv_r[:, :], kv_var[:, j % 2, :]).then_inc(kv_r_done, 1)
                dve.wait_ge(kv_r_done, 2 * q + 1)
                dve.tensor_tensor(kv_s[:, j % 2, :], kv_r[:, 0:HEADS], kv_r[:, HEADS:], ALU.mult).then_inc(kv_r_done, 1)
                dve.wait_ge(kv_r_done, 2 * q + 2)
                wait(dve, dots_done, q - prior(j) + 1)
                dve.tensor_tensor(ks[:, j % 2, :].rearrange("p (h d) -> p h d", d=DH),
                                  wide[j % 2][:, 0:INNER].rearrange("p (h d) -> p h d", d=DH),
                                  kv_s[:, j % 2, :].unsqueeze(2).to_broadcast([P, HEADS, DH]),
                                  ALU.mult).then_inc(k_scaled, 1)

            def kv_step(b, j, first):
                q = b * CH + j
                head = first and j == 0
                if not head:
                    add_group(2 * b, 2 * j - 1)
                select(2 * b, 2 * j + 1)
                if not head:
                    kv_stats(q - 1, (j - 1) % CH)
                add_group(2 * b, 2 * j)
                select(2 * b, 2 * j + 2)
                if not head:
                    kv_recip(q - 1, (j - 1) % CH)
            select(0, 0)
            for j in range(CH):
                kv_step(0, j, True)
            chunks(dve, 1, NC, lambda b: [kv_step(b, j, False) for j in range(CH)])
            kv_stats(NT - 1, CH - 1)
            kv_recip(NT - 1, CH - 1)

            wait(dve, dots_done, NT)
            for a in range(2):
                half = slice(a * DH, (a + 1) * DH)
                dve.tensor_scalar(bd[half, :, half], dotps[half, :, half], 1.0 / N, None, ALU.mult).then_inc(bd_done, 1)

            add_group(2 * B0, -1)
            dve.wait_ge(later_in, 16 * len(LATER))

            def layers(c1, c2, h=None, g0=0, g1=HG, selected_first=False, select_next=False):
                def group(g):
                    if g + 1 < g1 or select_next:
                        select(h, g + 1)
                    add_group(h, g)

                def logit(j):
                    wait(dve, gate_done, c2 * CH + j + 1)
                    dve.tensor_tensor(logits[:, j, :], wide[j % 2][:, 512:512 + E], gb_b[:], ALU.add).then_inc(logit_done, 1)

                if h is not None and not selected_first:
                    select(h, g0)
                for j in range(CH + 2):
                    if c1 is not None and j < CH:
                        dve.wait_ge(x_again[j], 16 * (c1 + 1))
                        row = X2[:, bass.ds(c1 * CH + j, 1), :].rearrange("p a d -> p (a d)")
                        dve.tensor_tensor(row, row, bout_b[:], ALU.add).then_inc(x_biased, 1)
                    if h is not None and j < CH:
                        for g in range(g0 + j * (g1 - g0) // CH, g0 + (j + 1) * (g1 - g0) // CH):
                            group(g)
                    if c2 is not None and j < CH:
                        wait(dve, y_turned, c2 * CH + j + 1)
                        wait(dve, gate_done, c2 * CH + j - prior(j) + 1)
                        dve.tensor_copy(yT[:, j % 2, :], yps).then_inc(y_copied, 1)
                    if c1 is not None:
                        q = c1 * CH + j
                        if 1 <= j <= CH:
                            row = X2[:, bass.ds(q - 1, 1), :].rearrange("p a d -> p (a d)")
                            dve.wait_ge(x_biased, q)
                            wait(dve, layers_done, q)
                            dve.tensor_tensor(row, row, wide[(j - 1) % 2][:, 0:D], ALU.add).then_inc(x2_done, 1)
                        if j >= 2:
                            wait(dve, x2_done, q - 1)
                            dve.sem_inc(dve_past)
                            dve.bn_stats(bn[:, j - 2, :], X2[:, bass.ds(q - 2, 1), :].rearrange("p a d -> p (a d)"))
                    if c2 is not None and 1 <= j <= CH:
                        logit(j - 1)
                dve.drain()
                if c1 is not None:
                    for j in range(CH):
                        dve.bn_aggr(mvc[:, j, :], bn[:, j, :])
                    dve.drain()
                    dve.tensor_copy(mv[:, bass.ds(c1 * CH, CH), :], mvc[:, :, :]).then_inc(y_stats, 1)
                if c2 is not None:
                    for j in range(CH):
                        dve.max(out=top8[:, j, :], in_=logits[:, j, :])
                    dve.drain()
                    for j in range(CH):
                        dve.max_index(out=top8_i[:, j, :], in_max=top8[:, j, :], in_values=logits[:, j, :])
                    dve.drain()
                    cols = bass.ds(c2 * CH, CH)
                    dve.tensor_copy(top[:, :, cols], top8[:, :, 0:2].rearrange("p j k -> p k j"))
                    dve.tensor_copy(slot_f[:, :, cols], top8_i[:, :, 0:2].rearrange("p j k -> p k j"))
                    dve.drain()
                if c1 is not None:
                    cols = bass.ds(c1 * CH, CH)
                    dve.wait_ge(y_std, c1 + 1)
                    dve.reciprocal(rstd[:, cols], rstd[:, cols])
                    dve.drain()
                    dve.scalar_tensor_tensor(out=nmr[:, cols], in0=mv[:, cols, 0], scalar=-1.0, in1=rstd[:, cols],
                                             op0=ALU.mult, op1=ALU.mult).then_inc(y_rstd, 1)

            def route(part, c0, c1, tile0, n_tiles, bank, beside):
                nt = (c1 - c0) * CH
                cols = slice(c0 * CH, c1 * CH)
                h1, h2, hs, ps_, tt, sc, ie = [t[:, 0:E * nt].rearrange("p (e i) -> p e i", e=E)
                                               for t in (H1, H2, Hs, pos, tot, scan, iota_e)]
                ends_here = c1 == NC
                dve.tensor_tensor(prob[:, 1, cols], top[:, 1, cols], top[:, 0, cols], ALU.subtract)
                dve.drain().then_inc(exp_in, 1)
                for e in range(E):
                    dve.memset(ie[:, e, :], float(e))
                pidx, pad, dummy = small[:, 128:129], small[:, 129:130], small[:, 130:131]
                dve.tensor_scalar(pad, pidx, float(P - PADDED), None, ALU.is_ge)
                dve.tensor_scalar(dummy, pidx, 2.0, float(SB * TS), ALU.mult, ALU.add)
                dve.drain()
                for k, H in enumerate((h1, h2)):
                    dve.tensor_tensor(H, ie, slot_f[:, k, cols].unsqueeze(1).to_broadcast([P, E, nt]), ALU.is_equal)
                dve.tensor_scalar(small[:, 131:132], pad, -1.0, 1.0, ALU.mult, ALU.add)
                dve.drain()
                if ends_here:
                    for H in (h1, h2):
                        dve.tensor_scalar(H[:, :, nt - 1], H[:, :, nt - 1], small[:, 131:132], None, ALU.mult)
                    dve.drain()
                dve.tensor_tensor(hs, h1, h2, ALU.add).then_inc(hot_done, 1)
                dve.wait_ge(ranked, part + 1)
                dve.tensor_copy(tot[:, 0:E * nt], ps[:, bank + 1, 0:E * nt])
                dve.drain()
                dve.tensor_tensor_scan(scan[:, 0:E * nt], tot[:, 0:E * nt], tot[:, 0:E * nt], 0.0, ALU.add, ALU.max)
                dve.drain()
                beside(0)
                ends = sc[:, :, nt - 1]
                cnt, pads, aend, adj = (small[:, 16 * i:16 * i + 16] for i in range(2, 6))
                dve.tensor_copy(cnt, ends)
                dve.drain()
                dve.tensor_tensor(cnt[:, 1:E], ends[:, 1:E], ends[:, 0:E - 1], ALU.subtract)
                dve.drain()
                beside(1)
                cnt_i = small[:, 96:112].bitcast(I32)
                dve.tensor_scalar(cnt_i, cnt, float(TS - 1), None, ALU.add)
                dve.drain()
                dve.tensor_scalar(cnt_i, cnt_i, TS.bit_length() - 1, None, ALU.arith_shift_right)
                dve.drain()
                dve.tensor_copy(pads, cnt_i)
                dve.drain()
                dve.tensor_tensor_scan(aend, pads, pads, 0.0, ALU.add, ALU.max)
                dve.drain()
                beside(2)
                dve.tensor_tensor(adj, aend, pads, ALU.subtract)
                dve.tensor_tensor(cnt, ends, cnt, ALU.subtract)
                dve.drain()
                dve.tensor_scalar(adj, adj, float(TS), None, ALU.mult)
                dve.tensor_tensor(sc, sc, tt, ALU.subtract)
                dve.drain()
                beside(3)
                dve.tensor_tensor(adj, adj, cnt, ALU.subtract)
                dve.drain()
                dve.tensor_tensor(ps_, sc, adj.unsqueeze(2).to_broadcast([P, E, nt]), ALU.add)
                dve.drain()
                dve.tensor_tensor(pos[:, 0:E * nt], pos[:, 0:E * nt], ps[:, bank, 0:E * nt], ALU.add)
                dve.drain()
                beside(4)
                for H in (h1, h2):
                    dve.tensor_tensor(H, H, ps_, ALU.mult)
                dve.drain()
                beside(5)
                for k, H in enumerate((h1, h2)):
                    dve.tensor_reduce(slot_f[:, k, cols], H.rearrange("p e i -> p i e"), AX.X, ALU.add)
                dve.drain()
                if ends_here:
                    for k in range(2):
                        dve.tensor_scalar(small[:, 132 + k:133 + k], dummy, float(k), None, ALU.add)
                    dve.drain()
                    for k in range(2):
                        dve.tensor_tensor(small[:, 134 + k:135 + k], small[:, 132 + k:133 + k], pad, ALU.mult)
                    dve.drain()
                    for k in range(2):
                        dve.tensor_tensor(slot_f[:, k, NT - 1:NT], slot_f[:, k, NT - 1:NT], small[:, 134 + k:135 + k], ALU.add)
                    dve.drain()
                dve.tensor_copy(slot_i[:, :, cols], slot_f[:, :, cols])
                jj = small[0:1, 136:137]
                cmp = cmp_t[0:1, 0:n_tiles, :]
                dve.tensor_tensor(cmp, iota[0:1, 0:n_tiles].unsqueeze(2).to_broadcast([1, n_tiles, E]),
                                  aend[0:1].unsqueeze(1).to_broadcast([1, n_tiles, E]), ALU.is_ge)
                dve.drain()
                row = tot[0:1, 0:n_tiles]
                dve.tensor_reduce(row, cmp, AX.X, ALU.add)
                dve.drain()
                dve.tensor_scalar(etab[:, tile0:tile0 + n_tiles], row, float(E - 1), None, ALU.min)
                dve.tensor_scalar(taken[:, tile0:tile0 + n_tiles], row, float(E), None, ALU.is_lt)
                beside(6)
                dve.wait_ge(exp_done, part + 1)
                dve.tensor_scalar(prob[:, 0, cols], prob[:, 1, cols], 1.0, None, ALU.add)
                dve.drain()
                dve.reciprocal(prob[:, 0, cols], prob[:, 0, cols])
                dve.drain()
                dve.tensor_tensor(prob[:, 1, cols], prob[:, 1, cols], prob[:, 0, cols], ALU.mult)
                dve.drain().then_inc(slots_done, 1)

            def moe_y(j, s):
                wait(dve, l2_done, j + 1)
                dve.wait_ge(w2_in[s], 8 * (j + 2 - s))
                if not (isinstance(j, int) and j < 2):
                    dve.wait_ge(ys_out[s], 8 * (j - s))
                dve.tensor_tensor(yo[s], outps.rearrange("p (h d) -> p h d", h=2),
                                  w2_sb[s][:, W2ROW:].unsqueeze(1).to_broadcast([P, 2, D]), ALU.add).then_inc(y_done, 1)

            layers(0, None, 2 * B0, selected_first=True, select_next=True)
            chunks(dve, 1, CA, lambda c: layers(c, c - 1, 2 * B0 + c, selected_first=True, select_next=True))
            layers(None, CA - 1, 2 * B0 + CA, selected_first=True)
            route(0, 0, CA, 0, SA, 4, lambda n: None)

            def one_round(i, c2, g0=0):
                h = 2 * B0 + CA + 1 + 4 * i
                for k in range(PER):
                    for g in share(k, g0):
                        select(h, g)
                        if g > g0:
                            add_group(h, g - 1)
                    if k:
                        moe_y(PER * i + k - 1, (k - 1) % 2)
                add_group(h, EXPERT_G - 1)
                select(h, EXPERT_G)
                moe_y(PER * i + PER - 1, 1)
                layers(CA + i, c2, h, EXPERT_G, 2 * BG, selected_first=True)
            for g in range(EARLY_G):
                select(2 * B0 + CA + 1, g)
                if g:
                    add_group(2 * B0 + CA + 1, g - 1)
            add_group(2 * B0 + CA + 1, EARLY_G - 1)
            one_round(0, None, EARLY_G)
            chunks(dve, 1, ROUNDS, lambda i: one_round(i, CA + i - 1))
            layers(NC - 1, NC - 2)
            layers(None, NC - 1)
            LATE_Y = {1: J0, 4: J0 + 1, 6: J0 + 2}

            def experts_beside(n):
                if n in LATE_Y:
                    moe_y(LATE_Y[n], LATE_Y[n] % 2)
            route(1, CA, NC, SA, SB, 0, experts_beside)
            for j in range(J0 + len(LATE_Y), SA):
                moe_y(j, j % 2)

            def finish_a(q, part):
                row = X2[:, bass.ds(q, 1), :].rearrange("p a d -> p (a d)")
                if part == 0:
                    dve.wait_ge(a_picked, 32 * (q + 1))
                    dve.wait_ge(a_again, q + 1)
                    for k in range(2):
                        dve.scalar_tensor_tensor(out=ay[:], in0=ring[:, k, :], scalar=prob[:, k, bass.ds(q, 1)],
                                                 in1=ay[:], op0=ALU.mult, op1=ALU.add)
                        dve.drain()
                    dve.sem_inc(a_summed)
                    dve.bn_stats(bn[:, 0, :], ay[:])
                    dve.tensor_tensor(row, row, beta_b[:], ALU.add)
                    dve.drain()
                    dve.bn_aggr(mvc[:, 0, :], bn[:, 0, :])
                    dve.drain().then_inc(a_stats, 1)
                else:
                    dve.wait_ge(a_std, q + 1)
                    dve.reciprocal(small[:, 49:50], small[:, 48:49])
                    dve.drain()
                    dve.scalar_tensor_tensor(out=small[:, 50:51], in0=mvc[:, 0, 0:1], scalar=-1.0,
                                             in1=small[:, 49:50], op0=ALU.mult, op1=ALU.mult).then_inc(a_rstd, 1)
                    dve.wait_ge(a_normed, q + 1)
                    dve.tensor_tensor(cy[:], cy[:], gamma_b[:], ALU.mult)
                    dve.drain()
                    dve.tensor_tensor(cy[:], cy[:], row, ALU.add).then_inc(a_done, 1)

            def residual(q):
                return aggT[:, :, bass.ds(q * P, P)]

            def by_half(t):
                return t.rearrange("p (k n) -> p k n", k=KD)

            def add_beta(q):
                dve.tensor_tensor(residual(q), by_half(X2[:, bass.ds(q, 1), :].rearrange("p a d -> p (a d)")),
                                  by_half(beta_b[:]), ALU.add).then_inc(beta_added, 1)

            def moe_a(i, first=False):
                q = i - SA // 2
                if not first:
                    moe_y(2 * i - 1, 1)
                finish_a(q, 0)
                moe_y(2 * i, 0)
                finish_a(q, 1)
                for s in range(2):
                    add_beta(CA * CH + 2 * q + s)
            moe_a(SA // 2, first=True)
            chunks(dve, SA // 2 + 1, SA // 2 + AC * CH, moe_a)
            moe_y(SA + 2 * AC * CH - 1, 1)
            chunks(dve, SA // 2 + AC * CH, NS // 2, lambda i: [moe_y(2 * i + s, s) for s in range(2)])

            def out_chunk(c, second=True):
                def weigh(j, k):
                    q = c * CH + j
                    if k == 0:
                        dve.wait_ge(picked[j], 32 * (c - AC + 1))
                        if second:
                            dve.wait_ge(f_out[j], 16 * (c - AC))
                            if j == 0:
                                dve.wait_ge(rows_again, (NC - CA) * CH)
                        else:
                            dve.wait_ge(y_again, q + 1 - AC * CH)
                    else:
                        wait(dve, half_summed, q + 1 - AC * CH)
                    rows = X2[:, bass.ds(q, 1), :].rearrange("p a d -> p (a d)") if second and k == 0 else tile_in[:, j, :]
                    dve.scalar_tensor_tensor(out=tile_in[:, j, :], in0=ring[:, 2 * j + k, :],
                                             scalar=prob[:, k, bass.ds(q, 1)], in1=rows,
                                             op0=ALU.mult, op1=ALU.add).then_inc((half_summed, summed)[k], 1)
                for j in range(CH + 1):
                    if j < CH:
                        weigh(j, 0)
                    if j:
                        weigh(j - 1, 1)
                dve.drain()
                for j in range(CH):
                    dve.bn_stats(bn[:, j, :], tile_in[:, j, :])
                dve.drain()
                for j in range(CH):
                    dve.bn_aggr(mvc[:, j, :], bn[:, j, :])
                dve.drain()
                dve.tensor_copy(small[:, 16:16 + CH], mvc[:, :, 1])
                dve.drain().then_inc(f_stats, 1)
                dve.wait_ge(f_std, c - AC + 1)
                dve.reciprocal(small[:, 24:24 + CH], small[:, 8:8 + CH])
                dve.drain()
                dve.scalar_tensor_tensor(out=small[:, 32:32 + CH], in0=mvc[:, :, 0], scalar=-1.0,
                                         in1=small[:, 24:24 + CH], op0=ALU.mult, op1=ALU.mult).then_inc(f_rstd, 1)
                if not second:
                    for j in range(CH):
                        row = X2[:, bass.ds(c * CH + j, 1), :].rearrange("p a d -> p (a d)")
                        dve.tensor_tensor(row, row, beta_b[:], ALU.add)
                for j in range(CH):
                    dve.wait_ge(f_normed, (c - AC) * CH + j + 1)
                    dve.tensor_tensor(tile_in[:, j, :], tile_in[:, j, :], gamma_b[:], ALU.mult)
                dve.drain()
                for j in range(CH):
                    row = X2[:, bass.ds(c * CH + j, 1), :].rearrange("p a d -> p (a d)")
                    t = by_half(tile_in[:, j, :])
                    dve.tensor_tensor(t, t, residual(c * CH + j) if second else by_half(row), ALU.add).then_inc(f_done, 1)
            for c in range(AC, CA):
                out_chunk(c, second=False)
            chunks(dve, CA, NC, out_chunk)

        @block.tensor
        def _(pe):
            start_counters(pe, LEADERS["tensor"])

            def edge_group(h, g):
                G = h * HG + g
                pe.wait_ge(selected, G + 1)
                wait(pe, group_added, G if g == 0 else G - 1)
                for t in range(GT):
                    m = g * GT + t
                    pe.wait_ge(gathered[m % RING], 16 * (h * (HB // RING) + m // RING + 1))
                    for f in range(KD):
                        mm = pe.matmul(aggps[g % 2][:, f * W:(f + 1) * W], ring[:, m % RING, f * P:(f + 1) * P],
                                       S[:, m % RING, :], start=(t == 0 and f == 0), stop=(t == GT - 1),
                                       skip_group_check=True)
                mm.then_inc(group_done, 1)

            def turn(n, c, j, passes):
                pe.wait_ge(tile_loaded[j], 16 * (c + 1 + passes * NC))
                wait(pe, turned_copied, n)
                for k in range(KD):
                    mm = pe.transpose(tps[:, k * P:(k + 1) * P], tile_in[:, j, k * P:(k + 1) * P], ident[:])
                mm.then_inc(tile_turned, 1)

            def kv_mm(q, j):
                wait(pe, turned_copied, q + 1)
                wait(pe, k_scaled, q - prior(j) + 1)
                wait(pe, v_copied, q - prior(j) + 1)
                for h in range(2):
                    for k in range(KD):
                        mm = pe.matmul(wide[j % 2][:, h * 512:(h + 1) * 512], tT[:, j % 2, k * P:(k + 1) * P],
                                       wkv_sb[:, k, h * 512:(h + 1) * 512], start=(k == 0), stop=(k == KD - 1))
                mm.then_inc(kv_done, 1)

            def dots(q, j, first):
                wait(pe, k_scaled, q + 1)
                wait(pe, v_copied, q + 1)
                for a in range(NJ):
                    mm = pe.matmul(dotps[:, a, :], vs[:, j % 2, a * P:(a + 1) * P], ks[:, j % 2, a * P:(a + 1) * P],
                                   start=(first and a == 0), stop=False, skip_group_check=True)
                mm.then_inc(dots_done, 1)

            def kv_step(b, j, first):
                q = b * CH + j
                edge_group(2 * b, 2 * j)
                turn(q, b, j, 0)
                edge_group(2 * b, 2 * j + 1)
                kv_mm(q, j)
                if not (first and j == 0):
                    dots(q - 1, (j - 1) % CH, first and j == 1)

            pe.wait_ge(pool_consts, 9)
            pe.wait_ge(bad_found, 1)
            pe.matmul(ps[:, 3, 0:1], ones[:], small[:, 4:5], start=True, stop=True).then_inc(bad_counted, 1)
            pe.wait_ge(dve_consts, 1)
            pe.wait_ge(flag_ready, 1)
            bad = pe.value_load(flag[0:1, 0:1], min_val=0, max_val=P)
            with pe.If(bad > 0):
                with pe.Fori(0, NG) as g:
                    with pe.Fori(0, NW) as v:
                        for t in range(GT):
                            pe.wait_ge(gen_gathered[t], 16 * (g + 1))
                        pe.wait_ge(gen_selected, g * NW + v + 1)
                        wait(pe, gen_added, g * NW + v)
                        for t in range(GT):
                            for f in range(KD):
                                mm = pe.matmul(ps[:, 4 + f, 0:GW], ring[:, t, f * P:(f + 1) * P], Sgen[:, t, :],
                                               start=(t == 0), stop=(t == GT - 1), skip_group_check=True)
                        mm.then_inc(gen_done, 1)
                wait(pe, gen_added, NG * NW)
            for j in range(CH):
                kv_step(0, j, True)
            chunks(pe, 1, NC, lambda b: [kv_step(b, j, False) for j in range(CH)])
            dots(NT - 1, CH - 1, False)

            pe.wait_ge(later_in, 16 * len(LATER))
            pe.wait_ge(bd_done, 2)
            for a in range(NJ):
                mm = pe.matmul(wide[0][:, a * D:(a + 1) * D], bd[:, a, :], wout_sb[:, a, :], start=True, stop=True)
            mm.then_inc(t1_done, 1)
            pe.wait_ge(t1_copied, 1)
            for k in range(KD):
                for a in range(NJ):
                    mm = pe.matmul(wide[1][:, k * D:(k + 1) * D], wq_sb[:, a, k * P:(k + 1) * P], T1[:, a, :],
                                   start=(a == 0), stop=(a == NJ - 1))
            mm.then_inc(m_done, 1)
            pe.wait_ge(m_copied, 1)

            def layers(c1, c2, h=None, g0=0, g1=HG):
                def mix_gnn(j):
                    q = c1 * CH + j
                    wait(pe, turned_copied, NT + q + 1)
                    pe.wait_ge(agg_staged, q + 1)
                    wait(pe, x2_done, q - prior(j) + 1)
                    for m, (lhs, rhs) in enumerate(((tT, M), (aT, gnn_sb))):
                        for k in range(KD):
                            mm = pe.matmul(wide[j % 2][:, 0:D], lhs[:, j % 2, k * P:(k + 1) * P], rhs[:, k, :],
                                           start=(m == 0 and k == 0), stop=(m == 1 and k == KD - 1))
                    mm.then_inc(layers_done, 1)

                def gate(j):
                    q = c2 * CH + j
                    wait(pe, y_copied, q + 1)
                    wait(pe, logit_done, q - prior(j) + 1)
                    for k in range(KD):
                        mm = pe.matmul(wide[j % 2][:, 512:512 + 96], yT[:, j % 2, k * P:(k + 1) * P], gate_sb[:, k, :],
                                       start=(k == 0), stop=(k == KD - 1))
                    mm.then_inc(gate_done, 1)

                for j in range(CH + 1):
                    if j < CH:
                        if h is not None:
                            for g in range(g0 + j * (g1 - g0) // CH, g0 + (j + 1) * (g1 - g0) // CH):
                                edge_group(h, g)
                        if c1 is not None:
                            turn(NT + c1 * CH + j, c1, j, 1)
                        if c2 is not None:
                            q = c2 * CH + j
                            pe.wait_ge(y_normed, q + 1)
                            wait(pe, y_copied, q)
                            for k in range(KD):
                                mm = pe.transpose(yps[:, k * P:(k + 1) * P], yt[:, j % 2, k * P:(k + 1) * P], ident[:])
                            mm.then_inc(y_turned, 1)
                    if j:
                        if c1 is not None:
                            mix_gnn(j - 1)
                        if c2 is not None:
                            gate(j - 1)

            def rank(part, nt, bank):
                pe.wait_ge(hot_done, part + 1)
                pe.matmul(ps[:, bank, 0:E * nt], upper[:], Hs[:, 0:E * nt], start=True, stop=True)
                pe.matmul(ps[:, bank + 1, 0:E * nt], ones[:], Hs[:, 0:E * nt], start=True, stop=True).then_inc(ranked, 1)

            def xg_turn(j, s):
                pe.wait_ge(xg_in[s], 8 * (j + 2 - s))
                wait(pe, xg_copied, j)
                for h in range(2):
                    for k in range(KD):
                        mm = pe.transpose(xgps[:, k * TS + h * P:k * TS + (h + 1) * P],
                                          xg[s][:, h, k * P:(k + 1) * P], ident[:])
                mm.then_inc(xg_turned, 1)

            def layer1(j, s):
                def products():
                    wait(pe, xg_copied, j + 1)
                    wait(pe, relu_done, j - 1)
                    pe.wait_ge(w1_in[s], 8 * (j + 2 - s))
                    for f in range(FC):
                        for k in range(KD):
                            mm = pe.matmul(wide[s][:, f * TS:(f + 1) * TS],
                                           w1_sb[s][:, k * F + f * P:k * F + (f + 1) * P], xgT[s][:, k, :],
                                           start=(k == 0), stop=(k == KD - 1))
                    mm.then_inc(l1_done, 1)
                where_taken(pe, j, products, (l1_done,), lambda _: j)

            def layer2(j, s):
                def products():
                    wait(pe, relu_done, j + 1)
                    wait(pe, y_done, j)
                    pe.wait_ge(w2_in[s], 8 * (j + 2 - s))
                    for h in range(2):
                        for f in range(FC):
                            mm = pe.matmul(outps[:, h * D:(h + 1) * D], hT[s][:, f, h * P:(h + 1) * P],
                                           w2_sb[s][:, f * D:(f + 1) * D], start=(f == 0), stop=(f == FC - 1))
                    mm.then_inc(l2_done, 1)
                where_taken(pe, j, products, (l2_done,), lambda _: j)

            def moe_tile(j, s, first=False, last=False, edges=()):
                layer1(j, s)
                for h, g in edges:
                    edge_group(h, g)
                if not last:
                    xg_turn(j + 1, 1 - s)
                if not first:
                    layer2(j - 1, 1 - s)

            layers(0, None, 2 * B0)
            chunks(pe, 1, CA, lambda c: layers(c, c - 1, 2 * B0 + c))
            layers(None, CA - 1, 2 * B0 + CA)
            rank(0, CA * CH, 4)
            for g in range(EARLY_G):
                edge_group(2 * B0 + CA + 1, g)
            pe.wait_ge(slots_done, 1)

            def one_round(i, c2, g0=0):
                h = 2 * B0 + CA + 1 + 4 * i
                if c2 is not None:
                    free_banks(CA + i, CA + i - 1)
                xg_turn(PER * i, 0)
                for k in range(PER):
                    moe_tile(PER * i + k, k % 2, first=(k == 0), last=(k == PER - 1),
                             edges=[(h, g) for g in share(k, g0)])
                layer2(PER * i + PER - 1, 1)
                wait(pe, y_done, PER * (i + 1))
                layers(CA + i, c2, h, EXPERT_G, 2 * BG)

            def free_banks(c1, c2):
                wait(pe, x2_done, c1 * CH)
                wait(pe, y_copied, c2 * CH)
                wait(pe, logit_done, c2 * CH)
            one_round(0, None, EARLY_G)
            chunks(pe, 1, ROUNDS, lambda i: one_round(i, CA + i - 1))
            layers(NC - 1, NC - 2)
            layers(None, NC - 1)

            free_banks(NC, NC)
            xg_turn(J0, 0)
            moe_tile(J0, 0, first=True)
            rank(1, (NC - CA) * CH, 0)
            for j in range(J0 + 1, SA):
                moe_tile(j, j % 2, last=(j == SA - 1))
            layer2(SA - 1, 1)
            pe.wait_ge(slots_done, 2)
            xg_turn(SA, 0)
            moe_tile(SA, 0, first=True)
            moe_tile(SA + 1, 1)
            chunks(pe, SA // 2 + 1, NS // 2 - 1, lambda i: [moe_tile(2 * i + s, s) for s in range(2)])
            moe_tile(NS - 2, 0)
            moe_tile(NS - 1, 1, last=True)
            layer2(NS - 1, 1)


def kernel(x, src, dst, edge_weight, L0_gnn_weight, L0_mix_Wqkv, L0_mix_Wout, L0_mix_bout,
           L0_ffn_gate_w, L0_ffn_gate_b, L0_ffn_w1, L0_ffn_b1, L0_ffn_w2, L0_ffn_b2, L0_ffn_gamma,
           L0_ffn_beta):
    import numpy as np
    import concourse.bacc as bacc
    from concourse.bass_utils import run_bass_kernel_spmd

    def pad(a, n, value):
        a = np.asarray(a)
        return np.concatenate([a, np.full((n - len(a),) + a.shape[1:], value, a.dtype)])

    def by_partition(w):
        w = np.asarray(w)
        return np.ascontiguousarray(w.reshape(-1, P, w.shape[1]).transpose(1, 0, 2))

    n_edges = ET * P
    src_p, dst_p = pad(src, n_edges, 0), pad(dst, n_edges, N - 1)
    wqkv = np.asarray(L0_mix_Wqkv)
    gate_w = np.zeros((D, 96), np.float32)
    gate_w[:, :E] = np.asarray(L0_ffn_gate_w)
    w1 = np.asarray(L0_ffn_w1).reshape(E, KD, P, F).transpose(0, 2, 1, 3).reshape(E, P, KD * F)
    b1 = np.asarray(L0_ffn_b1).reshape(E, FC, P).transpose(0, 2, 1)
    w2 = np.asarray(L0_ffn_w2).reshape(E, FC, P, D).transpose(0, 2, 1, 3).reshape(E, P, W2ROW)
    arrays = {
        "x": pad(x, NP, 0),
        "src": src_p.reshape(ET, P).T, "dst": dst_p.reshape(ET, P).T,
        "first_dst": dst_p[::GT * P].reshape(1, NG),
        "edge_w": pad(edge_weight, n_edges, 0).reshape(ET, P).T,
        "gnn_w": by_partition(L0_gnn_weight),
        "wkv": by_partition(wqkv[INNER:].T), "wq": by_partition(wqkv[:INNER]),
        "wout": by_partition(np.asarray(L0_mix_Wout).T),
        "bout": np.asarray(L0_mix_bout).reshape(1, D),
        "gate_w": by_partition(gate_w), "gate_b": np.asarray(L0_ffn_gate_b).reshape(1, E),
        "w1b": np.concatenate([w1, b1], axis=2),
        "w2b": np.concatenate([w2, np.broadcast_to(np.asarray(L0_ffn_b2)[:, None, :], (E, P, D))], axis=2),
        "gamma": np.asarray(L0_ffn_gamma).reshape(1, D), "beta": np.asarray(L0_ffn_beta).reshape(1, D),
    }
    nc = bacc.Bacc("TRN2", target_bir_lowering=False, num_devices=1)
    feed, args = {}, {}
    for name, a in arrays.items():
        a = np.ascontiguousarray(a)
        feed[f"in_{name}"] = a
        args[name] = nc.dram_tensor(f"in_{name}", a.shape, mybir.dt.from_np(a.dtype), kind="ExternalInput").ap()
    args["out"] = nc.dram_tensor("result", (NP, D), F32, kind="ExternalOutput").ap()
    gps_layer(nc, **args)
    r = run_bass_kernel_spmd(nc, [feed], core_ids=[0])
    return r.results[0]["result"][:N]
```
